# Optimizing a Trainium2 kernel written in Bass

```python
import numpy as np
import jax
import jax.numpy as jnp

def _softmax(x, axis=-1):
    return jax.nn.softmax(x, axis=axis)

def _gelu(x):
    return jax.nn.gelu(x, approximate=True)

def _silu(x):
    return jax.nn.silu(x)

def _sigmoid(x):
    return jax.nn.sigmoid(x)

def _layernorm(x, axis=-1, eps=1e-05):
    m = jnp.mean(x, axis=axis, keepdims=True)
    v = jnp.var(x, axis=axis, keepdims=True)
    return (x - m) / jnp.sqrt(v + eps)

def _scatter_add(tgt, idx, src, axis=0):
    return tgt.at[idx].add(src)

def _segment_sum(src, seg, n):
    return jax.ops.segment_sum(src, seg, n)
kernel_name = 'mk_early_fusion_d1_tok_img768_r4_b09305'

def setup_inputs(seed: int=0):
    np.random.seed(seed)
    _w = jnp.asarray

    def _rec_inputs():
        import jax
        import jax.numpy as jnp
        _rk = jax.random.key(seed)
        x = -0.00040386 + 0.999972 * jax.random.normal(jax.random.fold_in(_rk, 1), (8, 3, 128, 128), jnp.float32)
        txt = 0.198809 + 1.28268 * jax.random.normal(jax.random.fold_in(_rk, 2), (8, 32, 192), jnp.float32)
        return (x, txt)
    x, txt = _rec_inputs()

    def _L0_tok_setup():
        import jax, jax.numpy as jnp
        import numpy as np
        P = 16
        WIN = 64
        NH = 12

        def _layernorm(x, g, b, eps=1e-05):
            m = x.mean(-1, keepdims=True)
            v = ((x - m) ** 2).mean(-1, keepdims=True)
            return (x - m) * jax.lax.rsqrt(v + eps) * g + b

        def _sinusoidal_pe(n, d):
            pos = jnp.arange(n, dtype=jnp.float32)[:, None]
            i = jnp.arange(d // 2, dtype=jnp.float32)[None, :]
            ang = pos / jnp.power(10000.0, 2.0 * i / d)
            pe = jnp.zeros((n, d), jnp.float32)
            pe = pe.at[:, 0::2].set(jnp.sin(ang)).at[:, 1::2].set(jnp.cos(ang))
            return pe
        key = jax.random.key(seed)
        ks = jax.random.split(key, 8)
        B, C, H, W, D, F = (16, 3, 128, 128, 192, 768)
        s = lambda k, shape: jax.random.normal(k, shape, jnp.float32) * 0.02
        return {'input': jax.random.normal(ks[0], (B, C, H, W), jnp.float32), 'patch_w': s(ks[1], (D, C, P, P)), 'patch_b': jnp.zeros((D,), jnp.float32), 'ln_g': jnp.ones((D,), jnp.float32), 'ln_b': jnp.zeros((D,), jnp.float32), 'qkv_w': s(ks[2], (D, 3 * D)), 'qkv_b': jnp.zeros((3 * D,), jnp.float32), 'proj_w': s(ks[3], (D, D)), 'proj_b': jnp.zeros((D,), jnp.float32), 'ff1_w': s(ks[4], (D, F)), 'ff1_b': jnp.zeros((F,), jnp.float32), 'ff2_w': s(ks[5], (F, D)), 'ff2_b': jnp.zeros((D,), jnp.float32)}
    _L0_tok_all = _L0_tok_setup()
    _L0_tok_in = {k: v for k, v in _L0_tok_all.items() if k in ('patch_w', 'patch_b', 'ln_g', 'ln_b', 'qkv_w', 'qkv_b', 'proj_w', 'proj_b', 'ff1_w', 'ff1_b', 'ff2_w', 'ff2_b')}
    del _L0_tok_all

    def _L0_attn_setup():
        import jax, jax.numpy as jnp
        import numpy as np
        import math
        D_MODEL = 192
        N_HEADS = 12
        B, L = (2, 512)
        ALPHA = 0.3
        key = jax.random.key(seed)
        ks = jax.random.split(key, 7)
        s = 0.02
        return {'x': jax.random.normal(ks[0], (B, L, D_MODEL), dtype=jnp.float32), 'Wqkv_w': jax.random.normal(ks[1], (D_MODEL, 3 * D_MODEL), dtype=jnp.float32) * s, 'Wqkv_b': jax.random.normal(ks[2], (3 * D_MODEL,), dtype=jnp.float32) * s, 'sel_w': jax.random.normal(ks[3], (D_MODEL, 2), dtype=jnp.float32) * s, 'sel_b': jax.random.normal(ks[4], (2,), dtype=jnp.float32) * s, 'out_w': jax.random.normal(ks[5], (D_MODEL, D_MODEL), dtype=jnp.float32) * s, 'out_b': jax.random.normal(ks[6], (D_MODEL,), dtype=jnp.float32) * s, 'temperature': jnp.ones((1,), dtype=jnp.float32) * (math.sqrt(D_MODEL) * ALPHA)}
    _L0_attn_all = _L0_attn_setup()
    _L0_attn_in = {k: v for k, v in _L0_attn_all.items() if k in ('Wqkv_w', 'Wqkv_b', 'sel_w', 'sel_b', 'out_w', 'out_b', 'temperature')}
    del _L0_attn_all

    def _L0_ffn_setup():
        import jax, jax.numpy as jnp
        import numpy as np
        DIM = 192
        HID = 128
        E = 16
        G = 8
        TOPK_G = 4
        TOPK_E = 4
        SCALE = 2.5
        B, S = (2, 512)
        key = jax.random.key(seed)
        ks = jax.random.split(key, 9)
        init = lambda k, shape: jax.random.normal(k, shape, dtype=jnp.float32) * 0.02
        z = lambda shape: jnp.zeros(shape, jnp.float32)
        return {'x': jax.random.normal(ks[0], (B, S, DIM), dtype=jnp.float32), 'gate_w': init(ks[1], (DIM, E)), 'gate_b': z((E,)), 'bias': z((E,)), 'Wu': init(ks[2], (E, DIM, HID)), 'bu': z((E, HID)), 'Wg': init(ks[3], (E, DIM, HID)), 'bg': z((E, HID)), 'Wd': init(ks[4], (E, HID, DIM)), 'bd': z((E, DIM)), 'sWu': init(ks[5], (DIM, HID)), 'sbu': z((HID,)), 'sWg': init(ks[6], (DIM, HID)), 'sbg': z((HID,)), 'sWd': init(ks[7], (HID, DIM)), 'sbd': z((DIM,))}
    _L0_ffn_all = _L0_ffn_setup()
    _L0_ffn_in = {k: v for k, v in _L0_ffn_all.items() if k in ('gate_w', 'gate_b', 'bias', 'Wu', 'bu', 'Wg', 'bg', 'Wd', 'bd', 'sWu', 'sbu', 'sWg', 'sbg', 'sWd', 'sbd')}
    del _L0_ffn_all
    return {'x': x, 'txt': txt, 'L0_tok_patch_w': _L0_tok_in['patch_w'], 'L0_tok_patch_b': _L0_tok_in['patch_b'], 'L0_tok_ln_g': _L0_tok_in['ln_g'], 'L0_tok_ln_b': _L0_tok_in['ln_b'], 'L0_tok_qkv_w': _L0_tok_in['qkv_w'], 'L0_tok_qkv_b': _L0_tok_in['qkv_b'], 'L0_tok_proj_w': _L0_tok_in['proj_w'], 'L0_tok_proj_b': _L0_tok_in['proj_b'], 'L0_tok_ff1_w': _L0_tok_in['ff1_w'], 'L0_tok_ff1_b': _L0_tok_in['ff1_b'], 'L0_tok_ff2_w': _L0_tok_in['ff2_w'], 'L0_tok_ff2_b': _L0_tok_in['ff2_b'], 'L0_attn_Wqkv_w': _L0_attn_in['Wqkv_w'], 'L0_attn_Wqkv_b': _L0_attn_in['Wqkv_b'], 'L0_attn_sel_w': _L0_attn_in['sel_w'], 'L0_attn_sel_b': _L0_attn_in['sel_b'], 'L0_attn_out_w': _L0_attn_in['out_w'], 'L0_attn_out_b': _L0_attn_in['out_b'], 'L0_attn_temperature': _L0_attn_in['temperature'], 'L0_ffn_gate_w': _L0_ffn_in['gate_w'], 'L0_ffn_gate_b': _L0_ffn_in['gate_b'], 'L0_ffn_bias': _L0_ffn_in['bias'], 'L0_ffn_Wu': _L0_ffn_in['Wu'], 'L0_ffn_bu': _L0_ffn_in['bu'], 'L0_ffn_Wg': _L0_ffn_in['Wg'], 'L0_ffn_bg': _L0_ffn_in['bg'], 'L0_ffn_Wd': _L0_ffn_in['Wd'], 'L0_ffn_bd': _L0_ffn_in['bd'], 'L0_ffn_sWu': _L0_ffn_in['sWu'], 'L0_ffn_sbu': _L0_ffn_in['sbu'], 'L0_ffn_sWg': _L0_ffn_in['sWg'], 'L0_ffn_sbg': _L0_ffn_in['sbg'], 'L0_ffn_sWd': _L0_ffn_in['sWd'], 'L0_ffn_sbd': _L0_ffn_in['sbd']}

def reference(x, txt, L0_tok_patch_w, L0_tok_patch_b, L0_tok_ln_g, L0_tok_ln_b, L0_tok_qkv_w, L0_tok_qkv_b, L0_tok_proj_w, L0_tok_proj_b, L0_tok_ff1_w, L0_tok_ff1_b, L0_tok_ff2_w, L0_tok_ff2_b, L0_attn_Wqkv_w, L0_attn_Wqkv_b, L0_attn_sel_w, L0_attn_sel_b, L0_attn_out_w, L0_attn_out_b, L0_attn_temperature, L0_ffn_gate_w, L0_ffn_gate_b, L0_ffn_bias, L0_ffn_Wu, L0_ffn_bu, L0_ffn_Wg, L0_ffn_bg, L0_ffn_Wd, L0_ffn_bd, L0_ffn_sWu, L0_ffn_sbu, L0_ffn_sWg, L0_ffn_sbg, L0_ffn_sWd, L0_ffn_sbd):
    import jax
    import jax.numpy as jnp

    def _L0_tok_ref(input, patch_w, patch_b, ln_g, ln_b, qkv_w, qkv_b, proj_w, proj_b, ff1_w, ff1_b, ff2_w, ff2_b):
        import jax, jax.numpy as jnp
        import numpy as np
        P = 16
        WIN = 64
        NH = 12

        def _layernorm(x, g, b, eps=1e-05):
            m = x.mean(-1, keepdims=True)
            v = ((x - m) ** 2).mean(-1, keepdims=True)
            return (x - m) * jax.lax.rsqrt(v + eps) * g + b

        def _sinusoidal_pe(n, d):
            pos = jnp.arange(n, dtype=jnp.float32)[:, None]
            i = jnp.arange(d // 2, dtype=jnp.float32)[None, :]
            ang = pos / jnp.power(10000.0, 2.0 * i / d)
            pe = jnp.zeros((n, d), jnp.float32)
            pe = pe.at[:, 0::2].set(jnp.sin(ang)).at[:, 1::2].set(jnp.cos(ang))
            return pe
        B, C, H, W = input.shape
        D = patch_w.shape[0]
        dh = D // NH
        xp = input.reshape(B, C, H // P, P, W // P, P)
        x = jnp.einsum('bchpwq,dcpq->bhwd', xp, patch_w) + patch_b
        x = x.reshape(B, -1, D)
        x = _layernorm(x, ln_g, ln_b)
        N = x.shape[1]
        x = x + _sinusoidal_pe(N, D)

        def ff(y):
            return jax.nn.gelu(y @ ff1_w + ff1_b) @ ff2_w + ff2_b

        def sparse_attn(y):
            nW = N // WIN
            qkv = (y @ qkv_w + qkv_b).reshape(B, nW, WIN, 3, NH, dh)
            q, k, v = (qkv[:, :, :, 0], qkv[:, :, :, 1], qkv[:, :, :, 2])
            scores = jnp.einsum('bwqhd,bwkhd->bwhqk', q, k) * dh ** (-0.5)
            a = jax.nn.softmax(scores, axis=-1)
            o = jnp.einsum('bwhqk,bwkhd->bwqhd', a, v).reshape(B, N, D)
            return o @ proj_w + proj_b
        identity = x
        x = ff(x)
        x = sparse_attn(x)
        x = x + identity
        identity = x
        x = ff(x)
        x = x + identity
        return x

    def _L0_attn_ref(x, Wqkv_w, Wqkv_b, sel_w, sel_b, out_w, out_b, temperature):
        import jax, jax.numpy as jnp
        import numpy as np
        import math
        D_MODEL = 192
        N_HEADS = 12
        B, L = (2, 512)
        ALPHA = 0.3
        b, l, d = x.shape
        h = N_HEADS
        hd = d // h
        qkv = (x @ Wqkv_w + Wqkv_b).reshape(b, l, 3, h, hd)
        q, k_, v = (qkv[:, :, 0], qkv[:, :, 1], qkv[:, :, 2])
        scale = 1.0 / math.sqrt(hd)
        scores = jnp.einsum('bthd,bshd->bhts', q, k_ * scale)
        causal_mask = jnp.triu(jnp.full((l, l), -10000.0, dtype=scores.dtype), 1)
        attn = jax.nn.softmax(scores + causal_mask, axis=-1)
        ctx = jnp.einsum('bhts,bshd->bthd', attn, v).reshape(b, l, d)
        attn_output = ctx @ out_w + out_b
        selection = jax.nn.softmax((x @ sel_w + sel_b) / temperature, axis=-1)[..., 1:]
        k_sel = int(math.ceil(math.sqrt(l)))
        _, idx = jax.lax.top_k(selection[..., 0], k_sel)
        gated = attn_output * selection
        src = jnp.take_along_axis(gated, idx[..., None], axis=1)
        y = jax.vmap(lambda xb, ib, sb: xb.at[ib].add(sb))(x, idx, src)
        return y

    def _L0_ffn_ref(x, gate_w, gate_b, bias, Wu, bu, Wg, bg, Wd, bd, sWu, sbu, sWg, sbg, sWd, sbd):
        import jax, jax.numpy as jnp
        import numpy as np
        DIM = 192
        HID = 128
        E = 16
        G = 8
        TOPK_G = 4
        TOPK_E = 4
        SCALE = 2.5
        B, S = (2, 512)
        orig_shape = x.shape
        xt = x.reshape(-1, DIM)
        T = xt.shape[0]
        scores = jax.nn.softmax(xt @ gate_w + gate_b, axis=-1)
        orig_scores = jax.lax.stop_gradient(scores)
        s = scores + bias[None, :]
        s3 = s.reshape(T, G, E // G)
        group_scores = jax.lax.top_k(s3, 2)[0].sum(-1)
        gidx = jax.lax.top_k(group_scores, TOPK_G)[1]
        gmask = jnp.any(jnp.arange(G)[None, None, :] == gidx[:, :, None], axis=1)
        s_masked = jnp.where(gmask[:, :, None], s3, -jnp.inf).reshape(T, E)
        _, idx = jax.lax.top_k(s_masked, TOPK_E)
        w = jnp.take_along_axis(orig_scores, idx, axis=1) * SCALE
        w_full = jnp.zeros((T, E), xt.dtype).at[jnp.arange(T)[:, None], idx].add(w)
        up = jax.nn.silu(jnp.einsum('td,edh->teh', xt, Wu) + bu)
        gt = jnp.einsum('td,edh->teh', xt, Wg) + bg
        act = up * gt * w_full[:, :, None]
        y = jnp.einsum('teh,ehd->td', act, Wd) + w_full @ bd
        sh = jax.nn.silu(xt @ sWu + sbu) * (xt @ sWg + sbg)
        y = y + sh @ sWd + sbd
        return y.reshape(orig_shape)
    h = _L0_tok_ref(x, L0_tok_patch_w, L0_tok_patch_b, L0_tok_ln_g, L0_tok_ln_b, L0_tok_qkv_w, L0_tok_qkv_b, L0_tok_proj_w, L0_tok_proj_b, L0_tok_ff1_w, L0_tok_ff1_b, L0_tok_ff2_w, L0_tok_ff2_b)
    h = jnp.concatenate([h, txt], axis=1)
    h = h + _L0_attn_ref(_layernorm(h, axis=-1), L0_attn_Wqkv_w, L0_attn_Wqkv_b, L0_attn_sel_w, L0_attn_sel_b, L0_attn_out_w, L0_attn_out_b, L0_attn_temperature)
    h = h + _L0_ffn_ref(_layernorm(h, axis=-1), L0_ffn_gate_w, L0_ffn_gate_b, L0_ffn_bias, L0_ffn_Wu, L0_ffn_bu, L0_ffn_Wg, L0_ffn_bg, L0_ffn_Wd, L0_ffn_bd, L0_ffn_sWu, L0_ffn_sbu, L0_ffn_sWg, L0_ffn_sbg, L0_ffn_sWd, L0_ffn_sbd)
    return h

_drawn_inputs = setup_inputs


def setup_inputs(seed=0):
    import zlib

    import numpy as np

    out = dict(_drawn_inputs(seed))
    spreads = {'L0_tok_patch_b': (0.0, 0.1),
     'L0_tok_ln_g': (1.0, 0.2),
     'L0_tok_ln_b': (0.0, 0.1),
     'L0_tok_qkv_b': (0.0, 0.482),
     'L0_tok_proj_b': (0.0, 0.1),
     'L0_tok_ff1_b': (0.0, 0.396),
     'L0_tok_ff2_b': (0.0, 0.1),
     'L0_ffn_gate_b': (0.0, 0.8),
     'L0_ffn_bias': (0.0, 0.432),
     'L0_ffn_bu': (0.0, 0.8),
     'L0_ffn_bg': (0.0, 0.8),
     'L0_ffn_bd': (0.0, 0.477),
     'L0_ffn_sbu': (0.0, 0.8),
     'L0_ffn_sbg': (0.0, 0.8),
     'L0_ffn_sbd': (0.0, 0.8)}
    factors = {'L0_tok_qkv_w': 8.0,
     'L0_tok_proj_w': 3.125,
     'L0_attn_Wqkv_w': 8.0,
     'L0_attn_Wqkv_b': 8.0,
     'L0_attn_sel_w': 8.0,
     'L0_attn_sel_b': 64.0,
     'L0_attn_out_w': 8.0,
     'L0_attn_out_b': 8.0,
     'L0_ffn_gate_w': 7.015,
     'L0_ffn_Wu': 8.0,
     'L0_ffn_Wg': 8.0,
     'L0_ffn_Wd': 8.0,
     'L0_ffn_sWu': 8.0,
     'L0_ffn_sWg': 8.0,
     'L0_ffn_sWd': 8.0}
    for name, (base, spread) in spreads.items():
        noise = np.random.default_rng([zlib.crc32(name.encode()), seed]).standard_normal(out[name].shape)
        drawn = base * np.exp(spread * noise) if base else spread * noise
        out[name] = jnp.asarray(drawn.astype(out[name].dtype))
    for name, factor in factors.items():
        out[name] = (out[name] * factor).astype(out[name].dtype)
    return out
```

```python
from contextlib import ExitStack

import numpy as np

import concourse.bass as bass
from concourse import mybir

F32 = mybir.dt.float32
F32R = mybir.dt.float32r
ALU = mybir.AluOpType
ACT = mybir.ActivationFunctionType
AXX = mybir.AxisListType.X

IMAGES, CHANNELS, SIDE, PATCH = 8, 3, 128, 16
GRID = SIDE // PATCH
IMG_TOK = GRID * GRID
TXT_TOK = 32
TOK = IMG_TOK + TXT_TOK
DIM, HEADS, HEAD = 192, 12, 16
FF = 768
EXPERTS, GROUPS, TOPK, HID, ROUTE_SCALE = 16, 8, 4, 128, 2.5
PICKED = 10
EPS = 1e-5
FA, FB = 128, 64
HALF_IMG = IMAGES // 2
T1, H1 = IMAGES * IMG_TOK, HALF_IMG * IMG_TOK
T2, H2N = IMAGES * TOK, HALF_IMG * TOK
PK = CHANNELS * PATCH * PATCH // 128
FK = FF // 128
CH = 96
CHH = CH // HEAD
SLOTS = IMAGES * PICKED
QROWS = HEADS * PICKED
WPACK = 4 * HID + DIM + 2
DOWN0, BU, BG = 4 * HID, 4 * HID + DIM, 4 * HID + DIM + 1
LOW, GONE = -3.3e38, -3.0e38
DOWN_HI, DOWN_LO = {"A": slice(0, FA), "B": slice(FA, DIM)}, {"A": slice(DIM + FB, 2 * DIM), "B": slice(DIM, DIM + FB)}
B_BOTH = slice(FA, FA + 2 * FB)
VSEL = DIM + 2


def layout(parts):
    at, out = 0, {}
    for name, width in parts:
        out[name] = (at, at + width)
        at += width
    return out, at


CONST, NCONST = layout([("ident", 128), ("pe", DIM), ("causal", TOK), ("tri", TOK), ("head", CHH),
                        ("parity", 2), ("block", IMAGES), ("iota", PICKED)])
COLS, NCOLS = layout([("ff1_b", FK), ("ff2_bA", 1), ("ff2_bB", 1), ("q_b", 2), ("k_b", 2), ("aq_b", 2),
                      ("ak_b", 2), ("gate_b", 1), ("sbdA", 1), ("sbdB", 1)])
ROWS, NROWS = layout([("patch_b", DIM), ("ln_g", DIM), ("ln_b", DIM), ("v_b", DIM), ("proj_b", DIM),
                      ("ff2_b", DIM), ("av_b", DIM), ("out_b", DIM), ("sel_b", 2), ("bias", EXPERTS),
                      ("temp", 1)])


def build(nc, d):
    with ExitStack() as ctx:
        def sb(name, shape, dt=F32):
            return ctx.enter_context(nc.sbuf_tensor(name, shape, dt))

        def sem(name):
            return ctx.enter_context(nc.semaphore(name))

        bank = [ctx.enter_context(nc.psum_tensor(f"bank{i}", [128, 512], F32)) for i in range(8)]

        const = sb("const", [128, NCONST])
        cols = sb("cols", [128, NCOLS])
        rows = sb("rows", [128, NROWS])
        ff2_raw = sb("ff2_raw", [128, FK, DIM])
        proj_w = sb("proj_w", [128, 2, DIM])
        kv_raw = sb("kv_raw", [128, 2 * (DIM + VSEL)])
        aq_w = sb("aq_w", [128, 2, DIM])
        out_w = sb("out_w", [CH, 2, DIM])
        gate_raw = sb("gate_raw", [128, 2 * EXPERTS])
        bd_raw = sb("bd_raw", [48, DIM])
        expert_raw = sb("expert_raw", [128, 2, WPACK])
        kv_w = sb("kv_w", [128, 2, 2 * (DIM + VSEL)], F32R)
        gate_w = sb("gate_w", [128, 2, 2 * EXPERTS], F32R)
        bd_w = sb("bd_w", [48, 2, DIM], F32R)
        minus_half = sb("minus_half", [128, 4])
        x1 = sb("x1", [128, 4, DIM])
        x1b = sb("x1b", [128, 4, DIM])
        tA = sb("tA", [128, 2, T2], F32R)
        tB = sb("tB", [128, T2], F32R)
        act1 = sb("act1", [128, 2, FK, H1])
        v_blk = sb("v_blk", [128, IMAGES, 3, 64])
        h = sb("h", [TOK, IMAGES, DIM])
        st2 = sb("st2", [TOK, IMAGES, 6])
        mv2 = sb("mv2", [TOK, IMAGES, 2])
        ve2 = sb("ve2", [TOK, IMAGES])
        rs2 = sb("rs2", [TOK, IMAGES])
        xn = sb("xn", [TOK, IMAGES, DIM])
        pT = sb("pT", [IMAGES, TOK + 8])
        last2 = sb("last2", [IMAGES, 8])
        aq_blk = sb("aq_blk", [CH, 2, IMAGES, QROWS])
        h2 = sb("h2", [TOK, IMAGES, 256])
        grp = sb("grp", [TOK, IMAGES, GROUPS + 4])
        grp_val = sb("grp_val", [TOK, IMAGES, 8])
        exq = sb("exq", [TOK, IMAGES, EXPERTS + 4])
        exq_val = sb("exq_val", [TOK, IMAGES, 8])
        wT = sb("wT", [48, T2], F32R)
        ones2 = sb("ones2", [2, 128], F32R)

        first_life = ExitStack()

        def sb1(name, shape, dt=F32):
            return first_life.enter_context(nc.sbuf_tensor(name, shape, dt))

        ff1_w = sb1("ff1_w", [128, 2, 2 * FF], F32R)
        qkv_w = sb1("qkv_w", [128, 2, 2 * 3 * DIM], F32R)
        x = sb1("x", [128, 4, DIM])
        xpb = sb1("xpb", [128, 4, DIM])
        yA = sb1("yA", [128, 2, T1], F32R)
        yB = sb1("yB", [128, T1], F32R)
        ytmp = sb1("ytmp", [FB, T1])
        ybf = sb1("ybf", [FB, T1])
        bqm = sb1("bqm", [CH, 2, 2])
        smax = sb1("smax", [128, 2, 3, 8])
        ssum = sb1("ssum", [128, 2, 3, 8])
        srec = sb1("srec", [128, 2, 3, 8])

        with ExitStack() as early:
            def sb0(name, shape, dt=F32):
                return early.enter_context(nc.sbuf_tensor(name, shape, dt))

            patches = sb0("patches", [128, 4, PK, 128])
            patch_w = sb0("patch_w", [128, PK, DIM])
            ff1_raw = sb0("ff1_raw", [128, 2 * FF])
            qkv_raw = sb0("qkv_raw", [128, 2 * 3 * DIM])
            x0 = sb0("x0", [128, 4, DIM])
            st1 = sb0("st1", [128, 4, 6])
            mv1 = sb0("mv1", [128, 4, 2])
            ve1 = sb0("ve1", [128, 4])
            rs1 = sb0("rs1", [128, 4])
            bpe = sb0("bpe", [128, DIM])
            ff2_w = sb0("ff2_w", [128, FK, 2 * DIM], F32R)
            act1s = sb0("act1s", [128, 2, 2, FK, H1], F32R)

        q_blk = sb1("q_blk", [CH, 2, IMAGES, 2, IMG_TOK])
        kT = sb1("kT", [CH, 2, T1])
        prob = sb1("prob", [128, 2, 3, 512])
        probT = sb1("probT", [128, 2, 3, 512])
        otmp = sb1("otmp", [64, 2, 3, H1])
        o01 = sb1("o01", [128, T1])
        o2 = sb1("o2", [64, T1])

        first_life.close()

        ug_w = [sb(f"ug_w{p}", [128, 2, 4 * HID], F32R) for p in range(2)]
        dn_w = [sb(f"dn_w{p}", [128, 2 * DIM], F32R) for p in range(2)]
        xn2 = sb("xn2", [TOK, IMAGES, DIM])
        st3 = sb("st3", [TOK, IMAGES, 6])
        mv3 = sb("mv3", [TOK, IMAGES, 2])
        ve3 = sb("ve3", [TOK, IMAGES])
        rs3 = sb("rs3", [TOK, IMAGES])
        glT = sb("glT", [EXPERTS, T2])
        gmax = sb("gmax", [TOK, IMAGES])
        gexp = sb("gexp", [TOK, IMAGES, EXPERTS])
        gsum = sb("gsum", [TOK, IMAGES])
        grec = sb("grec", [TOK, IMAGES])
        score = sb("score", [TOK, IMAGES, EXPERTS])
        sbias = sb("sbias", [TOK, IMAGES, EXPERTS])
        grp_top = sb("grp_top", [TOK, IMAGES, 8])
        grp_out = sb("grp_out", [TOK, IMAGES, GROUPS + 4])
        grp_in = sb("grp_in", [TOK, IMAGES, GROUPS])
        grp_low = sb("grp_low", [TOK, IMAGES, GROUPS])
        smask = sb("smask", [TOK, IMAGES, EXPERTS])
        exq_top = sb("exq_top", [TOK, IMAGES, 8])
        exq_out = sb("exq_out", [TOK, IMAGES, EXPERTS + 4])
        exq_in = sb("exq_in", [TOK, IMAGES, EXPERTS])
        wfull = sb("wfull", [TOK, IMAGES, EXPERTS])
        silu = [sb(f"silu{i}", [128, H2N]) for i in range(2)]
        gated = [sb(f"gated{i}", [128, H2N]) for i in range(2)]
        hid = [sb(f"hid{i}", [128, H2N]) for i in range(2)]
        hid_s = [sb(f"hid_s{p}", [128, 2, T2], F32R) for p in range(2)]
        fin_tmp = sb("fin_tmp", [FB, T2])
        finA = sb("finA", [FA, T2])
        finB = sb("finB", [FB, T2])

        with ExitStack() as second_life:
            def sb2(name, shape, dt=F32):
                return second_life.enter_context(nc.sbuf_tensor(name, shape, dt))

            hx = sb2("hx", [TOK, IMAGES, DIM])
            akT = sb2("akT", [CH, 2, T2])
            av = sb2("av", [TOK, IMAGES, DIM])
            itemp = sb2("itemp", [TOK, 1])
            lg = sb2("lg", [TOK, IMAGES, 2])
            lgt = sb2("lgt", [TOK, IMAGES, 2])
            lmax = sb2("lmax", [TOK, IMAGES])
            ld = sb2("ld", [TOK, IMAGES, 2])
            le = sb2("le", [TOK, IMAGES, 2])
            lsum = sb2("lsum", [TOK, IMAGES])
            lrec = sb2("lrec", [TOK, IMAGES])
            psel = sb2("psel", [TOK, IMAGES])
            pT8 = sb2("pT8", [IMAGES, TOK + 8])
            pT10 = sb2("pT10", [IMAGES, TOK + 8])
            top8 = sb2("top8", [IMAGES, 8])
            next8 = sb2("next8", [IMAGES, 8])
            pickT = sb2("pickT", [IMAGES, TOK])
            pick = sb2("pick", [TOK, IMAGES])
            rank = sb2("rank", [TOK, IMAGES])
            hot = sb2("hot", [TOK, IMAGES, PICKED])
            hot_heads = sb2("hot_heads", [TOK, IMAGES, QROWS])
            hotp = sb2("hotp", [TOK, IMAGES, PICKED])
            hotpT = sb2("hotpT", [SLOTS, IMAGES, TOK])
            xsA = sb2("xsA", [FA, SLOTS])
            xsB = sb2("xsB", [FB, SLOTS])
            aq = sb2("aq", [CH, 2, SLOTS])
            aprob = sb2("aprob", [QROWS, 2, H2N])
            amax = sb2("amax", [QROWS, IMAGES])
            asum = sb2("asum", [QROWS, IMAGES])
            arec = sb2("arec", [QROWS, IMAGES])
            aprobT = sb2("aprobT", [TOK, 2, HALF_IMG * QROWS])
            actx = sb2("actx", [CH, 2, 2 * HALF_IMG, 60])
            ctxT = sb2("ctxT", [CH, 2, 2, HALF_IMG * PICKED])
            arow = sb2("arow", [SLOTS, DIM])

        wrow = sb("wrow", [2, EXPERTS * T2], F32R)

        def f(ap):
            return ap.bitcast(F32)

        def c(name, n=128, i=None):
            a, b = CONST[name]
            return const[0:n, a:b]

        def col(name, n, i=0):
            a = COLS[name][0] + i
            return cols[0:n, a:a + 1]

        def row(name, p0, p1):
            a, b = ROWS[name]
            return rows[p0:p1, a:b]

        def v3(ap, n):
            return ap.rearrange("p (a b) -> p a b", b=n)

        d_patch = [sem(f"d_patch{i}") for i in range(4)]
        (d_pw, d_const, d_cols, d_rows, d_ff1, d_ff2, d_qkv, d_proj, d_kv, d_aq, d_outw, d_gate, d_bd,
         d_txt, d_wrow, d_out) = [sem("d_" + n) for n in (
             "patch_w", "const", "cols", "rows", "ff1", "ff2", "qkv", "proj", "kv", "aq", "out_w", "gate",
             "bd", "txt", "wrow", "out")]
        d_raw = [sem(f"d_expert{p}") for p in range(2)]

        s = {n: sem(n) for n in (
            "patch_ps", "x0_done", "mv1_done", "rs1_done", "x_done", "xpb_done", "xT_ps", "tA_hi", "tB_hi",
            "tA_lo", "tB_lo", "ff1_hi", "ff1_lo", "ff2_hi", "ff2_lo", "qkv_hi", "qkv_lo", "hid1_ps",
            "gelu_done", "act1_hi", "act1_lo", "y_ps", "yA_hi", "yB_moved", "yB_sum", "yA_lo", "yB_hi", "yB_lo",
            "qk_ps", "bqm_done", "q_done", "k_done", "v_ps", "v_done", "s_ps", "s_sub",
            "s_exp", "s_norm", "pT_ps", "pT_act", "pT_vec", "o_ps", "o_even", "o_done", "proj_ps", "x1_done",
            "x1b_done", "hid2_ps", "gelu2_done", "ff2_ps", "h_img", "zeros_done",
            "mv2_done", "rs2_done", "xn_done", "hx_done", "hT_ps", "kv_split", "vsel_ps", "av_done", "ak_ps",
            "ak_even", "ak_odd", "ld_done", "le_done", "psel_done", "psT_ps", "pickT_done", "pick_ps",
            "pick_done", "cum_ps", "hot_done", "hot_spread", "xs_ps", "xs_done", "aq_ps", "aq_done", "hotpT_ps",
            "hotpT_done", "as_ps", "as_sub", "as_exp", "as_norm", "apT_ps", "apT_done", "ac_ps", "ac_done",
            "ao_ps", "ao_done", "h2_ps", "h2_done",
            "mv3_done", "rs3_done", "xn2_done", "h2T_ps", "gate_split", "bd_split", "gl_ps", "gl_done",
            "glt_ps", "gd_done", "ge_done", "wfull_done", "wT_ps", "wT_hi", "wT_lo", "init_done",
            "ug_hi", "ug_lo", "dn_hi", "dn_lo", "u_ps0", "u_ps1", "g_ps0", "g_ps1", "silu0", "silu1",
            "gated0", "gated1", "wb_ps", "weighed", "hid_hi", "hid_lo", "down_done", "fin_moved", "finA_done",
            "finB_done", "gp_step", "vec_step")}

        def chain(eng, signal):
            count = [0]

            def step(ins):
                count[0] += 1
                ins.then_inc(s[signal], 1)
                return count[0]

            def after(k):
                eng.wait_ge(s[signal], k)
            return step, after

        block = ctx.enter_context(nc.Block())

        @block.sync
        def _(sp):
            sp.dma_start(patches[:, 0], d["patches"][0]).then_inc(d_patch[0], 16)
            sp.dma_start(patch_w[:], d["patch_w"]).then_inc(d_pw, 16)
            sp.dma_start(patches[:, 1], d["patches"][1]).then_inc(d_patch[1], 16)
            sp.dma_start(rows[:, :], d["rows"].to_broadcast([128, NROWS])).then_inc(d_rows, 16)
            sp.dma_start(patches[:, 2], d["patches"][2]).then_inc(d_patch[2], 16)
            sp.dma_start(const[:, :], d["const"]).then_inc(d_const, 16)
            sp.dma_start(patches[:, 3], d["patches"][3]).then_inc(d_patch[3], 16)
            sp.dma_start(ff1_raw[:, :], d["ff1"]).then_inc(d_ff1, 16)
            sp.dma_start(cols[:, :], d["cols"]).then_inc(d_cols, 16)
            sp.dma_start(ff2_raw[:, :, :], d["ff2"]).then_inc(d_ff2, 16)
            sp.dma_start(qkv_raw[:, :], d["qkv"]).then_inc(d_qkv, 16)
            sp.dma_start(proj_w[:, :, :], d["proj"]).then_inc(d_proj, 16)
            sp.dma_start(kv_raw[:, :], d["kv"]).then_inc(d_kv, 16)
            sp.dma_start(h[IMG_TOK:TOK, :, :], d["txt"]).then_inc(d_txt, 16)
            sp.dma_start(aq_w[:, :, :], d["aq"]).then_inc(d_aq, 16)
            sp.dma_start(out_w[:, :, :], d["out_w"]).then_inc(d_outw, 16)
            sp.dma_start(gate_raw[:, :], d["gate"]).then_inc(d_gate, 16)
            sp.dma_start(bd_raw[:, :], d["bd"]).then_inc(d_bd, 16)
            for n in range(2):
                sp.dma_start(expert_raw[:, n, :], d["experts"][n]).then_inc(d_raw[n], 16)
            sp.wait_ge(s["wT_lo"], 2)
            for part in range(2):
                sp.dma_start(f(wrow[part:part + 1, :]).rearrange("p (e t) -> p e t", e=EXPERTS),
                             f(wT[32 * part:32 * part + EXPERTS, :])).then_inc(d_wrow, 16)

            def load(n, p):
                source = d["experts"][n] if isinstance(n, int) else d["experts"][bass.ds(n, 1), :, :]
                sp.wait_ge(s["gated1"], n - 1)
                sp.dma_start(expert_raw[:, p, :], source).then_inc(d_raw[p], 16)

            load(2, 0)
            load(3, 1)
            with sp.Fori(0, 6) as it:
                load(2 * it + 4, 0)
                load(2 * it + 5, 1)
            load(16, 0)
            sp.wait_ge(s["finA_done"], 1)
            sp.dma_start(d["out"][0:FA, :], finA[:, :]).then_inc(d_out, 16)
            sp.wait_ge(s["finB_done"], 1)
            sp.dma_start(d["out"][FA:DIM, :], finB[:, :]).then_inc(d_out, 16)
            sp.wait_ge(d_out, 32)

        @block.gpsimd
        def _(gp):
            g = nc.gpsimd
            step, after = chain(gp, "gp_step")
            step(g.memset(minus_half[:, :], -0.5))
            g.memset(v_blk[:, :, :, :], 0.0).then_inc(s["zeros_done"], 1)
            g.memset(aq_blk[:, :, :, :], 0.0).then_inc(s["zeros_done"], 1)
            g.memset(h2[:, :, DIM:256], 0.0).then_inc(s["zeros_done"], 1)
            g.memset(f(bd_w[:, :, :]), 0.0).then_inc(s["zeros_done"], 1)
            g.memset(f(wT[:, :]), 0.0).then_inc(s["zeros_done"], 1)
            g.memset(f(ones2[:, :]), 1.0).then_inc(s["zeros_done"], 1)
            g.memset(pT[:, TOK:TOK + 8], LOW).then_inc(s["zeros_done"], 1)
            g.memset(last2[:, 2:8], LOW).then_inc(s["zeros_done"], 1)
            g.memset(grp[:, :, GROUPS:GROUPS + 4], LOW).then_inc(s["zeros_done"], 1)
            g.memset(grp_val[:, :, 4:8], LOW).then_inc(s["zeros_done"], 1)
            g.memset(exq[:, :, EXPERTS:EXPERTS + 4], LOW).then_inc(s["zeros_done"], 1)
            g.memset(exq_val[:, :, 4:8], LOW).then_inc(s["zeros_done"], 1)

            def rsqrt(ve, mv, rs, lo, hi, n, done):
                k = step(g.tensor_scalar(ve[:, lo:hi], mv[:, lo:hi, 1], EPS, 1.0, ALU.add, ALU.mult))
                after(k)
                g.tensor_tensor(rs[:, lo:hi], ve[:, lo:hi], minus_half[0:n, 0:hi - lo], ALU.pow)\
                    .then_inc(s[done], 1)

            for hf in range(2):
                gp.wait_ge(s["mv1_done"], 2 * hf + 2)
                rsqrt(ve1, mv1, rs1, 2 * hf, 2 * hf + 2, 128, "rs1_done")
            for hf in range(2):
                gp.wait_ge(s["x_done"], hf + 1)
                t = slice(2 * hf, 2 * hf + 2)
                g.tensor_tensor(xpb[:, t, :], x[:, t, :],
                                row("proj_b", 0, 128).unsqueeze(1).to_broadcast([128, 2, DIM]), ALU.add)\
                    .then_inc(s["xpb_done"], 1)
            gp.wait_ge(d_kv, 16)
            k = step(g.tensor_scalar(kv_w[:, 0, :], kv_raw[:, :], 1.0, 1.0, ALU.mult, ALU.mult))
            after(k)
            g.tensor_tensor(kv_w[:, 1, :], kv_raw[:, :], f(kv_w[:, 0, :]), ALU.subtract)\
                .then_inc(s["kv_split"], 1)
            gp.wait_ge(d_gate, 16)
            k = step(g.tensor_scalar(gate_w[:, 0, :], gate_raw[:, :], 1.0, 1.0, ALU.mult, ALU.mult))
            after(k)
            g.tensor_tensor(gate_w[:, 1, :], gate_raw[:, :], f(gate_w[:, 0, :]), ALU.subtract)\
                .then_inc(s["gate_split"], 1)
            gp.wait_ge(d_bd, 16)
            gp.wait_ge(s["zeros_done"], 12)
            for p0 in (0, 32):
                k = step(g.tensor_scalar(bd_w[p0:p0 + EXPERTS, 0, :], bd_raw[p0:p0 + EXPERTS, :], 1.0, 1.0,
                                         ALU.mult, ALU.mult))
                after(k)
            g.tensor_tensor(bd_w[0:EXPERTS, 1, :], bd_raw[0:EXPERTS, :], f(bd_w[0:EXPERTS, 0, :]),
                            ALU.subtract).then_inc(s["bd_split"], 1)
            for hf in range(2):
                gp.wait_ge(s["x1_done"], hf + 1)
                t = slice(2 * hf, 2 * hf + 2)
                g.tensor_tensor(x1b[:, t, :], x1[:, t, :],
                                row("ff2_b", 0, 128).unsqueeze(1).to_broadcast([128, 2, DIM]), ALU.add)\
                    .then_inc(s["x1b_done"], 1)
            for hf in range(2):
                gp.wait_ge(s["mv2_done"], hf + 1)
                rsqrt(ve2, mv2, rs2, 4 * hf, 4 * hf + 4, TOK, "rs2_done")
            for hf in range(2):
                gp.wait_ge(s["xn_done"], hf + 1)
                b = slice(4 * hf, 4 * hf + 4)
                g.tensor_tensor(hx[:, b, :], h[:, b, :], xn[:, b, :], ALU.add).then_inc(s["hx_done"], 1)
            for hf in range(2):
                gp.wait_ge(s["mv3_done"], hf + 1)
                rsqrt(ve3, mv3, rs3, 4 * hf, 4 * hf + 4, TOK, "rs3_done")

        @block.tensor
        def _(pe):
            mm, tr = nc.tensor.matmul, nc.tensor.transpose

            def five(out, wA, wAl, wB, wBl, aA, aAl, aB, aBh, start=True):
                mm(out, wA, aA, start=start, stop=False)
                mm(out, wAl, aA, start=False, stop=False)
                mm(out, wA, aAl, start=False, stop=False)
                mm(out, wBl, aBh, start=False, stop=False)
                return mm(out, wB, aB, start=False, stop=True)

            def w_still(out, w, a0, b0, n, tok, lay=(tA, tB)):
                A, B = lay
                return five(out, w[:, 0, a0:a0 + n], w[:, 1, a0:a0 + n], w[:, 0, b0:b0 + n],
                            w[0:FB, 1, b0:b0 + n], A[:, 0, tok], A[:, 1, tok], B[:, tok], B[0:FB, tok])

            def x_still(out, w, a0, b0, n, tok, lay=(tA, tB)):
                A, B = lay
                mm(out, A[:, 0, tok], w[:, 0, a0:a0 + n], start=True, stop=False)
                mm(out, A[:, 0, tok], w[:, 1, a0:a0 + n], start=False, stop=False)
                mm(out, A[:, 1, tok], w[:, 0, a0:a0 + n], start=False, stop=False)
                mm(out, B[0:FB, tok], w[0:FB, 1, b0:b0 + n], start=False, stop=False)
                return mm(out, B[:, tok], w[:, 0, b0:b0 + n], start=False, stop=True)

            pe.wait_ge(d_pw, 16)
            for t in range(4):
                pe.wait_ge(d_patch[t], 16)
                out = bank[t][:, 0:DIM]
                for k in range(PK):
                    last = mm(out, patches[:, t, k, :], patch_w[:, k, :], start=(k == 0), stop=(k == PK - 1))
                last.then_inc(s["patch_ps"], 1)

            def turn_x(src, hf, atA, atB, done):
                for i in range(2):
                    t = 2 * hf + i
                    tr(atA[:, 128 * i:128 * i + 128], src[:, t, 0:FA], c("ident"))
                    last = tr(atB[0:FB, 128 * i:128 * i + 128], src[:, t, FA:DIM], c("ident"))
                last.then_inc(s[done], 1)

            pe.wait_ge(d_const, 16)
            for hf in range(2):
                pe.wait_ge(s["x_done"], hf + 1)
                turn_x(x, hf, bank[4 + 2 * hf], bank[5 + 2 * hf], "xT_ps")

            pe.wait_ge(s["ff1_lo"], 1)
            for hf in range(2):
                for sig in ("tA_hi", "tA_lo", "tB_lo"):
                    pe.wait_ge(s[sig], hf + 1)
                for m in range(FK):
                    i = FK * hf + m
                    if i >= 4:
                        pe.wait_ge(s["gelu_done"], i - 3)
                    w_still(bank[i % 4][:, 0:H1], ff1_w, 128 * m, FF + 128 * m, 128,
                            slice(H1 * hf, H1 * hf + H1)).then_inc(s["hid1_ps"], 1)
            pe.wait_ge(s["ff2_lo"], 2)
            for hf in range(2):
                outA, outB = bank[6 + hf][:, 0:H1], bank[6 + hf][:, H1:2 * H1]
                for part, out in ((0, outA), (1, outB)):
                    for k in range(FK):
                        if part == 0:
                            pe.wait_ge(s["act1_lo"], FK * hf + k + 1)
                        hi, lo = act1s[:, hf, 0, k, :], act1s[:, hf, 1, k, :]
                        if part == 0:
                            mm(out, ff2_w[:, k, DOWN_HI["A"]], hi, start=(k == 0), stop=False)
                            mm(out, ff2_w[:, k, DOWN_LO["A"]], hi, start=False, stop=False)
                            last = mm(out, ff2_w[:, k, DOWN_HI["A"]], lo, start=False, stop=(k == FK - 1))
                        else:
                            mm(out, ff2_w[:, k, B_BOTH], hi, start=(k == 0), stop=False,
                               skip_group_check=True)
                            last = mm(out[0:FB, :], ff2_w[:, k, DOWN_HI["B"]], lo, start=False,
                                      stop=(k == FK - 1), skip_group_check=True)
                last.then_inc(s["y_ps"], 1)

            pe.wait_ge(s["qkv_lo"], 1)
            for hf in range(2):
                for sig in ("yA_lo", "yB_lo"):
                    pe.wait_ge(s[sig], hf + 1)
                tok = slice(H1 * hf, H1 * hf + H1)
                for part in range(2):
                    for ch in range(2):
                        last = w_still(bank[4 + 2 * hf + part][0:CH, H1 * ch:H1 * ch + H1], qkv_w,
                                       DIM * part + CH * ch, 3 * DIM + DIM * part + CH * ch, CH, tok, (yA, yB))
                last.then_inc(s["qk_ps"], 1)
                for i in range(2):
                    t = 2 * hf + i
                    last = x_still(bank[2 + hf][:, DIM * i:DIM * i + DIM], qkv_w, 2 * DIM, 5 * DIM, DIM,
                                   slice(128 * t, 128 * t + 128), (yA, yB))
                last.then_inc(s["v_ps"], 1)

            for hf in range(2):
                pe.wait_ge(s["q_done"], 4 * hf + 4)
                pe.wait_ge(s["k_done"], 2 * hf + 2)
                pe.wait_ge(s["v_done"], 4 * hf + 4)
                for j in range(3):
                    out = bank[3 * hf + j]
                    for b in range(HALF_IMG):
                        for ch in range(2):
                            i = HALF_IMG * hf + b
                            last = mm(out[:, 64 * (2 * b + ch):64 * (2 * b + ch) + 64],
                                      q_blk[32 * j:32 * j + 32, ch, i, :, :],
                                      kT[32 * j:32 * j + 32, ch, IMG_TOK * i:IMG_TOK * i + IMG_TOK],
                                      start=True, stop=True)
                    last.then_inc(s["s_ps"], 1)
            for hf in range(2):
                for j in range(3):
                    pe.wait_ge(s["s_norm"], 3 * hf + j + 1)
                    for b in range(HALF_IMG):
                        last = tr(bank[3 * hf + j][:, 128 * b:128 * b + 128],
                                  prob[:, hf, j, 128 * b:128 * b + 128], c("ident"))
                    last.then_inc(s["pT_ps"], 1)
                for j in range(3):
                    if j == 1:
                        pe.wait_ge(s["pT_vec"], hf + 1)
                    else:
                        pe.wait_ge(s["pT_act"], 2 * hf + 1 + j // 2)
                    for b in range(HALF_IMG):
                        last = mm(bank[3 * hf + j][0:64, 128 * b:128 * b + 128],
                                  v_blk[:, HALF_IMG * hf + b, j, :], probT[:, hf, j, 128 * b:128 * b + 128],
                                  start=True, stop=True)
                    last.then_inc(s["o_ps"], 1)
            pe.wait_ge(d_proj, 16)
            for hf in range(2):
                pe.wait_ge(s["o_done"], 3 * hf + 3)
                for i in range(2):
                    tok = slice(128 * (2 * hf + i), 128 * (2 * hf + i) + 128)
                    out = bank[6 + hf][:, DIM * i:DIM * i + DIM]
                    mm(out, o01[:, tok], proj_w[:, 0, :], start=True, stop=False)
                    last = mm(out, o2[:, tok], proj_w[0:64, 1, :], start=False, stop=True)
                last.then_inc(s["proj_ps"], 1)

            for hf in range(2):
                pe.wait_ge(s["x1_done"], hf + 1)
                turn_x(x1, hf, bank[2 * hf], bank[2 * hf + 1], "xT_ps")
            for hf in range(2):
                for sig in ("tA_hi", "tA_lo", "tB_lo"):
                    pe.wait_ge(s[sig], hf + 3)
                for m in range(FK):
                    i = FK * hf + m
                    if i >= 4:
                        pe.wait_ge(s["gelu2_done"], i - 3)
                    w_still(bank[4 + i % 4][:, 0:H1], ff1_w, 128 * m, FF + 128 * m, 128,
                            slice(H1 * hf, H1 * hf + H1)).then_inc(s["hid2_ps"], 1)
            for hf in range(2):
                for i in range(2):
                    out = bank[2 + hf][:, DIM * i:DIM * i + DIM]
                    for k in range(FK):
                        if i == 0:
                            pe.wait_ge(s["gelu2_done"], FK * hf + k + 1)
                        last = mm(out, act1[:, hf, k, 128 * i:128 * i + 128], ff2_raw[:, k, :],
                                  start=(k == 0), stop=(k == FK - 1))
                last.then_inc(s["ff2_ps"], 1)

            def turn_h(src, hf, atA, atB, done):
                for i in range(HALF_IMG):
                    b = HALF_IMG * hf + i
                    tr(atA[:, TOK * i:TOK * i + TOK], src[:, b, 0:FA], c("ident", TOK)[:, 0:TOK])
                    last = tr(atB[0:FB, TOK * i:TOK * i + TOK], src[:, b, FA:DIM], c("ident", TOK)[:, 0:TOK])
                last.then_inc(s[done], 1)

            for hf in range(2):
                pe.wait_ge(s["xn_done"], hf + 1)
                turn_h(xn, hf, bank[2 * hf], bank[2 * hf + 1], "hT_ps")
            pe.wait_ge(s["kv_split"], 1)
            for i in range(4):
                if i % 2 == 0:
                    for sig in ("tA_hi", "tA_lo", "tB_lo"):
                        pe.wait_ge(s[sig], i // 2 + 5)
                for k in range(2):
                    b = 2 * i + k
                    last = x_still(bank[4 + i][0:TOK, VSEL * k:VSEL * k + VSEL], kv_w, DIM,
                                   2 * DIM + VSEL, VSEL, slice(TOK * b, TOK * b + TOK))
                last.then_inc(s["vsel_ps"], 1)
            for hf in range(2):
                for ch in range(2):
                    last = w_still(bank[2 * hf + ch][0:CH, 0:H2N], kv_w, CH * ch, DIM + VSEL + CH * ch, CH,
                                   slice(H2N * hf, H2N * hf + H2N))
                last.then_inc(s["ak_ps"], 1)
            pe.wait_ge(s["psel_done"], 1)
            tr(bank[4][0:IMAGES, 0:TOK], psel[:, :], c("ident", TOK)[:, 0:TOK]).then_inc(s["psT_ps"], 1)
            pe.wait_ge(s["pickT_done"], 1)
            tr(bank[4][0:TOK, 128:128 + IMAGES], pickT[:, :], c("ident", IMAGES)[:, 0:IMAGES])\
                .then_inc(s["pick_ps"], 1)
            pe.wait_ge(s["pick_done"], 1)
            mm(bank[4][0:TOK, 256:256 + IMAGES], c("tri", TOK), pick[:, :], start=True, stop=True)\
                .then_inc(s["cum_ps"], 1)
            pe.wait_ge(s["hot_done"], 2)
            for b in range(IMAGES):
                mm(bank[5][:, PICKED * b:PICKED * b + PICKED], xn[:, b, 0:FA], hot[:, b, :],
                   start=True, stop=True)
                last = mm(bank[6][0:FB, 256 + PICKED * b:256 + PICKED * b + PICKED], xn[:, b, FA:DIM],
                          hot[:, b, :], start=True, stop=True)
            last.then_inc(s["xs_ps"], 1)
            tr(bank[7][0:SLOTS, 0:TOK], hotp[:, :, :].rearrange("p a b -> p (a b)"),
               c("ident", TOK)[:, 0:TOK]).then_inc(s["hotpT_ps"], 1)
            pe.wait_ge(s["xs_done"], 2)
            pe.wait_ge(d_aq, 16)
            for ch in range(2):
                out = bank[6][0:CH, SLOTS * ch:SLOTS * ch + SLOTS]
                mm(out, aq_w[:, 0, CH * ch:CH * ch + CH], xsA[:, :], start=True, stop=False)
                last = mm(out, aq_w[0:FB, 1, CH * ch:CH * ch + CH], xsB[:, :], start=False, stop=True)
            last.then_inc(s["aq_ps"], 1)
            for hf in range(2):
                pe.wait_ge(s["ak_even"], hf + 1)
                pe.wait_ge(s["ak_odd"], hf + 1)
                pe.wait_ge(s["aq_done"], 2)
                pe.wait_ge(s["hot_spread"], 1)
                for i in range(HALF_IMG):
                    b = HALF_IMG * hf + i
                    out = bank[hf][0:QROWS, TOK * i:TOK * i + TOK]
                    mm(out, hot_heads[:, b, :], c("causal", TOK),
                       start=True, stop=False)
                    for ch in range(2):
                        last = mm(out, aq_blk[:, ch, b, :], akT[:, ch, TOK * b:TOK * b + TOK],
                                  start=False, stop=(ch == 1))
                last.then_inc(s["as_ps"], 1)
            for hf in range(2):
                pe.wait_ge(s["as_norm"], hf + 1)
                for i in range(HALF_IMG):
                    last = tr(bank[2 + hf][0:TOK, QROWS * i:QROWS * i + QROWS],
                              aprob[:, hf, TOK * i:TOK * i + TOK], c("ident", QROWS)[:, 0:QROWS])
                last.then_inc(s["apT_ps"], 1)
                pe.wait_ge(s["apT_done"], hf + 1)
                for ch in range(2):
                    for i in range(HALF_IMG):
                        at = 60 * (HALF_IMG * ch + i)
                        last = mm(bank[4 + hf][0:CH, at:at + 60], av[:, HALF_IMG * hf + i, CH * ch:CH * ch + CH],
                                  aprobT[:, hf, QROWS * i + 60 * ch:QROWS * i + 60 * ch + 60],
                                  start=True, stop=True)
                last.then_inc(s["ac_ps"], 1)
            pe.wait_ge(s["ac_done"], 4)
            pe.wait_ge(d_outw, 16)
            for ch in range(2):
                last = mm(bank[6][0:SLOTS, 0:DIM], ctxT[:, ch, :, :], out_w[:, ch, :],
                          start=(ch == 0), stop=(ch == 1))
            last.then_inc(s["ao_ps"], 1)
            pe.wait_ge(s["ao_done"], 1)
            pe.wait_ge(s["hotpT_done"], 1)
            for i in range(4):
                for k in range(2):
                    last = mm(bank[(7 + i) % 8][0:TOK, DIM * k:DIM * k + DIM], hotpT[:, 2 * i + k, :],
                              arow[:, :], start=True, stop=True)
                last.then_inc(s["h2_ps"], 1)

            for hf in range(2):
                pe.wait_ge(s["xn2_done"], hf + 1)
                turn_h(xn2, hf, bank[3 + 2 * hf], bank[4 + 2 * hf], "h2T_ps")
            pe.wait_ge(s["gate_split"], 1)
            for hf in range(2):
                for sig in ("tA_hi", "tA_lo", "tB_lo"):
                    pe.wait_ge(s[sig], hf + 7)
                w_still(bank[7 if hf == 0 else 0][0:EXPERTS, 0:H2N], gate_w, 0, EXPERTS, EXPERTS,
                        slice(H2N * hf, H2N * hf + H2N)).then_inc(s["gl_ps"], 1)
            pe.wait_ge(s["gl_done"], 2)
            for b in range(IMAGES):
                last = tr(bank[1][0:TOK, EXPERTS * b:EXPERTS * b + EXPERTS], glT[:, TOK * b:TOK * b + TOK],
                          c("ident", EXPERTS)[:, 0:EXPERTS])
            last.then_inc(s["glt_ps"], 1)

            cuts = ((0, 512, bank[0][:, 0:512], bank[2][:, 0:512]),
                    (512, T2, bank[1][:, 0:256], bank[1][:, 256:512]))

            def up_gate(n, hf, p):
                tok = slice(H2N * hf, H2N * hf + H2N)
                if not isinstance(n, int) or n >= 1:
                    pe.wait_ge(s[f"silu{hf}"], n)
                w_still(bank[3 + 2 * hf][:, 0:H2N], ug_w[p], 0, 2 * HID, HID, tok).then_inc(s[f"u_ps{hf}"], 1)
                if not isinstance(n, int) or n >= 1:
                    pe.wait_ge(s[f"gated{hf}"], n)
                w_still(bank[4 + 2 * hf][:, 0:H2N], ug_w[p], HID, 3 * HID, HID, tok)\
                    .then_inc(s[f"g_ps{hf}"], 1)

            def spread(n, hf):
                if isinstance(n, int):
                    rhs = wrow[:, (n - 1) * T2 + H2N * hf:(n - 1) * T2 + H2N * hf + H2N]
                else:
                    rhs = wrow[:, bass.ds((n - 1) * T2 + H2N * hf, H2N)]
                if not isinstance(n, int) or n > 1 or hf:
                    pe.wait_ge(s["weighed"], 2 * (n - 1) + hf)
                mm(bank[7][:, 0:H2N], ones2[:, :], rhs, start=True, stop=True).then_inc(s["wb_ps"], 1)

            def down(n, part, p):
                a, b, outA, outB = cuts[part]
                hi, lo = hid_s[p][:, 0, a:b], hid_s[p][:, 1, a:b]
                kw = {"start": False, "stop": False, "skip_group_check": True}
                mm(outA, dn_w[p][:, DOWN_HI["A"]], hi, **kw)
                mm(outA, dn_w[p][:, DOWN_LO["A"]], hi, **kw)
                mm(outA, dn_w[p][:, DOWN_HI["A"]], lo, **kw)
                mm(outB, dn_w[p][:, B_BOTH], hi, **kw)
                return mm(outB[0:FB, :], dn_w[p][:, DOWN_HI["B"]], lo, **kw)

            def expert(n, p):
                pe.wait_ge(s["ug_hi"], n + 1)
                pe.wait_ge(s["ug_lo"], n + 1)
                up_gate(n, 0, p)
                spread(n, 0)
                up_gate(n, 1, p)
                pe.wait_ge(s["hid_hi"], 2 * n)
                pe.wait_ge(s["hid_lo"], 2 * n)
                pe.wait_ge(s["dn_hi"], n)
                pe.wait_ge(s["dn_lo"], 2 * n)
                down(n - 1, 0, 1 - p)
                spread(n, 1)
                down(n - 1, 1, 1 - p).then_inc(s["down_done"], 1)

            pe.wait_ge(s["ug_hi"], 1)
            pe.wait_ge(s["ug_lo"], 1)
            up_gate(0, 0, 0)
            up_gate(0, 1, 0)
            pe.wait_ge(s["gd_done"], 1)
            started = set()
            for b in range(IMAGES):
                for t0, t1 in ((TOK * b, min(TOK * b + TOK, 512)), (max(TOK * b, 512), TOK * b + TOK)):
                    if t0 >= t1:
                        continue
                    cut = 0 if t1 <= 512 else 1
                    for part in range(2):
                        which = (cut, part) if cut == 0 else (1, 0)
                        out = cuts[cut][2 + part][:, t0 - cuts[cut][0]:t1 - cuts[cut][0]]
                        a = c("ident", TOK)[:, t0 - TOK * b:t1 - TOK * b]
                        mm(out, h2[:, b, FA * part:FA * part + FA], a, start=which not in started,
                           stop=False, skip_group_check=True)
                        started.add(which)
            for hf in range(2):
                pe.wait_ge(s["wfull_done"], 1)
                if hf == 1:
                    pe.wait_ge(s["wT_lo"], 1)
                for i in range(HALF_IMG):
                    last = tr(bank[7][0:EXPERTS, TOK * i:TOK * i + TOK], wfull[:, HALF_IMG * hf + i, :],
                              c("ident", TOK)[:, 0:TOK])
                last.then_inc(s["wT_ps"], 1)
            pe.wait_ge(s["wT_lo"], 2)
            pe.wait_ge(s["bd_split"], 1)
            for a, b, outA, outB in cuts:
                kw = {"start": False, "stop": False, "skip_group_check": True}
                mm(outA, bd_w[0:48, 0, 0:FA], wT[0:48, a:b], **kw)
                mm(outA, bd_w[0:EXPERTS, 1, 0:FA], wT[0:EXPERTS, a:b], **kw)
                mm(outB[0:FB, :], bd_w[0:48, 0, FA:DIM], wT[0:48, a:b], **kw)
                mm(outB[0:FB, :], bd_w[0:EXPERTS, 1, FA:DIM], wT[0:EXPERTS, a:b], **kw)
            pe.wait_ge(d_wrow, 32)
            expert(1, 1)
            with pe.Fori(0, 7) as it:
                expert(2 * it + 2, 0)
                expert(2 * it + 3, 1)
            expert(16, 0)
            pe.wait_ge(s["hid_hi"], 34)
            pe.wait_ge(s["hid_lo"], 34)
            pe.wait_ge(s["dn_hi"], 17)
            pe.wait_ge(s["dn_lo"], 34)
            down(16, 0, 0)
            down(16, 1, 0).then_inc(s["down_done"], 1)

        @block.scalar
        def _(act):
            a = nc.scalar.activation

            def hi_of_turned(atA, atB, n, tok, done, k):
                act.wait_ge(s[done], k)
                a(tA[:, 0, tok], atA, ACT.Copy).then_inc(s["tA_hi"], 1)
                a(tB[0:FB, tok], atB, ACT.Copy).then_inc(s["tB_hi"], 1)

            act.wait_ge(d_ff1, 16)
            a(ff1_w[:, 0, :], ff1_raw[:, :], ACT.Copy).then_inc(s["ff1_hi"], 1)
            for hf in range(2):
                hi_of_turned(bank[4 + 2 * hf][:, 0:H1], bank[5 + 2 * hf][0:FB, 0:H1], H1,
                             slice(H1 * hf, H1 * hf + H1), "xT_ps", hf + 1)
                if hf == 0:
                    act.wait_ge(d_ff2, 16)
                    a(ff2_w[:, :, 0:DIM], ff2_raw[:, :, :], ACT.Copy).then_inc(s["ff2_hi"], 1)
            act.wait_ge(d_cols, 16)
            for hf in range(2):
                for m in range(FK):
                    i = FK * hf + m
                    act.wait_ge(s["hid1_ps"], i + 1)
                    a(act1[:, hf, m, :], bank[i % 4][:, 0:H1], ACT.Gelu_apprx_tanh,
                      bias=col("ff1_b", 128, m)).then_inc(s["gelu_done"], 1)
                if hf == 0:
                    act.wait_ge(d_qkv, 16)
                    a(qkv_w[:, 0, :], qkv_raw[:, :], ACT.Copy).then_inc(s["qkv_hi"], 1)
            for hf in range(2):
                tok = slice(H1 * hf, H1 * hf + H1)
                act.wait_ge(s["y_ps"], hf + 1)
                a(ytmp[:, tok], bank[6 + hf][FB:128, H1:2 * H1], ACT.Copy).then_inc(s["yB_moved"], 1)
                a(yA[:, 0, tok], bank[6 + hf][:, 0:H1], ACT.Identity, bias=col("ff2_bA", 128))\
                    .then_inc(s["yA_hi"], 1)
                act.wait_ge(s["yB_sum"], hf + 1)
                a(yB[0:FB, tok], ybf[:, tok], ACT.Copy).then_inc(s["yB_hi"], 1)
            act.wait_ge(s["bqm_done"], 2)
            for hf in range(2):
                act.wait_ge(s["qk_ps"], hf + 1)
                for ch in range(2):
                    for par in range(2):
                        a(q_blk[:, ch, HALF_IMG * hf:HALF_IMG * hf + HALF_IMG, par, :],
                          v3(bank[4 + 2 * hf][0:CH, H1 * ch:H1 * ch + H1], IMG_TOK), ACT.Identity,
                          bias=bqm[:, ch, par:par + 1], scale=c("parity", CH)[:, par:par + 1])\
                            .then_inc(s["q_done"], 1)
            for hf in range(2):
                for j in range(3):
                    act.wait_ge(s["s_sub"], 3 * hf + j + 1)
                    a(prob[:, hf, j, :], prob[:, hf, j, :], ACT.Exp, scale=HEAD ** -0.5)\
                        .then_inc(s["s_exp"], 1)
            for hf in range(2):
                for j in (0, 2):
                    act.wait_ge(s["pT_ps"], 3 * hf + j + 1)
                    a(probT[:, hf, j, :], bank[3 * hf + j][:, :], ACT.Copy).then_inc(s["pT_act"], 1)
                for j in range(3):
                    act.wait_ge(s["o_ps"], 3 * hf + j + 1)
                    even = bank[3 * hf + j][0:64, :].rearrange("p (b h q) -> p b h q", h=2, q=IMG_TOK)[:, :, 0, :]
                    a(v3(otmp[:, hf, j, :], IMG_TOK), even, ACT.Copy, scale=c("parity", 64)[:, 0:1])\
                        .then_inc(s["o_even"], 1)
            for hf in range(2):
                hi_of_turned(bank[2 * hf][:, 0:H1], bank[2 * hf + 1][0:FB, 0:H1], H1,
                             slice(H1 * hf, H1 * hf + H1), "xT_ps", hf + 3)
            for hf in range(2):
                for m in range(FK):
                    i = FK * hf + m
                    act.wait_ge(s["hid2_ps"], i + 1)
                    a(act1[:, hf, m, :], bank[4 + i % 4][:, 0:H1], ACT.Gelu_apprx_tanh,
                      bias=col("ff1_b", 128, m)).then_inc(s["gelu2_done"], 1)

            for hf in range(2):
                hi_of_turned(bank[2 * hf][:, 0:H2N], bank[2 * hf + 1][0:FB, 0:H2N], H2N,
                             slice(H2N * hf, H2N * hf + H2N), "hT_ps", hf + 1)
            for hf in range(2):
                act.wait_ge(s["ak_ps"], hf + 1)
                a(akT[:, 0, H2N * hf:H2N * hf + H2N], bank[2 * hf][0:CH, 0:H2N], ACT.Identity,
                  bias=col("ak_b", CH, 0)).then_inc(s["ak_even"], 1)
            act.wait_ge(s["ld_done"], 1)
            a(le[:, :, :], ld[:, :, :], ACT.Exp).then_inc(s["le_done"], 1)
            act.wait_ge(s["hot_done"], 1)
            a(hot_heads[:, :, :].rearrange("p b (h i) -> p b h i", h=HEADS),
              hot[:, :, :].unsqueeze(2).to_broadcast([TOK, IMAGES, HEADS, PICKED]), ACT.Copy)\
                .then_inc(s["hot_spread"], 1)
            act.wait_ge(s["xs_ps"], 1)
            a(xsB[:, :], bank[6][0:FB, 256:256 + SLOTS], ACT.Copy).then_inc(s["xs_done"], 1)
            for hf in range(2):
                act.wait_ge(s["as_sub"], hf + 1)
                a(aprob[:, hf, :], aprob[:, hf, :], ACT.Exp).then_inc(s["as_exp"], 1)
            for hf in range(2):
                act.wait_ge(s["apT_ps"], hf + 1)
                a(aprobT[:, hf, :], bank[2 + hf][0:TOK, 0:HALF_IMG * QROWS], ACT.Copy)\
                    .then_inc(s["apT_done"], 1)

            for hf in range(2):
                hi_of_turned(bank[3 + 2 * hf][:, 0:H2N], bank[4 + 2 * hf][0:FB, 0:H2N], H2N,
                             slice(H2N * hf, H2N * hf + H2N), "h2T_ps", hf + 1)
            for hf in range(2):
                act.wait_ge(s["gl_ps"], hf + 1)
                a(glT[:, H2N * hf:H2N * hf + H2N], bank[7 if hf == 0 else 0][0:EXPERTS, 0:H2N], ACT.Identity,
                  bias=col("gate_b", EXPERTS)).then_inc(s["gl_done"], 1)
            act.wait_ge(d_raw[0], 16)
            a(ug_w[0][:, 0, :], expert_raw[:, 0, 0:4 * HID], ACT.Copy).then_inc(s["ug_hi"], 1)
            act.wait_ge(s["gd_done"], 1)
            a(gexp[:, :, :], gexp[:, :, :], ACT.Exp).then_inc(s["ge_done"], 1)

            def split_up(n, p):
                act.wait_ge(d_raw[p], 8 * (n - p) + 16)
                if not isinstance(n, int) or n >= 2:
                    act.wait_ge(s["u_ps1"], n - 1)
                    act.wait_ge(s["g_ps1"], n - 1)
                a(ug_w[p][:, 0, :], expert_raw[:, p, 0:4 * HID], ACT.Copy).then_inc(s["ug_hi"], 1)

            def gate_act(n, hf, p):
                act.wait_ge(s[f"u_ps{hf}"], n + 1)
                if not isinstance(n, int) or n >= 1:
                    act.wait_ge(s[f"gated{hf}"], n)
                a(silu[hf][:, :], bank[3 + 2 * hf][:, 0:H2N], ACT.Silu,
                  bias=expert_raw[:, p, BU:BU + 1]).then_inc(s[f"silu{hf}"], 1)

            def hid_hi(n, hf, p):
                if isinstance(n, int) and n == 0:
                    act.wait_ge(s[f"gated{hf}"], 1)
                else:
                    act.wait_ge(s["weighed"], 2 * (n - 1) + hf + 1)
                    if not isinstance(n, int) or n > 1:
                        act.wait_ge(s["down_done"], n - 1)
                a(hid_s[p][:, 0, H2N * hf:H2N * hf + H2N], hid[hf][:, :], ACT.Copy)\
                    .then_inc(s["hid_hi"], 1)

            def expert(n, p, more=True):
                if more:
                    split_up(n + 1, 1 - p)
                gate_act(n, 0, p)
                if not isinstance(n, int) or n > 1:
                    act.wait_ge(s["down_done"], n - 1)
                a(dn_w[p][:, 0:DIM], expert_raw[:, p, DOWN0:DOWN0 + DIM], ACT.Copy).then_inc(s["dn_hi"], 1)
                hid_hi(n, 0, p)
                gate_act(n, 1, p)
                hid_hi(n, 1, p)

            expert(0, 0)
            for hf in range(2):
                act.wait_ge(s["wT_ps"], hf + 1)
                if hf == 0:
                    act.wait_ge(s["zeros_done"], 12)
                a(wT[0:EXPERTS, H2N * hf:H2N * hf + H2N], bank[7][0:EXPERTS, 0:H2N], ACT.Copy)\
                    .then_inc(s["wT_hi"], 1)
            expert(1, 1)
            with act.Fori(0, 7) as it:
                expert(2 * it + 2, 0)
                expert(2 * it + 3, 1)
            expert(16, 0, more=False)
            act.wait_ge(s["down_done"], 17)
            a(fin_tmp[:, 0:512], bank[2][FB:128, 0:512], ACT.Copy).then_inc(s["fin_moved"], 1)
            a(fin_tmp[:, 512:T2], bank[1][FB:128, 256:512], ACT.Copy).then_inc(s["fin_moved"], 1)

        @block.vector
        def _(dve):
            v = nc.vector
            step, after = chain(dve, "vec_step")

            def lo_of_turned(atA, atB, tok, k):
                dve.wait_ge(s["tA_hi"], k)
                v.tensor_tensor(tA[:, 1, tok], atA, f(tA[:, 0, tok]), ALU.subtract).then_inc(s["tA_lo"], 1)
                dve.wait_ge(s["tB_hi"], k)
                v.tensor_tensor(tB[FB:128, tok], atB, f(tB[0:FB, tok]), ALU.subtract).then_inc(s["tB_lo"], 1)

            dve.wait_ge(d_rows, 16)
            for t in range(4):
                dve.wait_ge(s["patch_ps"], t + 1)
                v.tensor_tensor(x0[:, t, :], bank[t][:, 0:DIM],
                                row("patch_b", 0, 128), ALU.add).then_inc(s["x0_done"], 1)
                dve.wait_ge(s["x0_done"], t + 1)
                k = step(v.bn_stats(st1[:, t, :], x0[:, t, :]))
                after(k)
                v.bn_aggr(mv1[:, t, :], st1[:, t, :]).then_inc(s["mv1_done"], 1)
                if t == 1:
                    dve.wait_ge(d_const, 16)
                    kb = step(v.tensor_tensor(bpe[:, :], row("ln_b", 0, 128), c("pe"), ALU.add))
                    dve.wait_ge(d_ff1, 16)
                    dve.wait_ge(s["ff1_hi"], 1)
                    v.tensor_tensor(ff1_w[:, 1, :], ff1_raw[:, :], f(ff1_w[:, 0, :]), ALU.subtract)\
                        .then_inc(s["ff1_lo"], 1)
            dve.wait_ge(s["mv1_done"], 4)
            for hf in range(2):
                ts = slice(2 * hf, 2 * hf + 2)
                dve.wait_ge(s["rs1_done"], hf + 1)
                for t in (2 * hf, 2 * hf + 1):
                    k = step(v.tensor_scalar(x0[:, t, :], x0[:, t, :], mv1[:, t, 0:1], rs1[:, t:t + 1],
                                             ALU.subtract, ALU.mult))
                after(k)
                k = step(v.tensor_tensor(x0[:, ts, :], x0[:, ts, :],
                                         row("ln_g", 0, 128).unsqueeze(1).to_broadcast([128, 2, DIM]), ALU.mult))
                after(max(k, kb))
                v.tensor_tensor(x[:, ts, :], x0[:, ts, :], bpe[:, :].unsqueeze(1).to_broadcast([128, 2, DIM]),
                                ALU.add).then_inc(s["x_done"], 1)
            for hf in range(2):
                lo_of_turned(bank[4 + 2 * hf][:, 0:H1], bank[5 + 2 * hf][0:FB, 0:H1],
                             slice(H1 * hf, H1 * hf + H1), hf + 1)
            dve.wait_ge(s["ff2_hi"], 1)
            for part in "AB":
                v.tensor_tensor(ff2_w[:, :, DOWN_LO[part]], ff2_raw[:, :, DOWN_HI[part]],
                                f(ff2_w[:, :, DOWN_HI[part]]), ALU.subtract).then_inc(s["ff2_lo"], 1)
            for hf in range(2):
                for m in range(FK):
                    i = FK * hf + m
                    dve.wait_ge(s["gelu_done"], i + 1)
                    v.tensor_copy(act1s[:, hf, 0, m, :], act1[:, hf, m, :]).then_inc(s["act1_hi"], 1)
                    dve.wait_ge(s["act1_hi"], i + 1)
                    v.tensor_tensor(act1s[:, hf, 1, m, :], act1[:, hf, m, :], f(act1s[:, hf, 0, m, :]),
                                    ALU.subtract).then_inc(s["act1_lo"], 1)
                if hf == 0:
                    dve.wait_ge(s["qkv_hi"], 1)
                    v.tensor_tensor(qkv_w[:, 1, :], qkv_raw[:, :], f(qkv_w[:, 0, :]), ALU.subtract)\
                        .then_inc(s["qkv_lo"], 1)
                    dve.wait_ge(d_cols, 16)
                    for ch in range(2):
                        v.tensor_scalar(bqm[:, ch, :], c("parity", CH), col("q_b", CH, ch), None, ALU.mult)\
                            .then_inc(s["bqm_done"], 1)
            for hf in range(2):
                tok = slice(H1 * hf, H1 * hf + H1)
                dve.wait_ge(s["yB_moved"], hf + 1)
                dve.wait_ge(s["yA_hi"], hf + 1)
                v.scalar_tensor_tensor(ybf[:, tok], bank[6 + hf][0:FB, H1:2 * H1], col("ff2_bB", FB), ytmp[:, tok],
                                       ALU.add, ALU.add).then_inc(s["yB_sum"], 1)
                v.scalar_tensor_tensor(yA[:, 1, tok], bank[6 + hf][:, 0:H1], col("ff2_bA", 128), f(yA[:, 0, tok]),
                                       ALU.add, ALU.subtract).then_inc(s["yA_lo"], 1)
                dve.wait_ge(s["yB_hi"], hf + 1)
                v.tensor_tensor(yB[FB:128, tok], ybf[:, tok], f(yB[0:FB, tok]), ALU.subtract)\
                    .then_inc(s["yB_lo"], 1)
            dve.wait_ge(s["zeros_done"], 1)
            for hf in range(2):
                dve.wait_ge(s["qk_ps"], hf + 1)
                for ch in range(2):
                    v.tensor_scalar(kT[:, ch, H1 * hf:H1 * hf + H1],
                                    bank[5 + 2 * hf][0:CH, H1 * ch:H1 * ch + H1],
                                    col("k_b", CH, ch), None, ALU.add).then_inc(s["k_done"], 1)
                dve.wait_ge(s["v_ps"], hf + 1)
                for i in range(2):
                    for ch in range(2):
                        src = bank[2 + hf][64 * i:64 * i + 64, 0:2 * DIM].rearrange(
                            "p (t c j k) -> p t c j k", t=2, c=2, j=3)[:, :, ch, :, :]
                        bias = row("v_b", 64 * i, 64 * i + 64)[:, CH * ch:CH * ch + CH]
                        first = HALF_IMG * hf + i
                        v.tensor_tensor(v_blk[64 * ch:64 * ch + 64, first:first + 3:2, :, 32 * ch:32 * ch + 32],
                                        src, v3(bias, 32).unsqueeze(1).to_broadcast([64, 2, 3, 32]), ALU.add)\
                            .then_inc(s["v_done"], 1)

            def softmax_rows(src, dst, mx, sm, rc, n, groups, ready, k, sub, exp, norm):
                wide = [n, groups, src.shape[-1]]
                dve.wait_ge(s[ready], k)
                j = step(v.tensor_reduce(mx, src, AXX, ALU.max))
                after(j)
                v.tensor_tensor(dst, src, mx.unsqueeze(2).to_broadcast(wide), ALU.subtract).then_inc(s[sub], 1)

            def softmax_norm(dst, sm, rc, n, groups, k, exp, norm):
                wide = [n, groups, dst.shape[-1]]
                dve.wait_ge(s[exp], k)
                j = step(v.tensor_reduce(sm, dst, AXX, ALU.add))
                after(j)
                j = step(v.reciprocal(rc, sm))
                after(j)
                v.tensor_tensor(dst, dst, rc.unsqueeze(2).to_broadcast(wide), ALU.mult).then_inc(s[norm], 1)

            for hf in range(2):
                for j in range(3):
                    softmax_rows(v3(bank[3 * hf + j][:, :], IMG_TOK), v3(prob[:, hf, j, :], IMG_TOK),
                                 smax[:, hf, j, :], None, None, 128, 8, "s_ps", 3 * hf + j + 1, "s_sub",
                                 None, None)
                for j in range(3):
                    softmax_norm(v3(prob[:, hf, j, :], IMG_TOK), ssum[:, hf, j, :], srec[:, hf, j, :], 128, 8,
                                 3 * hf + j + 1, "s_exp", "s_norm")
            for hf in range(2):
                dve.wait_ge(s["pT_ps"], 3 * hf + 2)
                v.tensor_copy(probT[:, hf, 1, :], bank[3 * hf + 1][:, :]).then_inc(s["pT_vec"], 1)
                for j in range(3):
                    dve.wait_ge(s["o_even"], 3 * hf + j + 1)
                    odd = bank[3 * hf + j][0:64, :].rearrange("p (b h q) -> p b h q", h=2, q=IMG_TOK)[:, :, 1, :]
                    tok = slice(H1 * hf, H1 * hf + H1)
                    dst = (o01[0:64, tok], o01[64:128, tok], o2[:, tok])[j]
                    v.scalar_tensor_tensor(v3(dst, IMG_TOK), odd, c("parity", 64)[:, 1:2],
                                           v3(otmp[:, hf, j, :], IMG_TOK), ALU.mult, ALU.add)\
                        .then_inc(s["o_done"], 1)
            for hf in range(2):
                dve.wait_ge(s["proj_ps"], hf + 1)
                dve.wait_ge(s["xpb_done"], hf + 1)
                ts = slice(2 * hf, 2 * hf + 2)
                v.tensor_tensor(x1[:, ts, :], v3(bank[6 + hf][:, 0:2 * DIM], DIM), xpb[:, ts, :], ALU.add)\
                    .then_inc(s["x1_done"], 1)
            for hf in range(2):
                lo_of_turned(bank[2 * hf][:, 0:H1], bank[2 * hf + 1][0:FB, 0:H1],
                             slice(H1 * hf, H1 * hf + H1), hf + 3)

            def layer_norm(src, st, mv, rs, dst, hf, done_mv, done_rs, done):
                for b in range(HALF_IMG * hf, HALF_IMG * hf + HALF_IMG):
                    k = step(v.bn_stats(st[:, b, :], src[:, b, 0:DIM]))
                for b in range(HALF_IMG * hf, HALF_IMG * hf + HALF_IMG):
                    if b == HALF_IMG * hf:
                        after(k)
                    last = v.bn_aggr(mv[:, b, :], st[:, b, :])
                last.then_inc(s[done_mv], 1)

            def normalise(src, mv, rs, dst, hf, done_mv, done_rs, done):
                dve.wait_ge(s[done_mv], hf + 1)
                dve.wait_ge(s[done_rs], hf + 1)
                for b in range(HALF_IMG * hf, HALF_IMG * hf + HALF_IMG):
                    last = v.tensor_scalar(dst[:, b, :], src[:, b, 0:DIM], mv[:, b, 0:1], rs[:, b:b + 1],
                                           ALU.subtract, ALU.mult)
                last.then_inc(s[done], 1)

            dve.wait_ge(d_txt, 16)
            for hf in range(2):
                dve.wait_ge(s["ff2_ps"], hf + 1)
                dve.wait_ge(s["x1b_done"], hf + 1)
                for i in range(2):
                    first = HALF_IMG * hf + i
                    v.tensor_tensor(h[0:IMG_TOK, first:first + 3:2, :],
                                    v3(bank[2 + hf][64 * i:64 * i + 64, 0:2 * DIM], DIM),
                                    x1b[64 * i:64 * i + 64, 2 * hf:2 * hf + 2, :], ALU.add)\
                        .then_inc(s["h_img"], 1)
                dve.wait_ge(s["h_img"], 2 * hf + 2)
                layer_norm(h, st2, mv2, rs2, xn, hf, "mv2_done", "rs2_done", "xn_done")
            k = step(v.reciprocal(itemp[:, :], row("temp", 0, TOK)))
            for hf in range(2):
                normalise(h, mv2, rs2, xn, hf, "mv2_done", "rs2_done", "xn_done")
            for hf in range(2):
                lo_of_turned(bank[2 * hf][:, 0:H2N], bank[2 * hf + 1][0:FB, 0:H2N],
                             slice(H2N * hf, H2N * hf + H2N), hf + 5)
            for i in range(4):
                dve.wait_ge(s["vsel_ps"], i + 1)
                src = v3(bank[4 + i][0:TOK, 0:2 * VSEL], VSEL)
                two = slice(2 * i, 2 * i + 2)
                kl = step(v.tensor_tensor(lg[:, two, :], src[:, :, DIM:VSEL],
                                          row("sel_b", 0, TOK).unsqueeze(1).to_broadcast([TOK, 2, 2]), ALU.add))
                v.tensor_tensor(av[:, two, :], src[:, :, 0:DIM],
                                row("av_b", 0, TOK).unsqueeze(1).to_broadcast([TOK, 2, DIM]), ALU.add)\
                    .then_inc(s["av_done"], 1)
            after(kl)
            k = step(v.tensor_scalar(lgt[:, :, :], lg[:, :, :], itemp[:, 0:1], None, ALU.mult))
            after(k)
            k = step(v.tensor_tensor(lmax[:, :], lgt[:, :, 0], lgt[:, :, 1], ALU.max))
            after(k)
            v.tensor_tensor(ld[:, :, :], lgt[:, :, :], lmax[:, :].unsqueeze(2).to_broadcast([TOK, IMAGES, 2]),
                            ALU.subtract).then_inc(s["ld_done"], 1)
            dve.wait_ge(s["le_done"], 1)
            k = step(v.tensor_tensor(lsum[:, :], le[:, :, 0], le[:, :, 1], ALU.add))
            after(k)
            k = step(v.reciprocal(lrec[:, :], lsum[:, :]))
            after(k)
            v.tensor_tensor(psel[:, :], le[:, :, 1], lrec[:, :], ALU.mult).then_inc(s["psel_done"], 1)
            dve.wait_ge(s["psT_ps"], 1)
            dve.wait_ge(s["zeros_done"], 12)
            k = step(v.tensor_copy(pT[:, 0:TOK], bank[4][0:IMAGES, 0:TOK]))
            after(k)
            k = step(v.max(top8[:, :], pT[:, 0:TOK]))
            after(k)
            k = step(v.match_replace(out=pT8[:, :], in_to_replace=top8[:, :], in_values=pT[:, :], imm_value=GONE))
            after(k)
            k = step(v.max(next8[:, :], pT8[:, 0:TOK]))
            after(k)
            k = step(v.tensor_copy(last2[:, 0:2], next8[:, 0:2]))
            after(k)
            k = step(v.match_replace(out=pT10[:, :], in_to_replace=last2[:, :], in_values=pT8[:, :],
                                     imm_value=GONE))
            after(k)
            v.tensor_tensor(pickT[:, :], pT10[:, 0:TOK], pT[:, 0:TOK], ALU.not_equal)\
                .then_inc(s["pickT_done"], 1)
            dve.wait_ge(s["pick_ps"], 1)
            v.tensor_copy(pick[:, :], bank[4][0:TOK, 128:128 + IMAGES]).then_inc(s["pick_done"], 1)
            for hf in range(2):
                dve.wait_ge(s["ak_ps"], hf + 1)
                v.tensor_scalar(akT[:, 1, H2N * hf:H2N * hf + H2N], bank[2 * hf + 1][0:CH, 0:H2N],
                                col("ak_b", CH, 1), None, ALU.add).then_inc(s["ak_odd"], 1)
            dve.wait_ge(s["cum_ps"], 1)
            dve.wait_ge(s["pick_done"], 1)
            k = step(v.tensor_tensor(rank[:, :], bank[4][0:TOK, 256:256 + IMAGES], pick[:, :], ALU.mult))
            after(k)
            wide = [TOK, IMAGES, PICKED]
            v.tensor_tensor(hot[:, :, :], rank[:, :].unsqueeze(2).to_broadcast(wide),
                            c("iota", TOK).unsqueeze(1).to_broadcast(wide), ALU.is_equal)\
                .then_inc(s["hot_done"], 1)
            dve.wait_ge(s["hot_done"], 1)
            v.tensor_tensor(hotp[:, :, :], hot[:, :, :], psel[:, :].unsqueeze(2).to_broadcast(wide), ALU.mult)\
                .then_inc(s["hot_done"], 1)
            dve.wait_ge(s["xs_ps"], 1)
            v.tensor_copy(xsA[:, :], bank[5][:, 0:SLOTS]).then_inc(s["xs_done"], 1)
            dve.wait_ge(s["aq_ps"], 1)
            for ch in range(2):
                k = step(v.tensor_scalar(aq[:, ch, :], bank[6][0:CH, SLOTS * ch:SLOTS * ch + SLOTS],
                                         col("aq_b", CH, ch), HEAD ** -0.5, ALU.add, ALU.mult))
            after(k)
            wide = [CH, IMAGES, CHH, PICKED]
            for ch in range(2):
                dst = aq_blk[:, ch, :, 60 * ch:60 * ch + 60].rearrange("p b (h i) -> p b h i", h=CHH)
                v.tensor_tensor(dst, v3(aq[:, ch, :], PICKED).unsqueeze(2).to_broadcast(wide),
                                c("head", CH).unsqueeze(1).unsqueeze(3).to_broadcast(wide), ALU.mult)\
                    .then_inc(s["aq_done"], 1)
            dve.wait_ge(s["hotpT_ps"], 1)
            wide = [SLOTS, IMAGES, TOK]
            v.tensor_tensor(hotpT[:, :, :], bank[7][0:SLOTS, 0:TOK].unsqueeze(1).to_broadcast(wide),
                            c("block", SLOTS).unsqueeze(2).to_broadcast(wide), ALU.mult)\
                .then_inc(s["hotpT_done"], 1)
            for hf in range(2):
                b = slice(HALF_IMG * hf, HALF_IMG * hf + HALF_IMG)
                softmax_rows(v3(bank[hf][0:QROWS, 0:H2N], TOK), v3(aprob[:, hf, :], TOK), amax[:, b], None, None,
                             QROWS, HALF_IMG, "as_ps", hf + 1, "as_sub", None, None)
            for hf in range(2):
                b = slice(HALF_IMG * hf, HALF_IMG * hf + HALF_IMG)
                softmax_norm(v3(aprob[:, hf, :], TOK), asum[:, b], arec[:, b], QROWS, HALF_IMG, hf + 1,
                             "as_exp", "as_norm")
            for hf in range(2):
                dve.wait_ge(s["ac_ps"], hf + 1)
                wide = [CH, 2 * HALF_IMG, CHH, PICKED]
                buf = actx[:, hf, :, :]
                k = step(v.tensor_tensor(
                    buf.rearrange("p c (h i) -> p c h i", h=CHH),
                    bank[4 + hf][0:CH, 0:480].rearrange("p (c h i) -> p c h i", c=2 * HALF_IMG, h=CHH),
                    c("head", CH).unsqueeze(1).unsqueeze(3).to_broadcast(wide), ALU.mult))
                after(k)
                for ch in range(2):
                    v.tensor_reduce(v3(ctxT[:, ch, hf, :], PICKED),
                                    buf[:, HALF_IMG * ch:HALF_IMG * ch + HALF_IMG, :].rearrange(
                                        "p c (h i) -> p c i h", h=CHH), AXX, ALU.add)\
                        .then_inc(s["ac_done"], 1)
            dve.wait_ge(s["ao_ps"], 1)
            v.tensor_tensor(arow[:, :], bank[6][0:SLOTS, 0:DIM], row("out_b", 0, SLOTS), ALU.add)\
                .then_inc(s["ao_done"], 1)
            for i in range(4):
                dve.wait_ge(s["h2_ps"], i + 1)
                dve.wait_ge(s["hx_done"], i // 2 + 1)
                two = slice(2 * i, 2 * i + 2)
                v.tensor_tensor(h2[:, two, 0:DIM], v3(bank[(7 + i) % 8][0:TOK, 0:2 * DIM], DIM), hx[:, two, :],
                                ALU.add).then_inc(s["h2_done"], 1)
                if i % 2:
                    dve.wait_ge(s["h2_done"], i + 1)
                    layer_norm(h2, st3, mv3, rs3, xn2, i // 2, "mv3_done", "rs3_done", "xn2_done")
            for hf in range(2):
                normalise(h2, mv3, rs3, xn2, hf, "mv3_done", "rs3_done", "xn2_done")

            for hf in range(2):
                lo_of_turned(bank[3 + 2 * hf][:, 0:H2N], bank[4 + 2 * hf][0:FB, 0:H2N],
                             slice(H2N * hf, H2N * hf + H2N), hf + 7)
            dve.wait_ge(s["ug_hi"], 1)
            v.tensor_tensor(ug_w[0][:, 1, :], expert_raw[:, 0, 0:4 * HID], f(ug_w[0][:, 0, :]), ALU.subtract)\
                .then_inc(s["ug_lo"], 1)
            wide = [TOK, IMAGES, EXPERTS]
            dve.wait_ge(s["glt_ps"], 1)
            logits = v3(bank[1][0:TOK, 0:IMAGES * EXPERTS], EXPERTS)
            k = step(v.tensor_reduce(gmax[:, :], logits, AXX, ALU.max))
            after(k)
            v.tensor_tensor(gexp[:, :, :], logits, gmax[:, :].unsqueeze(2).to_broadcast(wide), ALU.subtract)\
                .then_inc(s["gd_done"], 1)
            dve.wait_ge(s["ge_done"], 1)
            k = step(v.tensor_reduce(gsum[:, :], gexp[:, :, :], AXX, ALU.add))
            after(k)
            k = step(v.reciprocal(grec[:, :], gsum[:, :]))
            after(k)
            k = step(v.tensor_tensor(score[:, :, :], gexp[:, :, :], grec[:, :].unsqueeze(2).to_broadcast(wide),
                                     ALU.mult))
            after(k)
            k = step(v.tensor_tensor(sbias[:, :, :], score[:, :, :],
                                     row("bias", 0, TOK).unsqueeze(1).to_broadcast(wide), ALU.add))
            after(k)
            pair = sbias[:, :, :].rearrange("p b (g e) -> p b g e", e=2)
            k = step(v.tensor_tensor(grp[:, :, 0:GROUPS], pair[:, :, :, 0], pair[:, :, :, 1], ALU.add))
            after(k)

            def best_four(values, top, picked, out, n):
                for b in range(IMAGES):
                    k = step(v.max(top[:, b, :], values[:, b, 0:n]))
                after(k)
                k = step(v.tensor_copy(picked[:, :, 0:TOPK], top[:, :, 0:TOPK]))
                after(k)
                for b in range(IMAGES):
                    k = step(v.match_replace(out=out[:, b, :], in_to_replace=picked[:, b, :],
                                             in_values=values[:, b, :], imm_value=GONE))
                after(k)

            best_four(grp, grp_top, grp_val, grp_out, GROUPS)
            k = step(v.tensor_tensor(grp_in[:, :, :], grp_out[:, :, 0:GROUPS], grp[:, :, 0:GROUPS],
                                     ALU.not_equal))
            after(k)
            step(v.tensor_scalar(grp_low[:, :, :], grp_in[:, :, :], 1.0, -GONE, ALU.subtract, ALU.mult))
            wide = [TOK, IMAGES, GROUPS, 2]
            k = step(v.tensor_tensor(smask[:, :, :].rearrange("p b (g e) -> p b g e", e=2), pair,
                                     grp_in[:, :, :].unsqueeze(3).to_broadcast(wide), ALU.mult))
            after(k)
            k = step(v.tensor_tensor(exq[:, :, 0:EXPERTS].rearrange("p b (g e) -> p b g e", e=2),
                                     smask[:, :, :].rearrange("p b (g e) -> p b g e", e=2),
                                     grp_low[:, :, :].unsqueeze(3).to_broadcast(wide), ALU.add))
            after(k)
            best_four(exq, exq_top, exq_val, exq_out, EXPERTS)
            k = step(v.tensor_tensor(exq_in[:, :, :], exq_out[:, :, 0:EXPERTS], exq[:, :, 0:EXPERTS],
                                     ALU.not_equal))
            after(k)
            v.scalar_tensor_tensor(wfull[:, :, :].rearrange("p b e -> p (b e)"),
                                   score[:, :, :].rearrange("p b e -> p (b e)"), ROUTE_SCALE,
                                   exq_in[:, :, :].rearrange("p b e -> p (b e)"), ALU.mult, ALU.mult)\
                .then_inc(s["wfull_done"], 1)

            def split_up(n, p):
                dve.wait_ge(s["ug_hi"], n + 1)
                v.tensor_tensor(ug_w[p][:, 1, :], expert_raw[:, p, 0:4 * HID], f(ug_w[p][:, 0, :]),
                                ALU.subtract).then_inc(s["ug_lo"], 1)

            def gate_mul(n, hf, p):
                first = isinstance(n, int) and n == 0
                dve.wait_ge(s[f"silu{hf}"], n + 1)
                dve.wait_ge(s[f"g_ps{hf}"], n + 1)
                if not isinstance(n, int) or n > 1:
                    dve.wait_ge(s["weighed"], 2 * (n - 1))
                v.scalar_tensor_tensor((hid if first else gated)[hf][:, :], bank[4 + 2 * hf][:, 0:H2N],
                                       expert_raw[:, p, BG:BG + 1],
                                       silu[hf][:, :], ALU.add, ALU.mult).then_inc(s[f"gated{hf}"], 1)
                if first:
                    dve.wait_ge(s[f"gated{hf}"], 1)
                else:
                    dve.wait_ge(s[f"gated{hf}"], n + 1)
                    dve.wait_ge(s["wb_ps"], 2 * (n - 1) + hf + 1)
                    dve.wait_ge(s["hid_hi"], 2 * (n - 1) + hf + 1)
                    dve.wait_ge(s["hid_lo"], 2 * (n - 1) + hf + 1)
                    v.tensor_tensor(hid[hf][:, :], bank[7][:, 0:H2N], gated[hf][:, :], ALU.mult)\
                        .then_inc(s["weighed"], 1)
                dve.wait_ge(s["hid_hi"], 2 * n + hf + 1)
                tok = slice(H2N * hf, H2N * hf + H2N)
                v.tensor_tensor(hid_s[p][:, 1, tok], hid[hf][:, :], f(hid_s[p][:, 0, tok]), ALU.subtract)\
                    .then_inc(s["hid_lo"], 1)

            def expert(n, p, more=True):
                if more:
                    split_up(n + 1, 1 - p)
                gate_mul(n, 0, p)
                dve.wait_ge(s["dn_hi"], n + 1)
                raw = expert_raw[:, p, DOWN0:DOWN0 + DIM]
                for part in "AB":
                    v.tensor_tensor(dn_w[p][:, DOWN_LO[part]], raw[:, DOWN_HI[part]],
                                    f(dn_w[p][:, DOWN_HI[part]]), ALU.subtract).then_inc(s["dn_lo"], 1)
                gate_mul(n, 1, p)

            expert(0, 0)
            for hf in range(2):
                dve.wait_ge(s["wT_hi"], hf + 1)
                tok = slice(H2N * hf, H2N * hf + H2N)
                v.tensor_tensor(wT[32:32 + EXPERTS, tok], bank[7][0:EXPERTS, 0:H2N], f(wT[0:EXPERTS, tok]),
                                ALU.subtract).then_inc(s["wT_lo"], 1)
            expert(1, 1)
            with dve.Fori(0, 7) as it:
                expert(2 * it + 2, 0)
                expert(2 * it + 3, 1)
            expert(16, 0, more=False)
            dve.wait_ge(s["down_done"], 17)
            step(v.tensor_scalar(finA[:, 0:512], bank[0][:, :], col("sbdA", 128), None, ALU.add))
            dve.wait_ge(s["fin_moved"], 2)
            v.tensor_scalar(finA[:, 512:T2], bank[1][:, 0:256], col("sbdA", 128), None, ALU.add)\
                .then_inc(s["finA_done"], 1)
            step(v.scalar_tensor_tensor(finB[:, 0:512], bank[2][0:FB, 0:512], col("sbdB", FB),
                                        fin_tmp[:, 0:512], ALU.add, ALU.add))
            v.scalar_tensor_tensor(finB[:, 512:T2], bank[1][0:FB, 256:512], col("sbdB", FB),
                                   fin_tmp[:, 512:T2], ALU.add, ALU.add).then_inc(s["finB_done"], 1)


def constants():
    out = np.zeros((128, NCONST), np.float32)

    def put(name, a):
        out[:a.shape[0], CONST[name][0]:CONST[name][1]] = a

    put("ident", np.eye(128, dtype=np.float32))
    pos = np.arange(IMG_TOK, dtype=np.float32)[:, None]
    i = np.arange(DIM // 2, dtype=np.float32)[None, :]
    ang = pos / np.power(np.float32(10000.0), np.float32(2.0) * i / np.float32(DIM))
    pe = np.zeros((IMG_TOK, DIM), np.float32)
    pe[:, 0::2], pe[:, 1::2] = np.sin(ang), np.cos(ang)
    put("pe", np.concatenate([pe, pe]))
    key = np.arange(TOK)
    put("causal", np.where(key[None, :] > key[:, None], -10000.0, 0.0))
    put("tri", (key[:, None] <= key[None, :]).astype(np.float32))
    feat = np.arange(128)
    put("head", (feat[:CH, None] // HEAD == np.arange(CHH)[None, :]).astype(np.float32))
    put("parity", (feat[:, None] // HEAD % 2 == np.arange(2)[None, :]).astype(np.float32))
    put("block", (np.arange(SLOTS)[:, None] // PICKED == np.arange(IMAGES)[None, :]).astype(np.float32))
    put("iota", np.tile(np.arange(1, PICKED + 1, dtype=np.float32), (128, 1)))
    return out


def arrays_of(i):
    i = {k: np.asarray(v) for k, v in i.items()}

    def ab(w):
        return [w[:FA], np.concatenate([w[FA:], w[FA:]])]

    def tall(w, n=128):
        out = np.zeros((n,) + w.shape[1:], w.dtype)
        out[:len(w)] = w
        return out

    x = i["x"].reshape(IMAGES, CHANNELS, GRID, PATCH, GRID, PATCH).transpose(1, 3, 5, 0, 2, 4)
    x = x.reshape(PK, 128, 4, 128).transpose(2, 1, 0, 3)
    tok, at, fn = "L0_tok_", "L0_attn_", "L0_ffn_"
    out = {"patches": x}
    out["patch_w"] = i[tok + "patch_w"].reshape(DIM, PK, 128).transpose(2, 1, 0)
    out["const"] = constants()
    cols = np.zeros((128, NCOLS), np.float32)

    def put(name, a):
        cols[:a.shape[0], COLS[name][0]:COLS[name][1]] = a

    put("ff1_b", i[tok + "ff1_b"].reshape(FK, 128).T)
    put("ff2_bA", i[tok + "ff2_b"][:FA, None])
    put("ff2_bB", i[tok + "ff2_b"][FA:, None])
    put("q_b", i[tok + "qkv_b"][:DIM].reshape(2, CH).T)
    put("k_b", i[tok + "qkv_b"][DIM:2 * DIM].reshape(2, CH).T)
    put("aq_b", i[at + "Wqkv_b"][:DIM].reshape(2, CH).T)
    put("ak_b", i[at + "Wqkv_b"][DIM:2 * DIM].reshape(2, CH).T)
    put("gate_b", i[fn + "gate_b"][:, None])
    put("sbdA", i[fn + "sbd"][:FA, None])
    put("sbdB", i[fn + "sbd"][FA:, None])
    out["cols"] = cols
    out["rows"] = np.concatenate([
        i[tok + "patch_b"], i[tok + "ln_g"], i[tok + "ln_b"], i[tok + "qkv_b"][2 * DIM:], i[tok + "proj_b"],
        i[tok + "ff2_b"], i[at + "Wqkv_b"][2 * DIM:], i[at + "out_b"], i[at + "sel_b"], i[fn + "bias"],
        i[at + "temperature"]])[None]
    out["ff1"] = np.concatenate(ab(i[tok + "ff1_w"]), 1)
    out["ff2"] = i[tok + "ff2_w"].reshape(FK, 128, DIM).transpose(1, 0, 2)
    out["qkv"] = np.concatenate(ab(i[tok + "qkv_w"]), 1)
    pw = i[tok + "proj_w"].reshape(2, 3, 32, DIM).transpose(1, 0, 2, 3).reshape(DIM, DIM)
    out["proj"] = np.stack([pw[:FA], tall(pw[FA:])], 1)
    kv = np.concatenate([i[at + "Wqkv_w"][:, DIM:], i[at + "sel_w"]], 1)
    out["kv"] = np.concatenate(ab(kv), 1)
    aq = i[at + "Wqkv_w"][:, :DIM]
    out["aq"] = np.stack([aq[:FA], tall(aq[FA:])], 1)
    out["out_w"] = i[at + "out_w"].reshape(2, CH, DIM).transpose(1, 0, 2)
    out["gate"] = np.concatenate(ab(i[fn + "gate_w"]), 1)
    bd = np.zeros((48, DIM), np.float32)
    bd[:EXPERTS], bd[32:] = i[fn + "bd"], i[fn + "bd"]
    out["bd"] = bd
    out["txt"] = i["txt"].transpose(1, 0, 2)
    wu = np.concatenate([i[fn + "sWu"][None], i[fn + "Wu"]])
    wg = np.concatenate([i[fn + "sWg"][None], i[fn + "Wg"]])
    wd = np.concatenate([i[fn + "sWd"][None], i[fn + "Wd"]])
    twice = [np.concatenate([w[:, FA:], w[:, FA:]], 1) for w in (wu, wg)]
    bu = np.concatenate([i[fn + "sbu"][None], i[fn + "bu"]])[:, :, None]
    bg = np.concatenate([i[fn + "sbg"][None], i[fn + "bg"]])[:, :, None]
    out["experts"] = np.concatenate([wu[:, :FA], wg[:, :FA], *twice, wd, bu, bg], 2)
    return {k: np.ascontiguousarray(v) for k, v in out.items()}


def kernel(**inputs):
    import concourse.bacc as _bacc
    from concourse.bass_utils import run_bass_kernel_spmd as _run

    nc = _bacc.Bacc("TRN2", target_bir_lowering=False, num_devices=1)
    arrays = arrays_of(inputs)
    args = {k: nc.dram_tensor("in_" + k, a.shape, mybir.dt.from_np(a.dtype), kind="ExternalInput").ap()
            for k, a in arrays.items()}
    args["out"] = nc.dram_tensor("out", (DIM, T2), F32, kind="ExternalOutput").ap()
    build(nc, args)
    r = _run(nc, [{"in_" + k: a for k, a in arrays.items()}], core_ids=[0])
    return np.ascontiguousarray(r.results[0]["out"].T.reshape(IMAGES, TOK, DIM))
```

```python
from contextlib import ExitStack

import numpy as np

import concourse.bass as bass
from concourse import mybir

F32 = mybir.dt.float32
F32R = mybir.dt.float32r
ALU = mybir.AluOpType
ACT = mybir.ActivationFunctionType
AXX = mybir.AxisListType.X

IMAGES, CHANNELS, SIDE, PATCH = 8, 3, 128, 16
GRID = SIDE // PATCH
IMG_TOK = GRID * GRID
TXT_TOK = 32
TOK = IMG_TOK + TXT_TOK
DIM, HEADS, HEAD = 192, 12, 16
FF = 768
EXPERTS, GROUPS, TOPK, HID, ROUTE_SCALE = 16, 8, 4, 128, 2.5
PICKED = 10
EPS = 1e-5
FA, FB = 128, 64
HALF_IMG = IMAGES // 2
T1, H1 = IMAGES * IMG_TOK, HALF_IMG * IMG_TOK
T2, H2N = IMAGES * TOK, HALF_IMG * TOK
PK = CHANNELS * PATCH * PATCH // 128
FK = FF // 128
CH = 96
CHH = CH // HEAD
SLOTS = IMAGES * PICKED
QROWS = HEADS * PICKED
WPACK = 4 * HID + DIM + 2
DOWN0, BU, BG = 4 * HID, 4 * HID + DIM, 4 * HID + DIM + 1
LOW, GONE = -3.3e38, -3.0e38
DOWN_HI, DOWN_LO = {"A": slice(0, FA), "B": slice(FA, DIM)}, {"A": slice(DIM + FB, 2 * DIM), "B": slice(DIM, DIM + FB)}
B_BOTH = slice(FA, FA + 2 * FB)
VSEL = DIM + 2


FILL = {"patches": 11, "turn_x0": 10, "hidden0": 1, "turn_x1": 10, "ff_out0": 1, "hidden1": 1,
        "qkv0": 1, "ff_out1": 1, "scores0": 1, "qkv1": 1, "prob0": 1, "scores3": 1, "values0": 6,
        "prob1": 1, "scores4": 1, "values1": 1, "prob2": 1, "scores5": 1, "values2": 1, "prob3": 1,
        "prob4": 7, "project0": 1, "values3": 1, "turn_x2": 1, "prob5": 1, "values5": 8,
        "hidden2": 1, "project1": 1, "ff_out2": 1, "turn_x3": 1, "hidden3": 14, "turn_h0": 1,
        "vk0": 12, "ff_out3": 1, "turn_h1": 26, "vk1": 8, "psel": 7, "pickT": 10, "pick": 2,
        "hot": 4, "xs": 2, "aq": 10, "as0": 12, "as1": 2, "ap0": 1, "ap1": 4, "ac": 8, "ao": 3,
        "xn2_0": 22, "xn2_1": 3, "gl": 1, "glt": 3, "ug0": 4, "wfull": 1, "wrow": 1}


def layout(parts):
    at, out = 0, {}
    for name, width in parts:
        out[name] = (at, at + width)
        at += width
    return out, at


CONST, NCONST = layout([("ident", 128), ("pe", DIM), ("causal", TOK), ("tri", TOK), ("head", CHH),
                        ("parity", 2), ("block", IMAGES), ("iota", PICKED)])
COLS, NCOLS = layout([("ff1_b", FK), ("ff2_bA", 1), ("ff2_bB", 1), ("q_b", 2), ("k_b", 2), ("aq_b", 2),
                      ("ak_b", 2), ("gate_b", 1), ("sbdA", 1), ("sbdB", 1)])
ROWS, NROWS = layout([("patch_b", DIM), ("ln_g", DIM), ("ln_b", DIM), ("v_b", DIM), ("proj_b", DIM),
                      ("ff2_b", DIM), ("av_b", DIM), ("out_b", DIM), ("sel_b", 2), ("bias", EXPERTS),
                      ("temp", 1)])


def build(nc, d):
    with ExitStack() as ctx:
        def sb(name, shape, dt=F32):
            return ctx.enter_context(nc.sbuf_tensor(name, shape, dt))

        def sem(name):
            return ctx.enter_context(nc.semaphore(name))

        bank = [ctx.enter_context(nc.psum_tensor(f"bank{i}", [128, 512], F32)) for i in range(8)]

        const = sb("const", [128, NCONST])
        cols = sb("cols", [128, NCOLS])
        rows = sb("rows", [128, NROWS])
        ff2_raw = sb("ff2_raw", [128, FK, DIM])
        proj_w = sb("proj_w", [128, 2, DIM])
        kv_raw = sb("kv_raw", [128, 2 * (DIM + VSEL)])
        aq_w = sb("aq_w", [128, 2, DIM])
        out_w = sb("out_w", [CH, 2, DIM])
        gate_raw = sb("gate_raw", [128, 2 * EXPERTS])
        bd_raw = sb("bd_raw", [48, DIM])
        expert_raw = sb("expert_raw", [128, 2, WPACK])
        kv_w = sb("kv_w", [128, 2, 2 * (DIM + VSEL)], F32R)
        gate_w = sb("gate_w", [128, 2, 2 * EXPERTS], F32R)
        bd_w = sb("bd_w", [48, 2, DIM], F32R)
        minus_half = sb("minus_half", [128, 4])
        filler = sb("filler", [128, 512], mybir.dt.bfloat16)
        table = sb("table", [1, 8])
        x1 = sb("x1", [128, 4, DIM])
        x1b = sb("x1b", [128, 4, DIM])
        tA = sb("tA", [128, 2, T2], F32R)
        tB = sb("tB", [128, T2], F32R)
        act1 = sb("act1", [128, 2, FK, H1])
        v_blk = sb("v_blk", [128, IMAGES, 3, 64])
        h = sb("h", [TOK, IMAGES, DIM])
        st2 = sb("st2", [TOK, IMAGES, 6])
        mv2 = sb("mv2", [TOK, IMAGES, 2])
        ve2 = sb("ve2", [TOK, IMAGES])
        rs2 = sb("rs2", [TOK, IMAGES])
        xn = sb("xn", [TOK, IMAGES, DIM])
        pT = sb("pT", [IMAGES, TOK + 8])
        last2 = sb("last2", [IMAGES, 8])
        aq_blk = sb("aq_blk", [CH, 2, IMAGES, QROWS])
        h2 = sb("h2", [TOK, IMAGES, 256])
        grp = sb("grp", [TOK, IMAGES, GROUPS + 4])
        grp_val = sb("grp_val", [TOK, IMAGES, 8])
        exq = sb("exq", [TOK, IMAGES, EXPERTS + 4])
        exq_val = sb("exq_val", [TOK, IMAGES, 8])
        wT = sb("wT", [48, T2], F32R)
        ones2 = sb("ones2", [2, 128], F32R)

        first_life = ExitStack()

        def sb1(name, shape, dt=F32):
            return first_life.enter_context(nc.sbuf_tensor(name, shape, dt))

        ff1_w = sb1("ff1_w", [128, 2, 2 * FF], F32R)
        qkv_w = sb1("qkv_w", [128, 2, 2 * 3 * DIM], F32R)
        x = sb1("x", [128, 4, DIM])
        xpb = sb1("xpb", [128, 4, DIM])
        yA = sb1("yA", [128, 2, T1], F32R)
        yB = sb1("yB", [128, T1], F32R)
        ytmp = sb1("ytmp", [FB, T1])
        ybf = sb1("ybf", [FB, T1])
        bqm = sb1("bqm", [CH, 2, 2])
        smax = sb1("smax", [128, 2, 3, 8])
        ssum = sb1("ssum", [128, 2, 3, 8])
        srec = sb1("srec", [128, 2, 3, 8])

        with ExitStack() as early:
            def sb0(name, shape, dt=F32):
                return early.enter_context(nc.sbuf_tensor(name, shape, dt))

            patches = sb0("patches", [128, 4, PK, 128])
            patch_w = sb0("patch_w", [128, PK, DIM])
            ff1_raw = sb0("ff1_raw", [128, 2 * FF])
            qkv_raw = sb0("qkv_raw", [128, 2 * 3 * DIM])
            x0 = sb0("x0", [128, 4, DIM])
            st1 = sb0("st1", [128, 4, 6])
            mv1 = sb0("mv1", [128, 4, 2])
            ve1 = sb0("ve1", [128, 4])
            rs1 = sb0("rs1", [128, 4])
            bpe = sb0("bpe", [128, DIM])
            ff2_w = sb0("ff2_w", [128, FK, 2 * DIM], F32R)
            act1s = sb0("act1s", [128, 2, 2, FK, H1], F32R)

        q_blk = sb1("q_blk", [CH, 2, IMAGES, 2, IMG_TOK])
        kT = sb1("kT", [CH, 2, T1])
        prob = sb1("prob", [128, 2, 3, 512])
        probT = sb1("probT", [128, 2, 3, 512])
        otmp = sb1("otmp", [64, 2, 3, H1])
        o01 = sb1("o01", [128, T1])
        o2 = sb1("o2", [64, T1])

        first_life.close()

        ug_w = [sb(f"ug_w{p}", [128, 2, 4 * HID], F32R) for p in range(2)]
        dn_w = [sb(f"dn_w{p}", [128, 2 * DIM], F32R) for p in range(2)]
        xn2 = sb("xn2", [TOK, IMAGES, DIM])
        st3 = sb("st3", [TOK, IMAGES, 6])
        mv3 = sb("mv3", [TOK, IMAGES, 2])
        ve3 = sb("ve3", [TOK, IMAGES])
        rs3 = sb("rs3", [TOK, IMAGES])
        glT = sb("glT", [EXPERTS, T2])
        gmax = sb("gmax", [TOK, IMAGES])
        gexp = sb("gexp", [TOK, IMAGES, EXPERTS])
        gsum = sb("gsum", [TOK, IMAGES])
        grec = sb("grec", [TOK, IMAGES])
        score = sb("score", [TOK, IMAGES, EXPERTS])
        sbias = sb("sbias", [TOK, IMAGES, EXPERTS])
        grp_top = sb("grp_top", [TOK, IMAGES, 8])
        grp_out = sb("grp_out", [TOK, IMAGES, GROUPS + 4])
        grp_in = sb("grp_in", [TOK, IMAGES, GROUPS])
        grp_low = sb("grp_low", [TOK, IMAGES, GROUPS])
        smask = sb("smask", [TOK, IMAGES, EXPERTS])
        exq_top = sb("exq_top", [TOK, IMAGES, 8])
        exq_out = sb("exq_out", [TOK, IMAGES, EXPERTS + 4])
        exq_in = sb("exq_in", [TOK, IMAGES, EXPERTS])
        wfull = sb("wfull", [TOK, IMAGES, EXPERTS])
        silu = [sb(f"silu{i}", [128, H2N]) for i in range(2)]
        gated = [sb(f"gated{i}", [128, H2N]) for i in range(2)]
        hid = [sb(f"hid{i}", [128, H2N]) for i in range(2)]
        hid_s = [sb(f"hid_s{p}", [128, 2, T2], F32R) for p in range(2)]
        fin_tmp = sb("fin_tmp", [FB, T2])
        finA = sb("finA", [FA, T2])
        finB = sb("finB", [FB, T2])

        with ExitStack() as second_life:
            def sb2(name, shape, dt=F32):
                return second_life.enter_context(nc.sbuf_tensor(name, shape, dt))

            hx = sb2("hx", [TOK, IMAGES, DIM])
            akT = sb2("akT", [CH, 2, T2])
            av = sb2("av", [TOK, IMAGES, DIM])
            itemp = sb2("itemp", [TOK, 1])
            lg = sb2("lg", [TOK, IMAGES, 2])
            lgt = sb2("lgt", [TOK, IMAGES, 2])
            lmax = sb2("lmax", [TOK, IMAGES])
            ld = sb2("ld", [TOK, IMAGES, 2])
            le = sb2("le", [TOK, IMAGES, 2])
            lsum = sb2("lsum", [TOK, IMAGES])
            lrec = sb2("lrec", [TOK, IMAGES])
            psel = sb2("psel", [TOK, IMAGES])
            pT8 = sb2("pT8", [IMAGES, TOK + 8])
            pT10 = sb2("pT10", [IMAGES, TOK + 8])
            top8 = sb2("top8", [IMAGES, 8])
            next8 = sb2("next8", [IMAGES, 8])
            pickT = sb2("pickT", [IMAGES, TOK])
            pick = sb2("pick", [TOK, IMAGES])
            rank = sb2("rank", [TOK, IMAGES])
            hot = sb2("hot", [TOK, IMAGES, PICKED])
            hot_heads = sb2("hot_heads", [TOK, IMAGES, QROWS])
            hotp = sb2("hotp", [TOK, IMAGES, PICKED])
            hotpT = sb2("hotpT", [SLOTS, IMAGES, TOK])
            xsA = sb2("xsA", [FA, SLOTS])
            xsB = sb2("xsB", [FB, SLOTS])
            aq = sb2("aq", [CH, 2, SLOTS])
            aprob = sb2("aprob", [QROWS, 2, H2N])
            amax = sb2("amax", [QROWS, IMAGES])
            asum = sb2("asum", [QROWS, IMAGES])
            arec = sb2("arec", [QROWS, IMAGES])
            aprobT = sb2("aprobT", [TOK, 2, HALF_IMG * QROWS])
            actx = sb2("actx", [CH, 2, 2 * HALF_IMG, 60])
            ctxT = sb2("ctxT", [CH, 2, 2, HALF_IMG * PICKED])
            arow = sb2("arow", [SLOTS, DIM])

        wrow = sb("wrow", [2, EXPERTS * T2], F32R)

        def f(ap):
            return ap.bitcast(F32)

        def c(name, n=128, i=None):
            a, b = CONST[name]
            return const[0:n, a:b]

        def col(name, n, i=0):
            a = COLS[name][0] + i
            return cols[0:n, a:a + 1]

        def row(name, p0, p1):
            a, b = ROWS[name]
            return rows[p0:p1, a:b]

        def v3(ap, n):
            return ap.rearrange("p (a b) -> p a b", b=n)

        d_patch = [sem(f"d_patch{i}") for i in range(4)]
        (d_pw, d_const, d_cols, d_rows, d_ff1, d_ff2, d_qkv, d_proj, d_kv, d_aq, d_outw, d_gate, d_bd,
         d_txt, d_wrow, d_out) = [sem("d_" + n) for n in (
             "patch_w", "const", "cols", "rows", "ff1", "ff2", "qkv", "proj", "kv", "aq", "out_w", "gate",
             "bd", "txt", "wrow", "out")]
        d_ug = [sem(f"d_up{p}") for p in range(2)]
        d_dn = [sem(f"d_down{p}") for p in range(2)]

        s = {n: sem(n) for n in (
            "patch_ps", "x0_done", "mv1_done", "rs1_done", "x_done", "xpb_done", "xT_ps", "tA_hi", "tB_hi",
            "tA_lo", "tB_lo", "ff1_hi", "ff1_lo", "ff2_hi", "ff2_lo", "qkv_hi", "qkv_lo", "hid1_ps",
            "gelu_done", "act1_hi", "act1_lo", "y_ps", "yA_hi", "yB_moved", "yB_sum", "yA_lo", "yB_hi", "yB_lo",
            "qk_ps", "bqm_done", "q_done", "k_done", "v_ps", "v_done", "s_ps", "s_sub",
            "s_exp", "s_norm", "pT_ps", "pT_done", "o_ps", "o_even", "o_done", "proj_ps", "x1_done",
            "x1b_done", "hid2_ps", "gelu2_done", "ff2_ps", "h_img", "zeros_done", "filler_done", "table_done",
            "mv2_done", "rs2_done", "xn_done", "hx_done", "hT_ps", "kv_split", "vsel_ps", "av_done", "ak_ps",
            "ak_even", "ak_odd", "ld_done", "le_done", "psel_done", "psT_ps", "pickT_done", "pick_ps",
            "pick_done", "cum_ps", "hot_done", "hot_spread", "xs_ps", "xs_done", "aq_ps", "aq_done", "hotpT_ps",
            "hotpT_done", "as_ps", "as_sub", "as_exp", "as_norm", "apT_ps", "apT_done", "ac_ps", "ac_done",
            "ao_ps", "ao_done", "h2_ps", "h2_done",
            "mv3_done", "rs3_done", "xn2_done", "h2T_ps", "gate_split", "bd_split", "gl_ps", "gl_done",
            "glt_ps", "gd_done", "ge_done", "wfull_done", "wT_ps", "wT_hi", "wT_lo", "init_done",
            "ug_hi", "ug_lo", "dn_hi", "dn_lo", "u_ps0", "u_ps1", "g_ps0", "g_ps1", "silu0", "silu1",
            "gated0", "gated1", "wb_ps", "weighed", "hid_hi", "hid_lo", "down_done", "fin_moved", "finA_done",
            "finB_done", "gp_step", "vec_step")}

        def chain(eng, signal):
            count = [0]

            def step(ins):
                count[0] += 1
                ins.then_inc(s[signal], 1)
                return count[0]

            def after(k):
                eng.wait_ge(s[signal], k)
            return step, after

        block = ctx.enter_context(nc.Block())

        @block.sync
        def _(sp):
            sp.dma_start(patches[:, 0], d["patches"][0]).then_inc(d_patch[0], 16)
            sp.dma_start(patch_w[:], d["patch_w"]).then_inc(d_pw, 16)
            sp.dma_start(patches[:, 1], d["patches"][1]).then_inc(d_patch[1], 16)
            sp.dma_start(rows[:, :], d["rows"].to_broadcast([128, NROWS])).then_inc(d_rows, 16)
            sp.dma_start(patches[:, 2], d["patches"][2]).then_inc(d_patch[2], 16)
            sp.dma_start(ff1_raw[:, :], d["ff1"]).then_inc(d_ff1, 16)
            sp.dma_start(const[:, :], d["const"]).then_inc(d_const, 16)
            sp.dma_start(patches[:, 3], d["patches"][3]).then_inc(d_patch[3], 16)
            sp.dma_start(cols[:, :], d["cols"]).then_inc(d_cols, 16)
            sp.dma_start(ff2_raw[:, :, :], d["ff2"]).then_inc(d_ff2, 16)
            sp.dma_start(qkv_raw[:, :], d["qkv"]).then_inc(d_qkv, 16)
            sp.dma_start(proj_w[:, :, :], d["proj"]).then_inc(d_proj, 16)
            sp.dma_start(kv_raw[:, :], d["kv"]).then_inc(d_kv, 16)
            sp.dma_start(h[IMG_TOK:TOK, :, :], d["txt"]).then_inc(d_txt, 16)
            sp.dma_start(aq_w[:, :, :], d["aq"]).then_inc(d_aq, 16)
            sp.dma_start(out_w[:, :, :], d["out_w"]).then_inc(d_outw, 16)
            sp.dma_start(gate_raw[:, :], d["gate"]).then_inc(d_gate, 16)
            sp.dma_start(bd_raw[:, :], d["bd"]).then_inc(d_bd, 16)
            for n in range(2):
                sp.dma_start(expert_raw[:, n, 0:DOWN0], d["experts"][n][:, 0:DOWN0]).then_inc(d_ug[n], 16)
                sp.dma_start(expert_raw[:, n, DOWN0:], d["experts"][n][:, DOWN0:]).then_inc(d_dn[n], 16)
            sp.wait_ge(s["wT_lo"], 2)
            for part in range(2):
                sp.dma_start(f(wrow[part:part + 1, :]).rearrange("p (e t) -> p e t", e=EXPERTS),
                             f(wT[32 * part:32 * part + EXPERTS, :])).then_inc(d_wrow, 16)

            def source(n, columns):
                if isinstance(n, int):
                    return d["experts"][n][:, columns]
                return d["experts"][bass.ds(n, 1), :, columns]

            def load_up(n, p):
                src = source(n, slice(0, DOWN0))
                sp.wait_ge(s["ug_lo"], n - 1)
                sp.dma_start(expert_raw[:, p, 0:DOWN0], src).then_inc(d_ug[p], 16)

            def load_down(n, p):
                src = source(n, slice(DOWN0, WPACK))
                sp.wait_ge(s["gated1"], n - 1)
                sp.dma_start(expert_raw[:, p, DOWN0:WPACK], src).then_inc(d_dn[p], 16)

            load_up(2, 0)
            load_down(2, 0)
            load_up(3, 1)
            load_down(3, 1)
            with sp.Fori(0, 6) as it:
                load_up(2 * it + 4, 0)
                load_down(2 * it + 4, 0)
                load_up(2 * it + 5, 1)
                load_down(2 * it + 5, 1)
            load_up(16, 0)
            load_down(16, 0)
            sp.wait_ge(s["finA_done"], 1)
            sp.dma_start(d["out"][0:FA, :], finA[:, :]).then_inc(d_out, 16)
            sp.wait_ge(s["finB_done"], 1)
            sp.dma_start(d["out"][FA:DIM, :], finB[:, :]).then_inc(d_out, 16)
            sp.wait_ge(d_out, 32)

        @block.gpsimd
        def _(gp):
            g = nc.gpsimd
            step, after = chain(gp, "gp_step")
            g.memset(filler[:, :], 1.0).then_inc(s["filler_done"], 1)
            g.memset(table[:, :], 0.0).then_inc(s["filler_done"], 1)
            step(g.memset(minus_half[:, :], -0.5))
            g.memset(v_blk[:, :, :, :], 0.0).then_inc(s["zeros_done"], 1)
            g.memset(aq_blk[:, :, :, :], 0.0).then_inc(s["zeros_done"], 1)
            g.memset(h2[:, :, DIM:256], 0.0).then_inc(s["zeros_done"], 1)
            g.memset(f(bd_w[:, :, :]), 0.0).then_inc(s["zeros_done"], 1)
            g.memset(f(wT[:, :]), 0.0).then_inc(s["zeros_done"], 1)
            g.memset(f(ones2[:, :]), 1.0).then_inc(s["zeros_done"], 1)
            g.memset(pT[:, TOK:TOK + 8], LOW).then_inc(s["zeros_done"], 1)
            g.memset(last2[:, 2:8], LOW).then_inc(s["zeros_done"], 1)
            g.memset(grp[:, :, GROUPS:GROUPS + 4], LOW).then_inc(s["zeros_done"], 1)
            g.memset(grp_val[:, :, 4:8], LOW).then_inc(s["zeros_done"], 1)
            g.memset(exq[:, :, EXPERTS:EXPERTS + 4], LOW).then_inc(s["zeros_done"], 1)
            g.memset(exq_val[:, :, 4:8], LOW).then_inc(s["zeros_done"], 1)

            def rsqrt(ve, mv, rs, lo, hi, n, done):
                k = step(g.tensor_scalar(ve[:, lo:hi], mv[:, lo:hi, 1], EPS, 1.0, ALU.add, ALU.mult))
                after(k)
                g.tensor_tensor(rs[:, lo:hi], ve[:, lo:hi], minus_half[0:n, 0:hi - lo], ALU.pow)\
                    .then_inc(s[done], 1)

            gp.wait_ge(s["mv1_done"], 2)
            rsqrt(ve1, mv1, rs1, 0, 2, 128, "rs1_done")
            gp.wait_ge(s["ff2_hi"], 1)
            for part in "AB":
                g.tensor_tensor(ff2_w[:, :, DOWN_LO[part]], ff2_raw[:, :, DOWN_HI[part]],
                                f(ff2_w[:, :, DOWN_HI[part]]), ALU.subtract).then_inc(s["ff2_lo"], 1)
            gp.wait_ge(s["mv1_done"], 4)
            rsqrt(ve1, mv1, rs1, 2, 4, 128, "rs1_done")
            gp.wait_ge(s["qkv_hi"], 1)
            g.tensor_tensor(qkv_w[:, 1, :], qkv_raw[:, :], f(qkv_w[:, 0, :]), ALU.subtract)\
                .then_inc(s["qkv_lo"], 1)
            for hf in range(2):
                gp.wait_ge(s["x_done"], hf + 1)
                t = slice(2 * hf, 2 * hf + 2)
                g.tensor_tensor(xpb[:, t, :], x[:, t, :],
                                row("proj_b", 0, 128).unsqueeze(1).to_broadcast([128, 2, DIM]), ALU.add)\
                    .then_inc(s["xpb_done"], 1)
            gp.wait_ge(d_kv, 16)
            k = step(g.tensor_scalar(kv_w[:, 0, :], kv_raw[:, :], 1.0, 1.0, ALU.mult, ALU.mult))
            after(k)
            g.tensor_tensor(kv_w[:, 1, :], kv_raw[:, :], f(kv_w[:, 0, :]), ALU.subtract)\
                .then_inc(s["kv_split"], 1)
            gp.wait_ge(d_gate, 16)
            k = step(g.tensor_scalar(gate_w[:, 0, :], gate_raw[:, :], 1.0, 1.0, ALU.mult, ALU.mult))
            after(k)
            g.tensor_tensor(gate_w[:, 1, :], gate_raw[:, :], f(gate_w[:, 0, :]), ALU.subtract)\
                .then_inc(s["gate_split"], 1)
            gp.wait_ge(d_bd, 16)
            gp.wait_ge(s["zeros_done"], 12)
            for p0 in (0, 32):
                k = step(g.tensor_scalar(bd_w[p0:p0 + EXPERTS, 0, :], bd_raw[p0:p0 + EXPERTS, :], 1.0, 1.0,
                                         ALU.mult, ALU.mult))
                after(k)
            g.tensor_tensor(bd_w[0:EXPERTS, 1, :], bd_raw[0:EXPERTS, :], f(bd_w[0:EXPERTS, 0, :]),
                            ALU.subtract).then_inc(s["bd_split"], 1)
            for hf in range(2):
                gp.wait_ge(s["x1_done"], hf + 1)
                t = slice(2 * hf, 2 * hf + 2)
                g.tensor_tensor(x1b[:, t, :], x1[:, t, :],
                                row("ff2_b", 0, 128).unsqueeze(1).to_broadcast([128, 2, DIM]), ALU.add)\
                    .then_inc(s["x1b_done"], 1)
            for hf in range(2):
                gp.wait_ge(s["mv2_done"], hf + 1)
                rsqrt(ve2, mv2, rs2, 4 * hf, 4 * hf + 4, TOK, "rs2_done")
            for hf in range(2):
                gp.wait_ge(s["xn_done"], hf + 1)
                b = slice(4 * hf, 4 * hf + 4)
                g.tensor_tensor(hx[:, b, :], h[:, b, :], xn[:, b, :], ALU.add).then_inc(s["hx_done"], 1)
            for hf in range(2):
                gp.wait_ge(s["mv3_done"], hf + 1)
                rsqrt(ve3, mv3, rs3, 4 * hf, 4 * hf + 4, TOK, "rs3_done")

        @block.tensor
        def _(pe):
            mm, tr = nc.tensor.matmul, nc.tensor.transpose

            def five(out, wA, wAl, wB, wBl, aA, aAl, aB, aBh, start=True):
                mm(out, wA, aA, start=start, stop=False)
                mm(out, wAl, aA, start=False, stop=False)
                mm(out, wA, aAl, start=False, stop=False)
                mm(out, wBl, aBh, start=False, stop=False)
                return mm(out, wB, aB, start=False, stop=True)

            def w_still(out, w, a0, b0, n, tok, lay=(tA, tB)):
                A, B = lay
                return five(out, w[:, 0, a0:a0 + n], w[:, 1, a0:a0 + n], w[:, 0, b0:b0 + n],
                            w[0:FB, 1, b0:b0 + n], A[:, 0, tok], A[:, 1, tok], B[:, tok], B[0:FB, tok])

            def x_still(out, w, a0, b0, n, tok, lay=(tA, tB)):
                A, B = lay
                mm(out, A[:, 0, tok], w[:, 0, a0:a0 + n], start=True, stop=False)
                mm(out, A[:, 0, tok], w[:, 1, a0:a0 + n], start=False, stop=False)
                mm(out, A[:, 1, tok], w[:, 0, a0:a0 + n], start=False, stop=False)
                mm(out, B[0:FB, tok], w[0:FB, 1, b0:b0 + n], start=False, stop=False)
                return mm(out, B[:, tok], w[:, 0, b0:b0 + n], start=False, stop=True)

            def keep_busy(site, out):
                for k in range(FILL[site]):
                    mm(out[:, :], filler[:, 0:128], filler[:, :], start=True, stop=True)

            def patch(t):
                pe.wait_ge(d_patch[t], 16)
                for k in range(PK):
                    last = mm(bank[4 * (t // 2) + t % 2][:, 0:DIM], patches[:, t, k, :], patch_w[:, k, :],
                              start=(k == 0), stop=(k == PK - 1))
                last.then_inc(s["patch_ps"], 1)

            def turn_x(src, hf, made, atA, atB):
                pe.wait_ge(s[made], hf + 1)
                for i in range(2):
                    t = 2 * hf + i
                    tr(atA[:, 128 * i:128 * i + 128], src[:, t, 0:FA], c("ident"))
                    last = tr(atB[0:FB, 128 * i:128 * i + 128], src[:, t, FA:DIM], c("ident"))
                last.then_inc(s["xT_ps"], 1)

            def hidden(hf, turned, banks, read, done):
                for sig in ("tA_hi", "tA_lo", "tB_lo"):
                    pe.wait_ge(s[sig], turned)
                for m in range(FK):
                    if m >= 3:
                        pe.wait_ge(s[read], FK * hf + m - 2)
                    w_still(bank[4 * hf + banks[m % 3]][:, 0:H1], ff1_w, 128 * m, FF + 128 * m, 128,
                            slice(H1 * hf, H1 * hf + H1)).then_inc(s[done], 1)

            def ff_out(hf):
                outA, outB = bank[4 * hf][:, 0:H1], bank[4 * hf][:, H1:2 * H1]
                for k in range(FK):
                    pe.wait_ge(s["act1_lo"], FK * hf + k + 1)
                    hi, lo = act1s[:, hf, 0, k, :], act1s[:, hf, 1, k, :]
                    mm(outA, ff2_w[:, k, DOWN_HI["A"]], hi, start=(k == 0), stop=False)
                    mm(outA, ff2_w[:, k, DOWN_LO["A"]], hi, start=False, stop=False)
                    mm(outA, ff2_w[:, k, DOWN_HI["A"]], lo, start=False, stop=(k == FK - 1))
                for k in range(FK):
                    hi, lo = act1s[:, hf, 0, k, :], act1s[:, hf, 1, k, :]
                    mm(outB, ff2_w[:, k, B_BOTH], hi, start=(k == 0), stop=False, skip_group_check=True)
                    last = mm(outB[0:FB, :], ff2_w[:, k, DOWN_HI["B"]], lo, start=False, stop=(k == FK - 1),
                              skip_group_check=True)
                last.then_inc(s["y_ps"], 1)

            def qkv(hf):
                for sig in ("yA_lo", "yB_lo"):
                    pe.wait_ge(s[sig], hf + 1)
                tok = slice(H1 * hf, H1 * hf + H1)
                for part in range(2):
                    for ch in range(2):
                        last = w_still(bank[4 * hf + 1 + part][0:CH, H1 * ch:H1 * ch + H1], qkv_w,
                                       DIM * part + CH * ch, 3 * DIM + DIM * part + CH * ch, CH, tok, (yA, yB))
                last.then_inc(s["qk_ps"], 1)
                for i in range(2):
                    t = 2 * hf + i
                    last = x_still(bank[4 * hf + 3][:, DIM * i:DIM * i + DIM], qkv_w, 2 * DIM, 5 * DIM, DIM,
                                   slice(128 * t, 128 * t + 128), (yA, yB))
                last.then_inc(s["v_ps"], 1)

            def window_scores(i):
                hf, j = i // 3, i % 3
                pe.wait_ge(s["q_done"], 4 * hf + 4)
                pe.wait_ge(s["k_done"], 2 * hf + 2)
                for b in range(HALF_IMG):
                    for ch in range(2):
                        img = HALF_IMG * hf + b
                        last = mm(bank[4 * hf + j][:, 64 * (2 * b + ch):64 * (2 * b + ch) + 64],
                                  q_blk[32 * j:32 * j + 32, ch, img, :, :],
                                  kT[32 * j:32 * j + 32, ch, IMG_TOK * img:IMG_TOK * img + IMG_TOK],
                                  start=True, stop=True)
                last.then_inc(s["s_ps"], 1)

            def turn_prob(i):
                hf, j = i // 3, i % 3
                pe.wait_ge(s["s_norm"], i + 1)
                for b in range(HALF_IMG):
                    last = tr(bank[4 * hf + j][:, 128 * b:128 * b + 128],
                              prob[:, hf, j, 128 * b:128 * b + 128], c("ident"))
                last.then_inc(s["pT_ps"], 1)

            def window_values(i):
                hf, j = i // 3, i % 3
                pe.wait_ge(s["pT_done"], i + 1)
                pe.wait_ge(s["v_done"], 4 * hf + 4)
                for b in range(HALF_IMG):
                    last = mm(bank[4 * hf + j][0:64, 128 * b:128 * b + 128],
                              v_blk[:, HALF_IMG * hf + b, j, :], probT[:, hf, j, 128 * b:128 * b + 128],
                              start=True, stop=True)
                last.then_inc(s["o_ps"], 1)

            def project(hf):
                pe.wait_ge(s["o_done"], 3 * hf + 3)
                for i in range(2):
                    tok = slice(128 * (2 * hf + i), 128 * (2 * hf + i) + 128)
                    out = bank[4 * hf + 3][:, DIM * i:DIM * i + DIM]
                    mm(out, o01[:, tok], proj_w[:, 0, :], start=True, stop=False)
                    last = mm(out, o2[:, tok], proj_w[0:64, 1, :], start=False, stop=True)
                last.then_inc(s["proj_ps"], 1)

            def ff_out2(hf):
                for i in range(2):
                    for k in range(FK):
                        if i == 0:
                            pe.wait_ge(s["gelu2_done"], FK * hf + k + 1)
                        last = mm(bank[4 * hf + 3][:, DIM * i:DIM * i + DIM],
                                  act1[:, hf, k, 128 * i:128 * i + 128], ff2_raw[:, k, :],
                                  start=(k == 0), stop=(k == FK - 1))
                last.then_inc(s["ff2_ps"], 1)

            def hidden1(hf):
                hidden(hf, hf + 1, (1, 2, 3), "gelu_done", "hid1_ps")

            def hidden2(hf):
                hidden(hf, hf + 3, (2, 0, 1), "gelu2_done", "hid2_ps")

            pe.wait_ge(s["filler_done"], 1)
            keep_busy("patches", bank[7])
            pe.wait_ge(d_pw, 16)
            patch(0)
            patch(1)
            patch(2)
            pe.wait_ge(d_const, 16)
            keep_busy("turn_x0", bank[2])
            turn_x(x, 0, "x_done", bank[2], bank[3])
            patch(3)
            keep_busy("hidden0", bank[1])
            pe.wait_ge(s["ff1_lo"], 1)
            hidden1(0)
            keep_busy("turn_x1", bank[6])
            turn_x(x, 1, "x_done", bank[6], bank[7])
            keep_busy("ff_out0", bank[0])
            pe.wait_ge(s["ff2_lo"], 2)
            ff_out(0)
            keep_busy("hidden1", bank[5])
            hidden1(1)
            keep_busy("qkv0", bank[1])
            pe.wait_ge(s["qkv_lo"], 1)
            qkv(0)
            keep_busy("ff_out1", bank[4])
            ff_out(1)
            keep_busy("scores0", bank[0])
            window_scores(0)
            window_scores(1)
            window_scores(2)
            keep_busy("qkv1", bank[5])
            qkv(1)
            pe.wait_ge(s["v_done"], 4)
            for i in range(3):
                keep_busy(f"prob{i}", bank[3])
                turn_prob(i)
                keep_busy(f"scores{3 + i}", bank[3])
                window_scores(3 + i)
                keep_busy(f"values{i}", bank[3])
                window_values(i)
            keep_busy("prob3", bank[3])
            turn_prob(3)
            keep_busy("prob4", bank[3])
            turn_prob(4)
            pe.wait_ge(d_proj, 16)
            keep_busy("project0", bank[3])
            project(0)
            keep_busy("values3", bank[0])
            window_values(3)
            window_values(4)
            keep_busy("turn_x2", bank[0])
            turn_x(x1, 0, "x1_done", bank[0], bank[1])
            keep_busy("prob5", bank[2])
            turn_prob(5)
            keep_busy("values5", bank[2])
            window_values(5)
            keep_busy("hidden2", bank[2])
            hidden2(0)
            keep_busy("project1", bank[7])
            project(1)
            keep_busy("ff_out2", bank[4])
            ff_out2(0)
            keep_busy("turn_x3", bank[4])
            turn_x(x1, 1, "x1_done", bank[4], bank[5])
            keep_busy("hidden3", bank[6])
            hidden2(1)

            def turn_h(src, hf, atA, atB, done):
                for i in range(HALF_IMG):
                    b = HALF_IMG * hf + i
                    tr(atA[:, TOK * i:TOK * i + TOK], src[:, b, 0:FA], c("ident", TOK)[:, 0:TOK])
                    last = tr(atB[0:FB, TOK * i:TOK * i + TOK], src[:, b, FA:DIM], c("ident", TOK)[:, 0:TOK])
                last.then_inc(s[done], 1)

            def values_keys(hf):
                for sig in ("tA_hi", "tA_lo", "tB_lo"):
                    pe.wait_ge(s[sig], hf + 5)
                for i in (2 * hf, 2 * hf + 1):
                    for k in range(2):
                        b = 2 * i + k
                        last = x_still(bank[4 * hf + 2 + i % 2][0:TOK, VSEL * k:VSEL * k + VSEL], kv_w, DIM,
                                       2 * DIM + VSEL, VSEL, slice(TOK * b, TOK * b + TOK))
                    last.then_inc(s["vsel_ps"], 1)
                for ch in range(2):
                    last = w_still(bank[4 * hf + ch][0:CH, 0:H2N], kv_w, CH * ch, DIM + VSEL + CH * ch, CH,
                                   slice(H2N * hf, H2N * hf + H2N))
                last.then_inc(s["ak_ps"], 1)

            keep_busy("turn_h0", bank[0])
            pe.wait_ge(s["kv_split"], 1)
            pe.wait_ge(s["xn_done"], 1)
            turn_h(xn, 0, bank[0], bank[1], "hT_ps")
            keep_busy("vk0", bank[2])
            values_keys(0)
            keep_busy("ff_out3", bank[7])
            ff_out2(1)
            keep_busy("turn_h1", bank[4])
            pe.wait_ge(s["xn_done"], 2)
            turn_h(xn, 1, bank[4], bank[5], "hT_ps")
            keep_busy("vk1", bank[6])
            values_keys(1)
            pe.wait_ge(s["av_done"], 4)
            keep_busy("psel", bank[3])
            pe.wait_ge(s["psel_done"], 1)
            tr(bank[2][0:IMAGES, 0:TOK], psel[:, :], c("ident", TOK)[:, 0:TOK]).then_inc(s["psT_ps"], 1)
            keep_busy("pickT", bank[3])
            pe.wait_ge(s["pickT_done"], 1)
            tr(bank[2][0:TOK, 128:128 + IMAGES], pickT[:, :], c("ident", IMAGES)[:, 0:IMAGES])\
                .then_inc(s["pick_ps"], 1)
            keep_busy("pick", bank[3])
            pe.wait_ge(s["pick_done"], 1)
            mm(bank[2][0:TOK, 256:256 + IMAGES], c("tri", TOK), pick[:, :], start=True, stop=True)\
                .then_inc(s["cum_ps"], 1)
            keep_busy("hot", bank[3])
            pe.wait_ge(s["hot_done"], 2)
            for b in range(IMAGES):
                mm(bank[3][:, PICKED * b:PICKED * b + PICKED], xn[:, b, 0:FA], hot[:, b, :],
                   start=True, stop=True)
                last = mm(bank[6][0:FB, 256 + PICKED * b:256 + PICKED * b + PICKED], xn[:, b, FA:DIM],
                          hot[:, b, :], start=True, stop=True)
            last.then_inc(s["xs_ps"], 1)
            tr(bank[2][0:SLOTS, 384:384 + TOK], hotp[:, :, :].rearrange("p a b -> p (a b)"),
               c("ident", TOK)[:, 0:TOK]).then_inc(s["hotpT_ps"], 1)
            keep_busy("xs", bank[7])
            pe.wait_ge(s["xs_done"], 2)
            pe.wait_ge(d_aq, 16)
            for ch in range(2):
                out = bank[7][0:CH, SLOTS * ch:SLOTS * ch + SLOTS]
                mm(out, aq_w[:, 0, CH * ch:CH * ch + CH], xsA[:, :], start=True, stop=False)
                last = mm(out, aq_w[0:FB, 1, CH * ch:CH * ch + CH], xsB[:, :], start=False, stop=True)
            last.then_inc(s["aq_ps"], 1)
            pe.wait_ge(s["ak_even"], 1)
            keep_busy("aq", bank[0])
            for hf in range(2):
                pe.wait_ge(s["ak_even"], hf + 1)
                pe.wait_ge(s["ak_odd"], hf + 1)
                pe.wait_ge(s["aq_done"], 2)
                pe.wait_ge(s["hot_spread"], 1)
                for i in range(HALF_IMG):
                    b = HALF_IMG * hf + i
                    out = bank[4 * hf][0:QROWS, TOK * i:TOK * i + TOK]
                    mm(out, hot_heads[:, b, :], c("causal", TOK),
                       start=True, stop=False)
                    for ch in range(2):
                        last = mm(out, aq_blk[:, ch, b, :], akT[:, ch, TOK * b:TOK * b + TOK],
                                  start=False, stop=(ch == 1))
                last.then_inc(s["as_ps"], 1)
            for hf in range(2):
                keep_busy(f"as{hf}", bank[4 * hf + 1])
                pe.wait_ge(s["as_norm"], hf + 1)
                for i in range(HALF_IMG):
                    last = tr(bank[4 * hf + 1][0:TOK, QROWS * i:QROWS * i + QROWS],
                              aprob[:, hf, TOK * i:TOK * i + TOK], c("ident", QROWS)[:, 0:QROWS])
                last.then_inc(s["apT_ps"], 1)
                pe.wait_ge(s["hotpT_done"], 1)
                keep_busy(f"ap{hf}", bank[4 * hf + 2])
                pe.wait_ge(s["apT_done"], hf + 1)
                for ch in range(2):
                    for i in range(HALF_IMG):
                        at = 60 * (HALF_IMG * ch + i)
                        last = mm(bank[4 * hf + 2][0:CH, at:at + 60], av[:, HALF_IMG * hf + i, CH * ch:CH * ch + CH],
                                  aprobT[:, hf, QROWS * i + 60 * ch:QROWS * i + 60 * ch + 60],
                                  start=True, stop=True)
                last.then_inc(s["ac_ps"], 1)
            keep_busy("ac", bank[3])
            pe.wait_ge(s["ac_done"], 4)
            pe.wait_ge(d_outw, 16)
            for ch in range(2):
                last = mm(bank[3][0:SLOTS, 0:DIM], ctxT[:, ch, :, :], out_w[:, ch, :],
                          start=(ch == 0), stop=(ch == 1))
            last.then_inc(s["ao_ps"], 1)
            keep_busy("ao", bank[7])
            pe.wait_ge(s["ao_done"], 1)
            pe.wait_ge(s["hotpT_done"], 1)
            for i in range(4):
                for k in range(2):
                    last = mm(bank[(7 + i) % 8][0:TOK, DIM * k:DIM * k + DIM], hotpT[:, 2 * i + k, :],
                              arow[:, :], start=True, stop=True)
                last.then_inc(s["h2_ps"], 1)

            for hf in range(2):
                keep_busy(f"xn2_{hf}", bank[3 + 2 * hf])
                pe.wait_ge(s["xn2_done"], hf + 1)
                turn_h(xn2, hf, bank[3 + 2 * hf], bank[4 + 2 * hf], "h2T_ps")
            keep_busy("gl", bank[7])
            pe.wait_ge(s["gate_split"], 1)
            for hf in range(2):
                for sig in ("tA_hi", "tA_lo", "tB_lo"):
                    pe.wait_ge(s[sig], hf + 7)
                w_still(bank[7 if hf == 0 else 0][0:EXPERTS, 0:H2N], gate_w, 0, EXPERTS, EXPERTS,
                        slice(H2N * hf, H2N * hf + H2N)).then_inc(s["gl_ps"], 1)
            keep_busy("glt", bank[1])
            pe.wait_ge(s["gl_done"], 2)
            for b in range(IMAGES):
                last = tr(bank[1][0:TOK, EXPERTS * b:EXPERTS * b + EXPERTS], glT[:, TOK * b:TOK * b + TOK],
                          c("ident", EXPERTS)[:, 0:EXPERTS])
            last.then_inc(s["glt_ps"], 1)

            cuts = ((0, 512, bank[0][:, 0:512], bank[2][:, 0:512]),
                    (512, T2, bank[1][:, 0:256], bank[1][:, 256:512]))

            def up_gate(n, hf, p):
                tok = slice(H2N * hf, H2N * hf + H2N)
                if not isinstance(n, int) or n >= 1:
                    pe.wait_ge(s[f"silu{hf}"], n)
                w_still(bank[3 + 2 * hf][:, 0:H2N], ug_w[p], 0, 2 * HID, HID, tok).then_inc(s[f"u_ps{hf}"], 1)
                if not isinstance(n, int) or n >= 1:
                    pe.wait_ge(s[f"gated{hf}"], n)
                w_still(bank[4 + 2 * hf][:, 0:H2N], ug_w[p], HID, 3 * HID, HID, tok)\
                    .then_inc(s[f"g_ps{hf}"], 1)

            def spread(n, hf):
                if isinstance(n, int):
                    rhs = wrow[:, (n - 1) * T2 + H2N * hf:(n - 1) * T2 + H2N * hf + H2N]
                else:
                    rhs = wrow[:, bass.ds((n - 1) * T2 + H2N * hf, H2N)]
                if not isinstance(n, int) or n > 1 or hf:
                    pe.wait_ge(s["weighed"], 2 * (n - 1) + hf)
                mm(bank[7][:, 0:H2N], ones2[:, :], rhs, start=True, stop=True).then_inc(s["wb_ps"], 1)

            def down(n, part, p):
                a, b, outA, outB = cuts[part]
                hi, lo = hid_s[p][:, 0, a:b], hid_s[p][:, 1, a:b]
                kw = {"start": False, "stop": False, "skip_group_check": True}
                mm(outA, dn_w[p][:, DOWN_HI["A"]], hi, **kw)
                mm(outA, dn_w[p][:, DOWN_LO["A"]], hi, **kw)
                mm(outA, dn_w[p][:, DOWN_HI["A"]], lo, **kw)
                mm(outB, dn_w[p][:, B_BOTH], hi, **kw)
                return mm(outB[0:FB, :], dn_w[p][:, DOWN_HI["B"]], lo, **kw)

            def expert(n, p):
                pe.wait_ge(s["ug_hi"], n + 1)
                pe.wait_ge(s["ug_lo"], n + 1)
                up_gate(n, 0, p)
                spread(n, 0)
                up_gate(n, 1, p)
                spread(n, 1)
                pe.wait_ge(s["hid_hi"], 2 * n)
                pe.wait_ge(s["hid_lo"], 2 * n)
                pe.wait_ge(s["dn_hi"], n)
                pe.wait_ge(s["dn_lo"], 2 * n)
                down(n - 1, 0, 1 - p)
                down(n - 1, 1, 1 - p).then_inc(s["down_done"], 1)

            keep_busy("ug0", bank[2])
            pe.wait_ge(s["ug_hi"], 1)
            pe.wait_ge(s["ug_lo"], 1)
            up_gate(0, 0, 0)
            up_gate(0, 1, 0)
            pe.wait_ge(s["gd_done"], 1)
            started = set()
            for b in range(IMAGES):
                for t0, t1 in ((TOK * b, min(TOK * b + TOK, 512)), (max(TOK * b, 512), TOK * b + TOK)):
                    if t0 >= t1:
                        continue
                    cut = 0 if t1 <= 512 else 1
                    for part in range(2):
                        which = (cut, part) if cut == 0 else (1, 0)
                        out = cuts[cut][2 + part][:, t0 - cuts[cut][0]:t1 - cuts[cut][0]]
                        a = c("ident", TOK)[:, t0 - TOK * b:t1 - TOK * b]
                        mm(out, h2[:, b, FA * part:FA * part + FA], a, start=which not in started,
                           stop=False, skip_group_check=True)
                        started.add(which)
            keep_busy("wfull", bank[7])
            for hf in range(2):
                pe.wait_ge(s["wfull_done"], 1)
                if hf == 1:
                    pe.wait_ge(s["wT_lo"], 1)
                for i in range(HALF_IMG):
                    last = tr(bank[7][0:EXPERTS, TOK * i:TOK * i + TOK], wfull[:, HALF_IMG * hf + i, :],
                              c("ident", TOK)[:, 0:TOK])
                last.then_inc(s["wT_ps"], 1)
            pe.wait_ge(s["wT_lo"], 2)
            pe.wait_ge(s["bd_split"], 1)
            for a, b, outA, outB in cuts:
                kw = {"start": False, "stop": False, "skip_group_check": True}
                mm(outA, bd_w[0:48, 0, 0:FA], wT[0:48, a:b], **kw)
                mm(outA, bd_w[0:EXPERTS, 1, 0:FA], wT[0:EXPERTS, a:b], **kw)
                mm(outB[0:FB, :], bd_w[0:48, 0, FA:DIM], wT[0:48, a:b], **kw)
                mm(outB[0:FB, :], bd_w[0:EXPERTS, 1, FA:DIM], wT[0:EXPERTS, a:b], **kw)
            keep_busy("wrow", bank[7])
            pe.wait_ge(d_wrow, 32)
            expert(1, 1)
            with pe.Fori(0, 7) as it:
                expert(2 * it + 2, 0)
                expert(2 * it + 3, 1)
            expert(16, 0)
            pe.wait_ge(s["hid_hi"], 34)
            pe.wait_ge(s["hid_lo"], 34)
            pe.wait_ge(s["dn_hi"], 17)
            pe.wait_ge(s["dn_lo"], 34)
            down(16, 0, 0)
            down(16, 1, 0).then_inc(s["down_done"], 1)

        @block.scalar
        def _(act):
            a = nc.scalar.activation

            def hi_of_turned(atA, atB, n, tok, done, k):
                act.wait_ge(s[done], k)
                a(tA[:, 0, tok], atA, ACT.Copy).then_inc(s["tA_hi"], 1)
                a(tB[0:FB, tok], atB, ACT.Copy).then_inc(s["tB_hi"], 1)

            def turned_hi(hf, k, atA, atB):
                hi_of_turned(atA[:, 0:H1], atB[0:FB, 0:H1], H1, slice(H1 * hf, H1 * hf + H1), "xT_ps", k)

            def gelu(hf, banks, ready, done):
                for m in range(FK):
                    act.wait_ge(s[ready], FK * hf + m + 1)
                    a(act1[:, hf, m, :], bank[4 * hf + banks[m % 3]][:, 0:H1], ACT.Gelu_apprx_tanh,
                      bias=col("ff1_b", 128, m)).then_inc(s[done], 1)

            def ff_out(hf):
                tok = slice(H1 * hf, H1 * hf + H1)
                act.wait_ge(s["y_ps"], hf + 1)
                a(ytmp[:, tok], bank[4 * hf][FB:128, H1:2 * H1], ACT.Copy).then_inc(s["yB_moved"], 1)
                a(yA[:, 0, tok], bank[4 * hf][:, 0:H1], ACT.Identity, bias=col("ff2_bA", 128))\
                    .then_inc(s["yA_hi"], 1)
                act.wait_ge(s["yB_sum"], hf + 1)
                a(yB[0:FB, tok], ybf[:, tok], ACT.Copy).then_inc(s["yB_hi"], 1)

            def queries(hf):
                act.wait_ge(s["qk_ps"], hf + 1)
                for ch in range(2):
                    for par in range(2):
                        a(q_blk[:, ch, HALF_IMG * hf:HALF_IMG * hf + HALF_IMG, par, :],
                          v3(bank[4 * hf + 1][0:CH, H1 * ch:H1 * ch + H1], IMG_TOK), ACT.Identity,
                          bias=bqm[:, ch, par:par + 1], scale=c("parity", CH)[:, par:par + 1])\
                            .then_inc(s["q_done"], 1)

            def window_exp(i):
                act.wait_ge(s["s_sub"], i + 1)
                a(prob[:, i // 3, i % 3, :], prob[:, i // 3, i % 3, :], ACT.Exp, scale=HEAD ** -0.5)\
                    .then_inc(s["s_exp"], 1)

            def prob_out(i):
                act.wait_ge(s["pT_ps"], i + 1)
                a(probT[:, i // 3, i % 3, :], bank[4 * (i // 3) + i % 3][:, :], ACT.Copy)\
                    .then_inc(s["pT_done"], 1)

            def even_heads(i):
                hf, j = i // 3, i % 3
                act.wait_ge(s["o_ps"], i + 1)
                even = bank[4 * hf + j][0:64, :].rearrange("p (b h q) -> p b h q", h=2, q=IMG_TOK)[:, :, 0, :]
                a(v3(otmp[:, hf, j, :], IMG_TOK), even, ACT.Copy, scale=c("parity", 64)[:, 0:1])\
                    .then_inc(s["o_even"], 1)

            def load_table(function, k):
                act.wait_ge(s["filler_done"], 2)
                if k:
                    act.wait_ge(s["table_done"], k)
                a(table[0:1, k:k + 1], table[0:1, k:k + 1], function).then_inc(s["table_done"], 1)

            load_table(ACT.Gelu_apprx_tanh, 0)
            act.wait_ge(d_ff1, 16)
            a(ff1_w[:, 0, :], ff1_raw[:, :], ACT.Copy).then_inc(s["ff1_hi"], 1)
            turned_hi(0, 1, bank[2], bank[3])
            act.wait_ge(d_ff2, 16)
            a(ff2_w[:, :, 0:DIM], ff2_raw[:, :, :], ACT.Copy).then_inc(s["ff2_hi"], 1)
            act.wait_ge(d_qkv, 16)
            a(qkv_w[:, 0, :], qkv_raw[:, :], ACT.Copy).then_inc(s["qkv_hi"], 1)
            act.wait_ge(d_cols, 16)
            gelu(0, (1, 2, 3), "hid1_ps", "gelu_done")
            turned_hi(1, 2, bank[6], bank[7])
            ff_out(0)
            gelu(1, (1, 2, 3), "hid1_ps", "gelu_done")
            load_table(ACT.Exp, 1)
            act.wait_ge(s["bqm_done"], 2)
            queries(0)
            ff_out(1)
            window_exp(0)
            window_exp(1)
            queries(1)
            window_exp(2)
            for i in range(3):
                prob_out(i)
                window_exp(3 + i)
                even_heads(i)
            prob_out(3)
            prob_out(4)
            even_heads(3)
            even_heads(4)
            load_table(ACT.Gelu_apprx_tanh, 2)
            turned_hi(0, 3, bank[0], bank[1])
            prob_out(5)
            even_heads(5)
            gelu(0, (2, 0, 1), "hid2_ps", "gelu2_done")
            turned_hi(1, 4, bank[4], bank[5])
            gelu(1, (2, 0, 1), "hid2_ps", "gelu2_done")

            load_table(ACT.Exp, 3)
            for hf in range(2):
                hi_of_turned(bank[4 * hf][:, 0:H2N], bank[4 * hf + 1][0:FB, 0:H2N], H2N,
                             slice(H2N * hf, H2N * hf + H2N), "hT_ps", hf + 1)
                act.wait_ge(s["ak_ps"], hf + 1)
                a(akT[:, 0, H2N * hf:H2N * hf + H2N], bank[4 * hf][0:CH, 0:H2N], ACT.Identity,
                  bias=col("ak_b", CH, 0)).then_inc(s["ak_even"], 1)
            act.wait_ge(s["ld_done"], 1)
            a(le[:, :, :], ld[:, :, :], ACT.Exp).then_inc(s["le_done"], 1)
            act.wait_ge(s["hot_done"], 1)
            a(hot_heads[:, :, :].rearrange("p b (h i) -> p b h i", h=HEADS),
              hot[:, :, :].unsqueeze(2).to_broadcast([TOK, IMAGES, HEADS, PICKED]), ACT.Copy)\
                .then_inc(s["hot_spread"], 1)
            act.wait_ge(s["xs_ps"], 1)
            a(xsB[:, :], bank[6][0:FB, 256:256 + SLOTS], ACT.Copy).then_inc(s["xs_done"], 1)
            for hf in range(2):
                act.wait_ge(s["as_sub"], hf + 1)
                a(aprob[:, hf, :], aprob[:, hf, :], ACT.Exp).then_inc(s["as_exp"], 1)
            for hf in range(2):
                act.wait_ge(s["apT_ps"], hf + 1)
                a(aprobT[:, hf, :], bank[4 * hf + 1][0:TOK, 0:HALF_IMG * QROWS], ACT.Copy)\
                    .then_inc(s["apT_done"], 1)

            for hf in range(2):
                hi_of_turned(bank[3 + 2 * hf][:, 0:H2N], bank[4 + 2 * hf][0:FB, 0:H2N], H2N,
                             slice(H2N * hf, H2N * hf + H2N), "h2T_ps", hf + 1)
            for hf in range(2):
                act.wait_ge(s["gl_ps"], hf + 1)
                a(glT[:, H2N * hf:H2N * hf + H2N], bank[7 if hf == 0 else 0][0:EXPERTS, 0:H2N], ACT.Identity,
                  bias=col("gate_b", EXPERTS)).then_inc(s["gl_done"], 1)
            act.wait_ge(d_ug[0], 16)
            a(ug_w[0][:, 0, :], expert_raw[:, 0, 0:4 * HID], ACT.Copy).then_inc(s["ug_hi"], 1)
            act.wait_ge(s["gd_done"], 1)
            a(gexp[:, :, :], gexp[:, :, :], ACT.Exp).then_inc(s["ge_done"], 1)

            load_table(ACT.Silu, 4)

            def split_up(n, p):
                act.wait_ge(d_ug[p], 8 * (n - p) + 16)
                if not isinstance(n, int) or n >= 2:
                    act.wait_ge(s["u_ps1"], n - 1)
                    act.wait_ge(s["g_ps1"], n - 1)
                a(ug_w[p][:, 0, :], expert_raw[:, p, 0:4 * HID], ACT.Copy).then_inc(s["ug_hi"], 1)

            def gate_act(n, hf, p):
                if hf == 0:
                    act.wait_ge(d_dn[p], 8 * (n - p) + 16)
                act.wait_ge(s[f"u_ps{hf}"], n + 1)
                if not isinstance(n, int) or n >= 1:
                    act.wait_ge(s[f"gated{hf}"], n)
                a(silu[hf][:, :], bank[3 + 2 * hf][:, 0:H2N], ACT.Silu,
                  bias=expert_raw[:, p, BU:BU + 1]).then_inc(s[f"silu{hf}"], 1)

            def hid_hi(n, hf, p):
                if isinstance(n, int) and n == 0:
                    act.wait_ge(s[f"gated{hf}"], 1)
                else:
                    act.wait_ge(s["weighed"], 2 * (n - 1) + hf + 1)
                    if not isinstance(n, int) or n > 1:
                        act.wait_ge(s["down_done"], n - 1)
                a(hid_s[p][:, 0, H2N * hf:H2N * hf + H2N], hid[hf][:, :], ACT.Copy)\
                    .then_inc(s["hid_hi"], 1)

            def expert(n, p, more=True):
                gate_act(n, 0, p)
                if not isinstance(n, int) or n > 1:
                    act.wait_ge(s["down_done"], n - 1)
                a(dn_w[p][:, 0:DIM], expert_raw[:, p, DOWN0:DOWN0 + DIM], ACT.Copy).then_inc(s["dn_hi"], 1)
                if more:
                    split_up(n + 1, 1 - p)
                gate_act(n, 1, p)
                hid_hi(n, 0, p)
                hid_hi(n, 1, p)

            expert(0, 0)
            for hf in range(2):
                act.wait_ge(s["wT_ps"], hf + 1)
                if hf == 0:
                    act.wait_ge(s["zeros_done"], 12)
                a(wT[0:EXPERTS, H2N * hf:H2N * hf + H2N], bank[7][0:EXPERTS, 0:H2N], ACT.Copy)\
                    .then_inc(s["wT_hi"], 1)
            expert(1, 1)
            with act.Fori(0, 7) as it:
                expert(2 * it + 2, 0)
                expert(2 * it + 3, 1)
            expert(16, 0, more=False)
            act.wait_ge(s["down_done"], 17)
            a(fin_tmp[:, 0:512], bank[2][FB:128, 0:512], ACT.Copy).then_inc(s["fin_moved"], 1)
            a(fin_tmp[:, 512:T2], bank[1][FB:128, 256:512], ACT.Copy).then_inc(s["fin_moved"], 1)

        @block.vector
        def _(dve):
            v = nc.vector
            step, after = chain(dve, "vec_step")

            def lo_of_turned(atA, atB, tok, k):
                dve.wait_ge(s["tA_hi"], k)
                v.tensor_tensor(tA[:, 1, tok], atA, f(tA[:, 0, tok]), ALU.subtract).then_inc(s["tA_lo"], 1)
                dve.wait_ge(s["tB_hi"], k)
                v.tensor_tensor(tB[FB:128, tok], atB, f(tB[0:FB, tok]), ALU.subtract).then_inc(s["tB_lo"], 1)

            def token_stats(t):
                dve.wait_ge(s["patch_ps"], t + 1)
                v.tensor_tensor(x0[:, t, :], bank[4 * (t // 2) + t % 2][:, 0:DIM],
                                row("patch_b", 0, 128), ALU.add).then_inc(s["x0_done"], 1)
                dve.wait_ge(s["x0_done"], t + 1)
                k = step(v.bn_stats(st1[:, t, :], x0[:, t, :]))
                after(k)
                v.bn_aggr(mv1[:, t, :], st1[:, t, :]).then_inc(s["mv1_done"], 1)

            def token_norm(hf, kb):
                ts = slice(2 * hf, 2 * hf + 2)
                dve.wait_ge(s["mv1_done"], 2 * hf + 2)
                dve.wait_ge(s["rs1_done"], hf + 1)
                for t in (2 * hf, 2 * hf + 1):
                    k = step(v.tensor_scalar(x0[:, t, :], x0[:, t, :], mv1[:, t, 0:1], rs1[:, t:t + 1],
                                             ALU.subtract, ALU.mult))
                after(k)
                k = step(v.tensor_tensor(x0[:, ts, :], x0[:, ts, :],
                                         row("ln_g", 0, 128).unsqueeze(1).to_broadcast([128, 2, DIM]), ALU.mult))
                after(max(k, kb))
                v.tensor_tensor(x[:, ts, :], x0[:, ts, :], bpe[:, :].unsqueeze(1).to_broadcast([128, 2, DIM]),
                                ALU.add).then_inc(s["x_done"], 1)

            def turned_lo(hf, k, atA, atB):
                lo_of_turned(atA[:, 0:H1], atB[0:FB, 0:H1], slice(H1 * hf, H1 * hf + H1), k)

            def split_hidden(hf):
                for m in range(FK):
                    i = FK * hf + m
                    dve.wait_ge(s["gelu_done"], i + 1)
                    v.tensor_copy(act1s[:, hf, 0, m, :], act1[:, hf, m, :]).then_inc(s["act1_hi"], 1)
                    dve.wait_ge(s["act1_hi"], i + 1)
                    v.tensor_tensor(act1s[:, hf, 1, m, :], act1[:, hf, m, :], f(act1s[:, hf, 0, m, :]),
                                    ALU.subtract).then_inc(s["act1_lo"], 1)

            def ff_out(hf):
                tok = slice(H1 * hf, H1 * hf + H1)
                dve.wait_ge(s["yB_moved"], hf + 1)
                dve.wait_ge(s["yA_hi"], hf + 1)
                v.scalar_tensor_tensor(ybf[:, tok], bank[4 * hf][0:FB, H1:2 * H1], col("ff2_bB", FB),
                                       ytmp[:, tok], ALU.add, ALU.add).then_inc(s["yB_sum"], 1)
                v.scalar_tensor_tensor(yA[:, 1, tok], bank[4 * hf][:, 0:H1], col("ff2_bA", 128),
                                       f(yA[:, 0, tok]), ALU.add, ALU.subtract).then_inc(s["yA_lo"], 1)
                dve.wait_ge(s["yB_hi"], hf + 1)
                v.tensor_tensor(yB[FB:128, tok], ybf[:, tok], f(yB[0:FB, tok]), ALU.subtract)\
                    .then_inc(s["yB_lo"], 1)

            def keys_values(hf):
                dve.wait_ge(s["qk_ps"], hf + 1)
                for ch in range(2):
                    v.tensor_scalar(kT[:, ch, H1 * hf:H1 * hf + H1],
                                    bank[4 * hf + 2][0:CH, H1 * ch:H1 * ch + H1],
                                    col("k_b", CH, ch), None, ALU.add).then_inc(s["k_done"], 1)
                dve.wait_ge(s["v_ps"], hf + 1)
                for i in range(2):
                    for ch in range(2):
                        src = bank[4 * hf + 3][64 * i:64 * i + 64, 0:2 * DIM].rearrange(
                            "p (t c j k) -> p t c j k", t=2, c=2, j=3)[:, :, ch, :, :]
                        bias = row("v_b", 64 * i, 64 * i + 64)[:, CH * ch:CH * ch + CH]
                        first = HALF_IMG * hf + i
                        v.tensor_tensor(v_blk[64 * ch:64 * ch + 64, first:first + 3:2, :, 32 * ch:32 * ch + 32],
                                        src, v3(bias, 32).unsqueeze(1).to_broadcast([64, 2, 3, 32]), ALU.add)\
                            .then_inc(s["v_done"], 1)

            def softmax_sub(src, dst, mx, n, groups, ready, k, sub):
                wide = [n, groups, src.shape[-1]]
                dve.wait_ge(s[ready], k)
                j = step(v.tensor_reduce(mx, src, AXX, ALU.max))
                after(j)
                v.tensor_tensor(dst, src, mx.unsqueeze(2).to_broadcast(wide), ALU.subtract).then_inc(s[sub], 1)

            def softmax_norm(dst, sm, rc, n, groups, k, exp, norm):
                wide = [n, groups, dst.shape[-1]]
                dve.wait_ge(s[exp], k)
                j = step(v.tensor_reduce(sm, dst, AXX, ALU.add))
                after(j)
                j = step(v.reciprocal(rc, sm))
                after(j)
                v.tensor_tensor(dst, dst, rc.unsqueeze(2).to_broadcast(wide), ALU.mult).then_inc(s[norm], 1)

            def window_sub(i):
                hf, j = i // 3, i % 3
                softmax_sub(v3(bank[4 * hf + j][:, :], IMG_TOK), v3(prob[:, hf, j, :], IMG_TOK),
                            smax[:, hf, j, :], 128, 8, "s_ps", i + 1, "s_sub")

            def window_norm(i):
                hf, j = i // 3, i % 3
                softmax_norm(v3(prob[:, hf, j, :], IMG_TOK), ssum[:, hf, j, :], srec[:, hf, j, :], 128, 8,
                             i + 1, "s_exp", "s_norm")

            def odd_heads(i):
                hf, j = i // 3, i % 3
                dve.wait_ge(s["o_even"], i + 1)
                odd = bank[4 * hf + j][0:64, :].rearrange("p (b h q) -> p b h q", h=2, q=IMG_TOK)[:, :, 1, :]
                tok = slice(H1 * hf, H1 * hf + H1)
                dst = (o01[0:64, tok], o01[64:128, tok], o2[:, tok])[j]
                v.scalar_tensor_tensor(v3(dst, IMG_TOK), odd, c("parity", 64)[:, 1:2],
                                       v3(otmp[:, hf, j, :], IMG_TOK), ALU.mult, ALU.add)\
                    .then_inc(s["o_done"], 1)

            def residual(hf):
                dve.wait_ge(s["proj_ps"], hf + 1)
                dve.wait_ge(s["xpb_done"], hf + 1)
                ts = slice(2 * hf, 2 * hf + 2)
                v.tensor_tensor(x1[:, ts, :], v3(bank[4 * hf + 3][:, 0:2 * DIM], DIM), xpb[:, ts, :], ALU.add)\
                    .then_inc(s["x1_done"], 1)

            dve.wait_ge(d_rows, 16)
            token_stats(0)
            token_stats(1)
            dve.wait_ge(d_const, 16)
            kb = step(v.tensor_tensor(bpe[:, :], row("ln_b", 0, 128), c("pe"), ALU.add))
            token_norm(0, kb)
            dve.wait_ge(d_ff1, 16)
            dve.wait_ge(s["ff1_hi"], 1)
            v.tensor_tensor(ff1_w[:, 1, :], ff1_raw[:, :], f(ff1_w[:, 0, :]), ALU.subtract)\
                .then_inc(s["ff1_lo"], 1)
            turned_lo(0, 1, bank[2], bank[3])
            dve.wait_ge(d_cols, 16)
            for ch in range(2):
                v.tensor_scalar(bqm[:, ch, :], c("parity", CH), col("q_b", CH, ch), None, ALU.mult)\
                    .then_inc(s["bqm_done"], 1)
            token_stats(2)
            token_stats(3)
            token_norm(1, kb)
            split_hidden(0)
            turned_lo(1, 2, bank[6], bank[7])
            ff_out(0)
            split_hidden(1)
            dve.wait_ge(s["zeros_done"], 1)
            keys_values(0)
            ff_out(1)
            window_sub(0)
            window_sub(1)
            window_norm(0)
            keys_values(1)
            window_sub(2)
            window_norm(1)
            window_sub(3)
            window_norm(2)
            odd_heads(0)
            window_sub(4)
            window_norm(3)
            odd_heads(1)
            window_sub(5)
            window_norm(4)
            odd_heads(2)
            window_norm(5)
            residual(0)
            odd_heads(3)
            turned_lo(0, 3, bank[0], bank[1])
            odd_heads(4)
            odd_heads(5)
            residual(1)

            def layer_norm(src, st, mv, rs, dst, hf, done_mv, done_rs, done):
                for b in range(HALF_IMG * hf, HALF_IMG * hf + HALF_IMG):
                    k = step(v.bn_stats(st[:, b, :], src[:, b, 0:DIM]))
                for b in range(HALF_IMG * hf, HALF_IMG * hf + HALF_IMG):
                    if b == HALF_IMG * hf:
                        after(k)
                    last = v.bn_aggr(mv[:, b, :], st[:, b, :])
                last.then_inc(s[done_mv], 1)

            def normalise(src, mv, rs, dst, hf, done_mv, done_rs, done):
                dve.wait_ge(s[done_mv], hf + 1)
                dve.wait_ge(s[done_rs], hf + 1)
                for b in range(HALF_IMG * hf, HALF_IMG * hf + HALF_IMG):
                    last = v.tensor_scalar(dst[:, b, :], src[:, b, 0:DIM], mv[:, b, 0:1], rs[:, b:b + 1],
                                           ALU.subtract, ALU.mult)
                last.then_inc(s[done], 1)

            def image_rows(hf):
                dve.wait_ge(s["ff2_ps"], hf + 1)
                dve.wait_ge(s["x1b_done"], hf + 1)
                for i in range(2):
                    first = HALF_IMG * hf + i
                    v.tensor_tensor(h[0:IMG_TOK, first:first + 3:2, :],
                                    v3(bank[4 * hf + 3][64 * i:64 * i + 64, 0:2 * DIM], DIM),
                                    x1b[64 * i:64 * i + 64, 2 * hf:2 * hf + 2, :], ALU.add)\
                        .then_inc(s["h_img"], 1)
                dve.wait_ge(s["h_img"], 2 * hf + 2)
                layer_norm(h, st2, mv2, rs2, xn, hf, "mv2_done", "rs2_done", "xn_done")

            def values_keys(hf):
                for i in (2 * hf, 2 * hf + 1):
                    dve.wait_ge(s["vsel_ps"], i + 1)
                    src = v3(bank[4 * hf + 2 + i % 2][0:TOK, 0:2 * VSEL], VSEL)
                    two = slice(2 * i, 2 * i + 2)
                    kl = step(v.tensor_tensor(lg[:, two, :], src[:, :, DIM:VSEL],
                                              row("sel_b", 0, TOK).unsqueeze(1).to_broadcast([TOK, 2, 2]),
                                              ALU.add))
                    v.tensor_tensor(av[:, two, :], src[:, :, 0:DIM],
                                    row("av_b", 0, TOK).unsqueeze(1).to_broadcast([TOK, 2, DIM]), ALU.add)\
                        .then_inc(s["av_done"], 1)
                return kl

            def keys_chunk1(hf):
                dve.wait_ge(s["ak_ps"], hf + 1)
                v.tensor_scalar(akT[:, 1, H2N * hf:H2N * hf + H2N], bank[4 * hf + 1][0:CH, 0:H2N],
                                col("ak_b", CH, 1), None, ALU.add).then_inc(s["ak_odd"], 1)

            dve.wait_ge(d_txt, 16)
            image_rows(0)
            turned_lo(1, 4, bank[4], bank[5])
            normalise(h, mv2, rs2, xn, 0, "mv2_done", "rs2_done", "xn_done")
            k = step(v.reciprocal(itemp[:, :], row("temp", 0, TOK)))
            lo_of_turned(bank[0][:, 0:H2N], bank[1][0:FB, 0:H2N], slice(0, H2N), 5)
            values_keys(0)
            keys_chunk1(0)
            image_rows(1)
            normalise(h, mv2, rs2, xn, 1, "mv2_done", "rs2_done", "xn_done")
            lo_of_turned(bank[4][:, 0:H2N], bank[5][0:FB, 0:H2N], slice(H2N, T2), 6)
            kl = values_keys(1)
            after(kl)
            k = step(v.tensor_scalar(lgt[:, :, :], lg[:, :, :], itemp[:, 0:1], None, ALU.mult))
            after(k)
            k = step(v.tensor_tensor(lmax[:, :], lgt[:, :, 0], lgt[:, :, 1], ALU.max))
            after(k)
            v.tensor_tensor(ld[:, :, :], lgt[:, :, :], lmax[:, :].unsqueeze(2).to_broadcast([TOK, IMAGES, 2]),
                            ALU.subtract).then_inc(s["ld_done"], 1)
            dve.wait_ge(s["le_done"], 1)
            k = step(v.tensor_tensor(lsum[:, :], le[:, :, 0], le[:, :, 1], ALU.add))
            after(k)
            k = step(v.reciprocal(lrec[:, :], lsum[:, :]))
            after(k)
            v.tensor_tensor(psel[:, :], le[:, :, 1], lrec[:, :], ALU.mult).then_inc(s["psel_done"], 1)
            dve.wait_ge(s["psT_ps"], 1)
            dve.wait_ge(s["zeros_done"], 12)
            k = step(v.tensor_copy(pT[:, 0:TOK], bank[2][0:IMAGES, 0:TOK]))
            after(k)
            k = step(v.max(top8[:, :], pT[:, 0:TOK]))
            after(k)
            k = step(v.match_replace(out=pT8[:, :], in_to_replace=top8[:, :], in_values=pT[:, :], imm_value=GONE))
            after(k)
            k = step(v.max(next8[:, :], pT8[:, 0:TOK]))
            after(k)
            k = step(v.tensor_copy(last2[:, 0:2], next8[:, 0:2]))
            after(k)
            k = step(v.match_replace(out=pT10[:, :], in_to_replace=last2[:, :], in_values=pT8[:, :],
                                     imm_value=GONE))
            after(k)
            v.tensor_tensor(pickT[:, :], pT10[:, 0:TOK], pT[:, 0:TOK], ALU.not_equal)\
                .then_inc(s["pickT_done"], 1)
            dve.wait_ge(s["pick_ps"], 1)
            v.tensor_copy(pick[:, :], bank[2][0:TOK, 128:128 + IMAGES]).then_inc(s["pick_done"], 1)
            keys_chunk1(1)
            dve.wait_ge(s["cum_ps"], 1)
            dve.wait_ge(s["pick_done"], 1)
            k = step(v.tensor_tensor(rank[:, :], bank[2][0:TOK, 256:256 + IMAGES], pick[:, :], ALU.mult))
            after(k)
            wide = [TOK, IMAGES, PICKED]
            v.tensor_tensor(hot[:, :, :], rank[:, :].unsqueeze(2).to_broadcast(wide),
                            c("iota", TOK).unsqueeze(1).to_broadcast(wide), ALU.is_equal)\
                .then_inc(s["hot_done"], 1)
            dve.wait_ge(s["hot_done"], 1)
            v.tensor_tensor(hotp[:, :, :], hot[:, :, :], psel[:, :].unsqueeze(2).to_broadcast(wide), ALU.mult)\
                .then_inc(s["hot_done"], 1)
            dve.wait_ge(s["xs_ps"], 1)
            v.tensor_copy(xsA[:, :], bank[3][:, 0:SLOTS]).then_inc(s["xs_done"], 1)
            dve.wait_ge(s["aq_ps"], 1)
            for ch in range(2):
                k = step(v.tensor_scalar(aq[:, ch, :], bank[7][0:CH, SLOTS * ch:SLOTS * ch + SLOTS],
                                         col("aq_b", CH, ch), HEAD ** -0.5, ALU.add, ALU.mult))
            after(k)
            wide = [CH, IMAGES, CHH, PICKED]
            for ch in range(2):
                dst = aq_blk[:, ch, :, 60 * ch:60 * ch + 60].rearrange("p b (h i) -> p b h i", h=CHH)
                v.tensor_tensor(dst, v3(aq[:, ch, :], PICKED).unsqueeze(2).to_broadcast(wide),
                                c("head", CH).unsqueeze(1).unsqueeze(3).to_broadcast(wide), ALU.mult)\
                    .then_inc(s["aq_done"], 1)
            dve.wait_ge(s["hotpT_ps"], 1)
            wide = [SLOTS, IMAGES, TOK]
            v.tensor_tensor(hotpT[:, :, :], bank[2][0:SLOTS, 384:384 + TOK].unsqueeze(1).to_broadcast(wide),
                            c("block", SLOTS).unsqueeze(2).to_broadcast(wide), ALU.mult)\
                .then_inc(s["hotpT_done"], 1)
            for hf in range(2):
                b = slice(HALF_IMG * hf, HALF_IMG * hf + HALF_IMG)
                softmax_sub(v3(bank[4 * hf][0:QROWS, 0:H2N], TOK), v3(aprob[:, hf, :], TOK), amax[:, b],
                            QROWS, HALF_IMG, "as_ps", hf + 1, "as_sub")
            for hf in range(2):
                b = slice(HALF_IMG * hf, HALF_IMG * hf + HALF_IMG)
                softmax_norm(v3(aprob[:, hf, :], TOK), asum[:, b], arec[:, b], QROWS, HALF_IMG, hf + 1,
                             "as_exp", "as_norm")
            for hf in range(2):
                dve.wait_ge(s["ac_ps"], hf + 1)
                wide = [CH, 2 * HALF_IMG, CHH, PICKED]
                buf = actx[:, hf, :, :]
                k = step(v.tensor_tensor(
                    buf.rearrange("p c (h i) -> p c h i", h=CHH),
                    bank[4 * hf + 2][0:CH, 0:480].rearrange("p (c h i) -> p c h i", c=2 * HALF_IMG, h=CHH),
                    c("head", CH).unsqueeze(1).unsqueeze(3).to_broadcast(wide), ALU.mult))
                after(k)
                for ch in range(2):
                    v.tensor_reduce(v3(ctxT[:, ch, hf, :], PICKED),
                                    buf[:, HALF_IMG * ch:HALF_IMG * ch + HALF_IMG, :].rearrange(
                                        "p c (h i) -> p c i h", h=CHH), AXX, ALU.add)\
                        .then_inc(s["ac_done"], 1)
            dve.wait_ge(s["ao_ps"], 1)
            v.tensor_tensor(arow[:, :], bank[3][0:SLOTS, 0:DIM], row("out_b", 0, SLOTS), ALU.add)\
                .then_inc(s["ao_done"], 1)
            for i in range(4):
                dve.wait_ge(s["h2_ps"], i + 1)
                dve.wait_ge(s["hx_done"], i // 2 + 1)
                two = slice(2 * i, 2 * i + 2)
                v.tensor_tensor(h2[:, two, 0:DIM], v3(bank[(7 + i) % 8][0:TOK, 0:2 * DIM], DIM), hx[:, two, :],
                                ALU.add).then_inc(s["h2_done"], 1)
                if i % 2:
                    dve.wait_ge(s["h2_done"], i + 1)
                    layer_norm(h2, st3, mv3, rs3, xn2, i // 2, "mv3_done", "rs3_done", "xn2_done")
            for hf in range(2):
                normalise(h2, mv3, rs3, xn2, hf, "mv3_done", "rs3_done", "xn2_done")

            for hf in range(2):
                lo_of_turned(bank[3 + 2 * hf][:, 0:H2N], bank[4 + 2 * hf][0:FB, 0:H2N],
                             slice(H2N * hf, H2N * hf + H2N), hf + 7)
            dve.wait_ge(s["ug_hi"], 1)
            v.tensor_tensor(ug_w[0][:, 1, :], expert_raw[:, 0, 0:4 * HID], f(ug_w[0][:, 0, :]), ALU.subtract)\
                .then_inc(s["ug_lo"], 1)
            wide = [TOK, IMAGES, EXPERTS]
            dve.wait_ge(s["glt_ps"], 1)
            logits = v3(bank[1][0:TOK, 0:IMAGES * EXPERTS], EXPERTS)
            k = step(v.tensor_reduce(gmax[:, :], logits, AXX, ALU.max))
            after(k)
            v.tensor_tensor(gexp[:, :, :], logits, gmax[:, :].unsqueeze(2).to_broadcast(wide), ALU.subtract)\
                .then_inc(s["gd_done"], 1)
            dve.wait_ge(s["ge_done"], 1)
            k = step(v.tensor_reduce(gsum[:, :], gexp[:, :, :], AXX, ALU.add))
            after(k)
            k = step(v.reciprocal(grec[:, :], gsum[:, :]))
            after(k)
            k = step(v.tensor_tensor(score[:, :, :], gexp[:, :, :], grec[:, :].unsqueeze(2).to_broadcast(wide),
                                     ALU.mult))
            after(k)
            k = step(v.tensor_tensor(sbias[:, :, :], score[:, :, :],
                                     row("bias", 0, TOK).unsqueeze(1).to_broadcast(wide), ALU.add))
            after(k)
            pair = sbias[:, :, :].rearrange("p b (g e) -> p b g e", e=2)
            k = step(v.tensor_tensor(grp[:, :, 0:GROUPS], pair[:, :, :, 0], pair[:, :, :, 1], ALU.add))
            after(k)

            def best_four(values, top, picked, out, n):
                for b in range(IMAGES):
                    k = step(v.max(top[:, b, :], values[:, b, 0:n]))
                after(k)
                k = step(v.tensor_copy(picked[:, :, 0:TOPK], top[:, :, 0:TOPK]))
                after(k)
                for b in range(IMAGES):
                    k = step(v.match_replace(out=out[:, b, :], in_to_replace=picked[:, b, :],
                                             in_values=values[:, b, :], imm_value=GONE))
                after(k)

            best_four(grp, grp_top, grp_val, grp_out, GROUPS)
            k = step(v.tensor_tensor(grp_in[:, :, :], grp_out[:, :, 0:GROUPS], grp[:, :, 0:GROUPS],
                                     ALU.not_equal))
            after(k)
            step(v.tensor_scalar(grp_low[:, :, :], grp_in[:, :, :], 1.0, -GONE, ALU.subtract, ALU.mult))
            wide = [TOK, IMAGES, GROUPS, 2]
            k = step(v.tensor_tensor(smask[:, :, :].rearrange("p b (g e) -> p b g e", e=2), pair,
                                     grp_in[:, :, :].unsqueeze(3).to_broadcast(wide), ALU.mult))
            after(k)
            k = step(v.tensor_tensor(exq[:, :, 0:EXPERTS].rearrange("p b (g e) -> p b g e", e=2),
                                     smask[:, :, :].rearrange("p b (g e) -> p b g e", e=2),
                                     grp_low[:, :, :].unsqueeze(3).to_broadcast(wide), ALU.add))
            after(k)
            best_four(exq, exq_top, exq_val, exq_out, EXPERTS)
            k = step(v.tensor_tensor(exq_in[:, :, :], exq_out[:, :, 0:EXPERTS], exq[:, :, 0:EXPERTS],
                                     ALU.not_equal))
            after(k)
            v.scalar_tensor_tensor(wfull[:, :, :].rearrange("p b e -> p (b e)"),
                                   score[:, :, :].rearrange("p b e -> p (b e)"), ROUTE_SCALE,
                                   exq_in[:, :, :].rearrange("p b e -> p (b e)"), ALU.mult, ALU.mult)\
                .then_inc(s["wfull_done"], 1)

            def split_up(n, p):
                dve.wait_ge(s["ug_hi"], n + 1)
                v.tensor_tensor(ug_w[p][:, 1, :], expert_raw[:, p, 0:4 * HID], f(ug_w[p][:, 0, :]),
                                ALU.subtract).then_inc(s["ug_lo"], 1)

            def gate(n, hf, p):
                first = isinstance(n, int) and n == 0
                dve.wait_ge(s[f"silu{hf}"], n + 1)
                dve.wait_ge(s[f"g_ps{hf}"], n + 1)
                if not isinstance(n, int) or n > 1:
                    dve.wait_ge(s["weighed"], 2 * (n - 1))
                v.scalar_tensor_tensor((hid if first else gated)[hf][:, :], bank[4 + 2 * hf][:, 0:H2N],
                                       expert_raw[:, p, BG:BG + 1],
                                       silu[hf][:, :], ALU.add, ALU.mult).then_inc(s[f"gated{hf}"], 1)

            def weigh(n, hf):
                if isinstance(n, int) and n == 0:
                    return
                dve.wait_ge(s[f"gated{hf}"], n + 1)
                dve.wait_ge(s["wb_ps"], 2 * (n - 1) + hf + 1)
                dve.wait_ge(s["hid_hi"], 2 * (n - 1) + hf + 1)
                dve.wait_ge(s["hid_lo"], 2 * (n - 1) + hf + 1)
                v.tensor_tensor(hid[hf][:, :], bank[7][:, 0:H2N], gated[hf][:, :], ALU.mult)\
                    .then_inc(s["weighed"], 1)

            def hidden_lo(n, hf, p):
                dve.wait_ge(s["hid_hi"], 2 * n + hf + 1)
                tok = slice(H2N * hf, H2N * hf + H2N)
                v.tensor_tensor(hid_s[p][:, 1, tok], hid[hf][:, :], f(hid_s[p][:, 0, tok]), ALU.subtract)\
                    .then_inc(s["hid_lo"], 1)

            def expert(n, p, more=True):
                gate(n, 0, p)
                weigh(n, 0)
                dve.wait_ge(s["dn_hi"], n + 1)
                raw = expert_raw[:, p, DOWN0:DOWN0 + DIM]
                for part in "AB":
                    v.tensor_tensor(dn_w[p][:, DOWN_LO[part]], raw[:, DOWN_HI[part]],
                                    f(dn_w[p][:, DOWN_HI[part]]), ALU.subtract).then_inc(s["dn_lo"], 1)
                if more:
                    split_up(n + 1, 1 - p)
                gate(n, 1, p)
                hidden_lo(n, 0, p)
                weigh(n, 1)
                hidden_lo(n, 1, p)

            expert(0, 0)
            for hf in range(2):
                dve.wait_ge(s["wT_hi"], hf + 1)
                tok = slice(H2N * hf, H2N * hf + H2N)
                v.tensor_tensor(wT[32:32 + EXPERTS, tok], bank[7][0:EXPERTS, 0:H2N], f(wT[0:EXPERTS, tok]),
                                ALU.subtract).then_inc(s["wT_lo"], 1)
            expert(1, 1)
            with dve.Fori(0, 7) as it:
                expert(2 * it + 2, 0)
                expert(2 * it + 3, 1)
            expert(16, 0, more=False)
            dve.wait_ge(s["down_done"], 17)
            step(v.tensor_scalar(finA[:, 0:512], bank[0][:, :], col("sbdA", 128), None, ALU.add))
            dve.wait_ge(s["fin_moved"], 2)
            v.tensor_scalar(finA[:, 512:T2], bank[1][:, 0:256], col("sbdA", 128), None, ALU.add)\
                .then_inc(s["finA_done"], 1)
            step(v.scalar_tensor_tensor(finB[:, 0:512], bank[2][0:FB, 0:512], col("sbdB", FB),
                                        fin_tmp[:, 0:512], ALU.add, ALU.add))
            v.scalar_tensor_tensor(finB[:, 512:T2], bank[1][0:FB, 256:512], col("sbdB", FB),
                                   fin_tmp[:, 512:T2], ALU.add, ALU.add).then_inc(s["finB_done"], 1)


def constants():
    out = np.zeros((128, NCONST), np.float32)

    def put(name, a):
        out[:a.shape[0], CONST[name][0]:CONST[name][1]] = a

    put("ident", np.eye(128, dtype=np.float32))
    pos = np.arange(IMG_TOK, dtype=np.float32)[:, None]
    i = np.arange(DIM // 2, dtype=np.float32)[None, :]
    ang = pos / np.power(np.float32(10000.0), np.float32(2.0) * i / np.float32(DIM))
    pe = np.zeros((IMG_TOK, DIM), np.float32)
    pe[:, 0::2], pe[:, 1::2] = np.sin(ang), np.cos(ang)
    put("pe", np.concatenate([pe, pe]))
    key = np.arange(TOK)
    put("causal", np.where(key[None, :] > key[:, None], -10000.0, 0.0))
    put("tri", (key[:, None] <= key[None, :]).astype(np.float32))
    feat = np.arange(128)
    put("head", (feat[:CH, None] // HEAD == np.arange(CHH)[None, :]).astype(np.float32))
    put("parity", (feat[:, None] // HEAD % 2 == np.arange(2)[None, :]).astype(np.float32))
    put("block", (np.arange(SLOTS)[:, None] // PICKED == np.arange(IMAGES)[None, :]).astype(np.float32))
    put("iota", np.tile(np.arange(1, PICKED + 1, dtype=np.float32), (128, 1)))
    return out


def arrays_of(i):
    i = {k: np.asarray(v) for k, v in i.items()}

    def ab(w):
        return [w[:FA], np.concatenate([w[FA:], w[FA:]])]

    def tall(w, n=128):
        out = np.zeros((n,) + w.shape[1:], w.dtype)
        out[:len(w)] = w
        return out

    x = i["x"].reshape(IMAGES, CHANNELS, GRID, PATCH, GRID, PATCH).transpose(1, 3, 5, 0, 2, 4)
    x = x.reshape(PK, 128, 4, 128).transpose(2, 1, 0, 3)
    tok, at, fn = "L0_tok_", "L0_attn_", "L0_ffn_"
    out = {"patches": x}
    out["patch_w"] = i[tok + "patch_w"].reshape(DIM, PK, 128).transpose(2, 1, 0)
    out["const"] = constants()
    cols = np.zeros((128, NCOLS), np.float32)

    def put(name, a):
        cols[:a.shape[0], COLS[name][0]:COLS[name][1]] = a

    put("ff1_b", i[tok + "ff1_b"].reshape(FK, 128).T)
    put("ff2_bA", i[tok + "ff2_b"][:FA, None])
    put("ff2_bB", i[tok + "ff2_b"][FA:, None])
    put("q_b", i[tok + "qkv_b"][:DIM].reshape(2, CH).T)
    put("k_b", i[tok + "qkv_b"][DIM:2 * DIM].reshape(2, CH).T)
    put("aq_b", i[at + "Wqkv_b"][:DIM].reshape(2, CH).T)
    put("ak_b", i[at + "Wqkv_b"][DIM:2 * DIM].reshape(2, CH).T)
    put("gate_b", i[fn + "gate_b"][:, None])
    put("sbdA", i[fn + "sbd"][:FA, None])
    put("sbdB", i[fn + "sbd"][FA:, None])
    out["cols"] = cols
    out["rows"] = np.concatenate([
        i[tok + "patch_b"], i[tok + "ln_g"], i[tok + "ln_b"], i[tok + "qkv_b"][2 * DIM:], i[tok + "proj_b"],
        i[tok + "ff2_b"], i[at + "Wqkv_b"][2 * DIM:], i[at + "out_b"], i[at + "sel_b"], i[fn + "bias"],
        i[at + "temperature"]])[None]
    out["ff1"] = np.concatenate(ab(i[tok + "ff1_w"]), 1)
    out["ff2"] = i[tok + "ff2_w"].reshape(FK, 128, DIM).transpose(1, 0, 2)
    out["qkv"] = np.concatenate(ab(i[tok + "qkv_w"]), 1)
    pw = i[tok + "proj_w"].reshape(2, 3, 32, DIM).transpose(1, 0, 2, 3).reshape(DIM, DIM)
    out["proj"] = np.stack([pw[:FA], tall(pw[FA:])], 1)
    kv = np.concatenate([i[at + "Wqkv_w"][:, DIM:], i[at + "sel_w"]], 1)
    out["kv"] = np.concatenate(ab(kv), 1)
    aq = i[at + "Wqkv_w"][:, :DIM]
    out["aq"] = np.stack([aq[:FA], tall(aq[FA:])], 1)
    out["out_w"] = i[at + "out_w"].reshape(2, CH, DIM).transpose(1, 0, 2)
    out["gate"] = np.concatenate(ab(i[fn + "gate_w"]), 1)
    bd = np.zeros((48, DIM), np.float32)
    bd[:EXPERTS], bd[32:] = i[fn + "bd"], i[fn + "bd"]
    out["bd"] = bd
    out["txt"] = i["txt"].transpose(1, 0, 2)
    wu = np.concatenate([i[fn + "sWu"][None], i[fn + "Wu"]])
    wg = np.concatenate([i[fn + "sWg"][None], i[fn + "Wg"]])
    wd = np.concatenate([i[fn + "sWd"][None], i[fn + "Wd"]])
    twice = [np.concatenate([w[:, FA:], w[:, FA:]], 1) for w in (wu, wg)]
    bu = np.concatenate([i[fn + "sbu"][None], i[fn + "bu"]])[:, :, None]
    bg = np.concatenate([i[fn + "sbg"][None], i[fn + "bg"]])[:, :, None]
    out["experts"] = np.concatenate([wu[:, :FA], wg[:, :FA], *twice, wd, bu, bg], 2)
    return {k: np.ascontiguousarray(v) for k, v in out.items()}


def kernel(**inputs):
    import concourse.bacc as _bacc
    from concourse.bass_utils import run_bass_kernel_spmd as _run

    nc = _bacc.Bacc("TRN2", target_bir_lowering=False, num_devices=1)
    arrays = arrays_of(inputs)
    args = {k: nc.dram_tensor("in_" + k, a.shape, mybir.dt.from_np(a.dtype), kind="ExternalInput").ap()
            for k, a in arrays.items()}
    args["out"] = nc.dram_tensor("out", (DIM, T2), F32, kind="ExternalOutput").ap()
    build(nc, args)
    r = _run(nc, [{"in_" + k: a for k, a in arrays.items()}], core_ids=[0])
    return np.ascontiguousarray(r.results[0]["out"].T.reshape(IMAGES, TOK, DIM))
```

```python
from contextlib import ExitStack

import numpy as np

import concourse.bass as bass
from concourse import mybir

F32 = mybir.dt.float32
F32R = mybir.dt.float32r
ALU = mybir.AluOpType
ACT = mybir.ActivationFunctionType
AXX = mybir.AxisListType.X

IMAGES, CHANNELS, SIDE, PATCH = 8, 3, 128, 16
GRID = SIDE // PATCH
IMG_TOK = GRID * GRID
TXT_TOK = 32
TOK = IMG_TOK + TXT_TOK
DIM, HEADS, HEAD = 192, 12, 16
FF = 768
EXPERTS, GROUPS, TOPK, HID, ROUTE_SCALE = 16, 8, 4, 128, 2.5
PICKED = 10
EPS = 1e-5
FA, FB = 128, 64
HALF_IMG = IMAGES // 2
T1, H1 = IMAGES * IMG_TOK, HALF_IMG * IMG_TOK
T2, H2N = IMAGES * TOK, HALF_IMG * TOK
PK = CHANNELS * PATCH * PATCH // 128
FK = FF // 128
CH = 96
CHH = CH // HEAD
SLOTS = IMAGES * PICKED
QROWS = HEADS * PICKED
WPACK = 4 * HID + DIM + 2
DOWN0, BU, BG = 4 * HID, 4 * HID + DIM, 4 * HID + DIM + 1
LOW, GONE = -3.3e38, -3.0e38
DOWN_HI, DOWN_LO = {"A": slice(0, FA), "B": slice(FA, DIM)}, {"A": slice(DIM + FB, 2 * DIM), "B": slice(DIM, DIM + FB)}
B_BOTH = slice(FA, FA + 2 * FB)
VSEL = DIM + 2


FILL = {
    "patches": 7, "turn_x0": 1, "hidden0": 12, "turn_x1": 0, "hidden1": 7, "ff_out0": 0, "ff_out1": 0,
    "qkv0": 0, "scores0": 3, "qkv1": 0, "scores1": 0, "scores2": 0, "prob0": 0, "scores3": 1, "prob1":
    1, "values0": 0, "scores4": 0, "prob2": 0, "values1": 0, "scores5": 0, "values2": 0, "prob3": 0,
    "project0": 3, "values3": 0, "prob4": 0, "turn_x2": 0, "prob5": 0, "values5": 4, "hidden2": 0,
    "project1": 0, "turn_x3": 3, "ff_out2": 0, "hidden3": 0, "turn_h0": 11, "ff_out3": 0, "vk0": 0,
    "turn_h1": 3, "vk1": 8, "psel": 4, "pickT": 2, "pick": 2, "hot": 3, "xs": 2, "aq": 0, "as0": 0,
    "ap0": 0, "ap1": 0, "ac": 5, "ao": 3, "xn2_0": 12, "xn2_1": 3, "gl": 1, "glt0": 2, "glt1": 3, "ug1":
    0, "wfull": 0}


def layout(parts):
    at, out = 0, {}
    for name, width in parts:
        out[name] = (at, at + width)
        at += width
    return out, at


CONST, NCONST = layout([("ident", 128), ("pe", DIM), ("causal", TOK), ("tri", TOK), ("head", CHH),
                        ("parity", 2), ("block", IMAGES), ("iota", PICKED)])
COLS, NCOLS = layout([("ff1_b", FK), ("ff2_bA", 1), ("ff2_bB", 1), ("q_b", 2), ("k_b", 2), ("aq_b", 2),
                      ("ak_b", 2), ("gate_b", 1), ("sel_b", 1), ("sbdA", 1), ("sbdB", 1)])
ROWS, NROWS = layout([("patch_b", DIM), ("ln_g", DIM), ("ln_b", DIM), ("v_b", DIM), ("proj_b", DIM),
                      ("ff2_b", DIM), ("av_b", DIM), ("out_b", DIM), ("bias", EXPERTS),
                      ("temp", 1)])
ROWS_FIRST = ROWS["v_b"][0]


def build(nc, d):
    with ExitStack() as ctx:
        def sb(name, shape, dt=F32):
            return ctx.enter_context(nc.sbuf_tensor(name, shape, dt))

        def sem(name):
            return ctx.enter_context(nc.semaphore(name))

        bank = [ctx.enter_context(nc.psum_tensor(f"bank{i}", [128, 512], F32)) for i in range(8)]

        h2_bank = [bank[i] for i in (3, 6, 0, 1)]
        ctx_bank = [bank[2], bank[4]]

        const = sb("const", [128, NCONST])
        cols = sb("cols", [128, NCOLS])
        rows = sb("rows", [128, NROWS])
        ff2_raw = sb("ff2_raw", [128, FK, DIM])
        proj_w = sb("proj_w", [128, 2, DIM])
        kv_raw = sb("kv_raw", [128, 2 * (DIM + VSEL)])
        aq_w = sb("aq_w", [128, 2, DIM])
        out_w = sb("out_w", [CH, 2, DIM])
        gate_raw = sb("gate_raw", [128, 2 * EXPERTS])
        bd_raw = sb("bd_raw", [48, DIM])
        expert_raw = sb("expert_raw", [128, 2, WPACK])
        kv_w = sb("kv_w", [128, 2, 2 * (DIM + VSEL)], F32R)
        gate_w = sb("gate_w", [128, 2, 2 * EXPERTS], F32R)
        bd_w = sb("bd_w", [48, 2, DIM], F32R)
        minus_half = sb("minus_half", [128, 4])
        filler = sb("filler", [128, 512], mybir.dt.bfloat16)
        table = sb("table", [1, 8])
        x1 = sb("x1", [128, 4, DIM])
        x1b = sb("x1b", [128, 4, DIM])
        tA = sb("tA", [128, 2, T2], F32R)
        tB = sb("tB", [128, T2], F32R)
        act1 = sb("act1", [128, 2, FK, H1])
        v_blk = sb("v_blk", [128, IMAGES, 3, 64])
        h = sb("h", [TOK, IMAGES, DIM])
        st2 = sb("st2", [TOK, IMAGES, 6])
        mv2 = sb("mv2", [TOK, IMAGES, 2])
        ve2 = sb("ve2", [TOK, IMAGES])
        rs2 = sb("rs2", [TOK, IMAGES])
        xn = sb("xn", [TOK, IMAGES, DIM])
        pT = sb("pT", [IMAGES, TOK + 8])
        last2 = sb("last2", [IMAGES, 8])
        aq_blk = sb("aq_blk", [CH, 2, IMAGES, QROWS])
        h2 = sb("h2", [TOK, IMAGES, 256])
        grp = sb("grp", [TOK, IMAGES, GROUPS + 4])
        grp_val = sb("grp_val", [TOK, IMAGES, 8])
        exq = sb("exq", [TOK, IMAGES, EXPERTS + 4])
        exq_val = sb("exq_val", [TOK, IMAGES, 8])
        wT = sb("wT", [128, T2], F32R)
        sel = sb("sel", [128, 1])
        ones = sb("ones", [128, 128])
        sel_w = sb("sel_w", [128, 128], F32R)

        first_life = ExitStack()

        def sb1(name, shape, dt=F32):
            return first_life.enter_context(nc.sbuf_tensor(name, shape, dt))

        ff1_w = sb1("ff1_w", [128, 2, 2 * FF], F32R)
        qkv_w = sb1("qkv_w", [128, 2, 2 * 3 * DIM], F32R)
        x = sb1("x", [128, 4, DIM])
        xpb = sb1("xpb", [128, 4, DIM])
        yA = sb1("yA", [128, 2, T1], F32R)
        yB = sb1("yB", [128, T1], F32R)
        ytmp = sb1("ytmp", [FB, T1])
        ybf = sb1("ybf", [FB, T1])
        bqm = sb1("bqm", [CH, 2, 2])
        smax = sb1("smax", [128, 2, 3, 8])
        ssum = sb1("ssum", [128, 2, 3, 8])
        srec = sb1("srec", [128, 2, 3, 8])

        with ExitStack() as early:
            def sb0(name, shape, dt=F32):
                return early.enter_context(nc.sbuf_tensor(name, shape, dt))

            patches = sb0("patches", [128, 4, PK, 128])
            patch_w = sb0("patch_w", [128, PK, DIM])
            ff1_raw = sb0("ff1_raw", [128, 2 * FF])
            qkv_raw = sb0("qkv_raw", [128, 2 * 3 * DIM])
            x0 = sb0("x0", [128, 4, DIM])
            st1 = sb0("st1", [128, 4, 6])
            mv1 = sb0("mv1", [128, 4, 2])
            ve1 = sb0("ve1", [128, 4])
            rs1 = sb0("rs1", [128, 4])
            bpe = sb0("bpe", [128, DIM])
            ff2_w = sb0("ff2_w", [128, FK, 2 * DIM], F32R)
            act1s = sb0("act1s", [128, 2, 2, FK, H1], F32R)

        q_blk = sb1("q_blk", [CH, 2, IMAGES, 2, IMG_TOK])
        kT = sb1("kT", [CH, 2, T1])
        prob = sb1("prob", [128, 2, 3, 512])
        probT = sb1("probT", [128, 2, 3, 512])
        otmp = sb1("otmp", [64, 2, 3, H1])
        o01 = sb1("o01", [128, T1])
        o2 = sb1("o2", [64, T1])

        first_life.close()

        ug_w = [sb(f"ug_w{p}", [128, 2, 4 * HID], F32R) for p in range(2)]
        dn_w = [sb(f"dn_w{p}", [128, 2 * DIM], F32R) for p in range(2)]
        xn2 = sb("xn2", [TOK, IMAGES, DIM])
        st3 = sb("st3", [TOK, IMAGES, 6])
        mv3 = sb("mv3", [TOK, IMAGES, 2])
        ve3 = sb("ve3", [TOK, IMAGES])
        rs3 = sb("rs3", [TOK, IMAGES])
        glT = sb("glT", [EXPERTS, T2])
        gmax = sb("gmax", [TOK, IMAGES])
        gexp = sb("gexp", [TOK, IMAGES, EXPERTS])
        gsum = sb("gsum", [TOK, IMAGES])
        grec = sb("grec", [TOK, IMAGES])
        score = sb("score", [TOK, IMAGES, EXPERTS])
        sbias = sb("sbias", [TOK, IMAGES, EXPERTS])
        grp_top = sb("grp_top", [TOK, IMAGES, 8])
        grp_out = sb("grp_out", [TOK, IMAGES, GROUPS + 4])
        grp_in = sb("grp_in", [TOK, IMAGES, GROUPS])
        grp_low = sb("grp_low", [TOK, IMAGES, GROUPS])
        smask = sb("smask", [TOK, IMAGES, EXPERTS])
        exq_top = sb("exq_top", [TOK, IMAGES, 8])
        exq_out = sb("exq_out", [TOK, IMAGES, EXPERTS + 4])
        exq_in = sb("exq_in", [TOK, IMAGES, EXPERTS])
        wfull = sb("wfull", [TOK, IMAGES, EXPERTS])
        silu = [sb(f"silu{i}", [128, H2N]) for i in range(2)]
        gated = [sb(f"gated{i}", [128, H2N]) for i in range(2)]
        hid = [sb(f"hid{i}", [128, H2N]) for i in range(2)]
        hid_s = [sb(f"hid_s{p}", [128, 2, T2], F32R) for p in range(2)]
        fin_tmp = sb("fin_tmp", [FB, T2])
        finA = sb("finA", [FA, T2])
        finB = sb("finB", [FB, T2])

        with ExitStack() as second_life:
            def sb2(name, shape, dt=F32):
                return second_life.enter_context(nc.sbuf_tensor(name, shape, dt))

            hx = sb2("hx", [TOK, IMAGES, DIM])
            akT = sb2("akT", [CH, 2, T2])
            av = sb2("av", [TOK, IMAGES, DIM])
            itemp = sb2("itemp", [TOK, 1])
            lgT = sb2("lgT", [2, T2])
            lgt = sb2("lgt", [TOK, IMAGES, 2])
            lmax = sb2("lmax", [TOK, IMAGES])
            ld = sb2("ld", [TOK, IMAGES, 2])
            le = sb2("le", [TOK, IMAGES, 2])
            lsum = sb2("lsum", [TOK, IMAGES])
            lrec = sb2("lrec", [TOK, IMAGES])
            psel = sb2("psel", [TOK, IMAGES])
            pT8 = sb2("pT8", [IMAGES, TOK + 8])
            pT10 = sb2("pT10", [IMAGES, TOK + 8])
            top8 = sb2("top8", [IMAGES, 8])
            next8 = sb2("next8", [IMAGES, 8])
            pickT = sb2("pickT", [IMAGES, TOK])
            pick = sb2("pick", [TOK, IMAGES])
            rank = sb2("rank", [TOK, IMAGES])
            hot = sb2("hot", [TOK, IMAGES, PICKED])
            hot_heads = sb2("hot_heads", [TOK, IMAGES, QROWS])
            hotp = sb2("hotp", [TOK, IMAGES, PICKED])
            hotpT = sb2("hotpT", [SLOTS, IMAGES, TOK])
            xsA = sb2("xsA", [FA, SLOTS])
            xsB = sb2("xsB", [FB, SLOTS])
            aq = sb2("aq", [CH, 2, SLOTS])
            aprob = sb2("aprob", [QROWS, 2, H2N])
            amax = sb2("amax", [QROWS, IMAGES])
            asum = sb2("asum", [QROWS, IMAGES])
            arec = sb2("arec", [QROWS, IMAGES])
            aprobT = sb2("aprobT", [TOK, 2, HALF_IMG * QROWS])
            actx = sb2("actx", [CH, 2, 2 * HALF_IMG, 60])
            ctxT = sb2("ctxT", [CH, 2, 2, HALF_IMG * PICKED])
            arow = sb2("arow", [SLOTS, DIM])

        w_flat = sb("w_flat", [EXPERTS, T2])
        w_all = [sb(f"w_all{p}", [128, T2]) for p in range(2)]

        def f(ap):
            return ap.bitcast(F32)

        def c(name, n=128, i=None):
            a, b = CONST[name]
            return const[0:n, a:b]

        def col(name, n, i=0):
            a = COLS[name][0] + i
            return cols[0:n, a:a + 1]

        def row(name, p0, p1):
            a, b = ROWS[name]
            return rows[p0:p1, a:b]

        def v3(ap, n):
            return ap.rearrange("p (a b) -> p a b", b=n)

        d_pw = [sem(f"d_patch_w{i}") for i in range(2)]
        d_patch0 = [sem(f"d_patch0_{i}") for i in range(2)]
        d_patch = [None] + [sem(f"d_patch{i}") for i in range(1, 4)]
        (d_const, d_cols, d_rows, d_ff1, d_ff2, d_qkv, d_proj, d_kv, d_aq,
         d_txt, d_out, d_rows2) = [sem("d_" + n) for n in (
             "const", "cols", "rows", "ff1", "ff2", "qkv", "proj", "kv", "aq", "txt", "out", "rows_rest")]
        d_ug = [sem(f"d_up{p}") for p in range(2)]
        d_dn = [sem(f"d_down{p}") for p in range(2)]
        d_w_all = [sem(f"d_w_all{p}") for p in range(2)]

        s = {n: sem(n) for n in (
            "patch_ps", "mv1_done", "rs1_done", "x_done", "xpb_done", "xT_ps", "t_hi", "t_lo", "ff1_hi", "ff1_lo",
            "ff1_lo_last", "ff2_hi", "ff2_lo", "qkv_hi", "qkv_lo", "hid1_ps",
            "gelu_done", "act1_lo", "y_ps", "yA_hi", "yB_moved", "yB_sum", "yB_hi", "y_lo",
            "q_ps", "k_ps", "bqm_done", "q_done", "k_done", "v_ps", "v_done", "s_ps", "s_sub",
            "s_exp", "s_norm", "s_rec", "pT_ps", "pT_done", "o_ps", "o_even", "o_done", "proj_ps", "x1_done",
            "x1b_done", "hid2_ps", "gelu2_done", "ff2_ps", "zeros_done", "filler_done",
            "mv2_done", "rs2_done", "xn_done", "hx_done", "hT_ps", "small_split", "lg_ps", "lg_read", "av_ps",
            "av_done", "ak_ps",
            "ak_even", "ak_odd", "ld_done", "le_done", "psel_done", "psT_ps", "pickT_done", "pick_ps",
            "pick_done", "cum_ps", "hot_done", "hot_spread", "xs_ps", "xs_done", "aq_ps", "aq_done", "hotpT_ps",
            "hotpT_done", "as_ps", "as_sub", "as_exp", "as_norm", "apT_ps", "apT_done", "ac_ps", "ac_done",
            "ao_ps", "ao_done", "h2_ps", "h2_done", "h2_read",
            "mv3_done", "rs3_done", "xn2_done", "h2T_ps", "gl_ps", "gl_done", "glt_ps", "gd_done", "lgT_done",
            "lgT_ps", "first_lo",
            "sel_done", "w_flat_done", "sum_done", "ge_done", "wfull_done", "wT_ps", "wT_hi", "wT_lo",
            "ug_hi", "ug_lo", "dn_hi", "dn_lo", "u_ps0", "u_ps1", "g_ps0", "g_ps1", "silu0", "silu1",
            "gated0", "gated1", "wb_ps", "weighed", "hid_hi", "hid_lo", "down_done", "fin_moved", "finA_done",
            "finB_done", "gp_step", "vec_step")}

        def chain(eng, signal):
            count = [0]

            def step(ins):
                count[0] += 1
                ins.then_inc(s[signal], 1)
                return count[0]

            def after(k):
                eng.wait_ge(s[signal], k)
            return step, after

        w_dram = nc.dram_tensor("routing_weights", (EXPERTS, T2), F32, kind="Internal").ap()
        block = ctx.enter_context(nc.Block())

        @block.sync
        def _(sp):
            first = PK // 2
            for k, part in enumerate((slice(0, first), slice(first, PK))):
                sp.dma_start(patch_w[:, part, :], d["patch_w"][:, part, :]).then_inc(d_pw[k], 16)
                sp.dma_start(patches[:, 0, part], d["patches"][0][:, part]).then_inc(d_patch0[k], 16)
            sp.dma_start(patches[:, 1], d["patches"][1]).then_inc(d_patch[1], 16)
            sp.dma_start(rows[:, 0:ROWS_FIRST], d["rows"][:, 0:ROWS_FIRST].to_broadcast([128, ROWS_FIRST]))\
                .then_inc(d_rows, 16)
            sp.dma_start(patches[:, 2], d["patches"][2]).then_inc(d_patch[2], 16)
            sp.dma_start(const[:, :], d["const"]).then_inc(d_const, 16)
            sp.dma_start(patches[:, 3], d["patches"][3]).then_inc(d_patch[3], 16)
            sp.dma_start(ff1_raw[:, :], d["ff1"]).then_inc(d_ff1, 16)
            sp.dma_start(cols[:, :], d["cols"]).then_inc(d_cols, 16)
            sp.dma_start(ff2_raw[:, :, :], d["ff2"]).then_inc(d_ff2, 16)
            sp.dma_start(qkv_raw[:, :], d["qkv"]).then_inc(d_qkv, 16)
            sp.dma_start(rows[:, ROWS_FIRST:], d["rows"][:, ROWS_FIRST:].to_broadcast([128, NROWS - ROWS_FIRST]))\
                .then_inc(d_rows2, 16)
            sp.dma_start(proj_w[:, :, :], d["proj"]).then_inc(d_proj, 16)
            sp.dma_start(kv_raw[:, :], d["kv"]).then_inc(d_kv, 16)
            sp.dma_start(h[IMG_TOK:TOK, :, :], d["txt"]).then_inc(d_txt, 16)
            sp.dma_start(aq_w[:, :, :], d["aq"]).then_inc(d_aq, 16)
            sp.dma_start(out_w[:, :, :], d["out_w"]).then_inc(d_aq, 16)
            sp.dma_start(gate_raw[:, :], d["gate"]).then_inc(d_kv, 16)
            sp.dma_start(bd_raw[:, :], d["bd"]).then_inc(d_kv, 16)
            for n in range(2):
                sp.dma_start(expert_raw[:, n, 0:DOWN0], d["experts"][n][:, 0:DOWN0]).then_inc(d_ug[n], 16)
                sp.dma_start(expert_raw[:, n, DOWN0:], d["experts"][n][:, DOWN0:]).then_inc(d_dn[n], 16)
            def source(n, columns):
                if isinstance(n, int):
                    return d["experts"][n][:, columns]
                return d["experts"][bass.ds(n, 1), :, columns]

            def load_up(n, p):
                src = source(n, slice(0, DOWN0))
                if isinstance(n, int) and n < 4:
                    sp.wait_ge(s["first_lo"], n - 1)
                else:
                    sp.wait_ge(s["ug_lo"], n - 3)
                sp.dma_start(expert_raw[:, p, 0:DOWN0], src).then_inc(d_ug[p], 16)

            def load_down(n, p):
                src = source(n, slice(DOWN0, WPACK))
                if isinstance(n, int) and n == 2:
                    sp.wait_ge(s["dn_lo"], 2)
                sp.wait_ge(s["gated1"], n - 1)
                sp.dma_start(expert_raw[:, p, DOWN0:WPACK], src).then_inc(d_dn[p], 16)

            def load_weights(n, p):
                if isinstance(n, int):
                    src = w_dram[n - 1:n, :]
                else:
                    src = w_dram[bass.ds(n - 1, 1), :]
                if not isinstance(n, int) or n > 3:
                    sp.wait_ge(s["weighed"], 2 * (n - 2))
                sp.dma_start(w_all[p][:, :], src.to_broadcast([128, T2])).then_inc(d_w_all[p], 16)

            load_up(2, 0)
            sp.wait_ge(s["w_flat_done"], 2)
            sp.dma_start(w_dram, w_flat[:, :]).then_inc(d_out, 16)
            sp.wait_ge(d_out, 16)
            load_weights(2, 0)
            load_weights(3, 1)
            load_down(2, 0)
            load_up(3, 1)
            load_down(3, 1)
            with sp.Fori(0, 6) as it:
                load_up(2 * it + 4, 0)
                load_down(2 * it + 4, 0)
                load_weights(2 * it + 4, 0)
                load_up(2 * it + 5, 1)
                load_down(2 * it + 5, 1)
                load_weights(2 * it + 5, 1)
            load_up(16, 0)
            load_down(16, 0)
            load_weights(16, 0)
            sp.wait_ge(s["finA_done"], 1)
            sp.dma_start(d["out"][0:FA, 0:512], finA[:, 0:512]).then_inc(d_out, 16)
            sp.wait_ge(s["finB_done"], 1)
            sp.dma_start(d["out"][FA:DIM, 0:512], finB[:, 0:512]).then_inc(d_out, 16)
            sp.wait_ge(s["fin_moved"], 3)
            sp.dma_start(d["out"][0:FA, 512:T2], finA[:, 512:T2]).then_inc(d_out, 16)
            sp.wait_ge(s["finB_done"], 2)
            sp.dma_start(d["out"][FA:DIM, 512:T2], finB[:, 512:T2]).then_inc(d_out, 16)
            sp.wait_ge(d_out, 80)

        @block.gpsimd
        def _(gp):
            g = nc.gpsimd
            step, after = chain(gp, "gp_step")
            g.memset(filler[:, :], 1.0).then_inc(s["filler_done"], 1)
            g.memset(table[:, :], 0.0).then_inc(s["filler_done"], 1)
            g.memset(ones[:, :], 1.0).then_inc(s["filler_done"], 1)
            step(g.memset(minus_half[:, :], -0.5))
            g.memset(v_blk[:, :, :, :], 0.0).then_inc(s["zeros_done"], 1)
            g.memset(aq_blk[:, :, :, :], 0.0).then_inc(s["zeros_done"], 1)
            g.memset(h2[:, :, DIM:256], 0.0).then_inc(s["zeros_done"], 1)
            g.memset(f(bd_w[:, :, :]), 0.0).then_inc(s["zeros_done"], 1)
            g.memset(f(wT[:, :]), 0.0).then_inc(s["zeros_done"], 1)
            g.memset(pT[:, TOK:TOK + 8], LOW).then_inc(s["zeros_done"], 1)
            g.memset(last2[:, 2:8], LOW).then_inc(s["zeros_done"], 1)
            g.memset(grp[:, :, GROUPS:GROUPS + 4], LOW).then_inc(s["zeros_done"], 1)
            g.memset(grp_val[:, :, 4:8], LOW).then_inc(s["zeros_done"], 1)
            g.memset(exq[:, :, EXPERTS:EXPERTS + 4], LOW).then_inc(s["zeros_done"], 1)
            g.memset(exq_val[:, :, 4:8], LOW).then_inc(s["zeros_done"], 1)

            def rsqrt(ve, mv, rs, lo, hi, n, done):
                k = step(g.tensor_scalar(ve[:, lo:hi], mv[:, lo:hi, 1], EPS, 1.0, ALU.add, ALU.mult))
                after(k)
                g.tensor_tensor(rs[:, lo:hi], ve[:, lo:hi], minus_half[0:n, 0:hi - lo], ALU.pow)\
                    .then_inc(s[done], 1)

            for hf in range(2):
                gp.wait_ge(s["mv1_done"], 2 * hf + 2)
                rsqrt(ve1, mv1, rs1, 2 * hf, 2 * hf + 2, 128, "rs1_done")
                if hf == 0:
                    gp.wait_ge(s["ff1_hi"], 1)
                    g.tensor_tensor(v3(ff1_w[:, 1, :], FF)[:, :, FF // 2:], v3(ff1_raw[:, :], FF)[:, :, FF // 2:],
                                    v3(f(ff1_w[:, 0, :]), FF)[:, :, FF // 2:], ALU.subtract)\
                        .then_inc(s["ff1_lo_last"], 1)
            gp.wait_ge(s["ff2_hi"], 1)
            for part in "AB":
                g.tensor_tensor(ff2_w[:, :, DOWN_LO[part]], ff2_raw[:, :, DOWN_HI[part]],
                                f(ff2_w[:, :, DOWN_HI[part]]), ALU.subtract).then_inc(s["ff2_lo"], 1)
            gp.wait_ge(s["qkv_hi"], 1)
            g.tensor_tensor(qkv_w[:, 1, :], qkv_raw[:, :], f(qkv_w[:, 0, :]), ALU.subtract)\
                .then_inc(s["qkv_lo"], 1)
            gp.wait_ge(d_rows2, 16)
            for hf in range(2):
                gp.wait_ge(s["x_done"], hf + 1)
                t = slice(2 * hf, 2 * hf + 2)
                g.tensor_tensor(xpb[:, t, :], x[:, t, :],
                                row("proj_b", 0, 128).unsqueeze(1).to_broadcast([128, 2, DIM]), ALU.add)\
                    .then_inc(s["xpb_done"], 1)
            gp.wait_ge(d_kv, 48)
            k = step(g.tensor_scalar(kv_w[:, 0, :], kv_raw[:, :], 1.0, 1.0, ALU.mult, ALU.mult))
            after(k)
            g.tensor_tensor(kv_w[:, 1, :], kv_raw[:, :], f(kv_w[:, 0, :]), ALU.subtract)\
                .then_inc(s["small_split"], 1)
            k = step(g.tensor_scalar(gate_w[:, 0, :], gate_raw[:, :], 1.0, 1.0, ALU.mult, ALU.mult))
            after(k)
            g.tensor_tensor(gate_w[:, 1, :], gate_raw[:, :], f(gate_w[:, 0, :]), ALU.subtract)\
                .then_inc(s["small_split"], 1)
            gp.wait_ge(s["zeros_done"], 11)
            for p0 in (0, 32):
                k = step(g.tensor_scalar(bd_w[p0:p0 + EXPERTS, 0, :], bd_raw[p0:p0 + EXPERTS, :], 1.0, 1.0,
                                         ALU.mult, ALU.mult))
                after(k)
            g.tensor_tensor(bd_w[0:EXPERTS, 1, :], bd_raw[0:EXPERTS, :], f(bd_w[0:EXPERTS, 0, :]),
                            ALU.subtract).then_inc(s["small_split"], 1)
            gp.wait_ge(d_const, 16)
            k = step(g.tensor_tensor(sel[:, :], c("ident")[:, 0:1], c("ident")[:, 32:33], ALU.add))
            after(k)
            g.tensor_scalar(sel_w[:, :], ones[:, :], sel[:, 0:1], None, ALU.mult).then_inc(s["sel_done"], 1)
            for i in range(6):
                gp.wait_ge(s["s_rec"], i + 1)
                hf, j = i // 3, i % 3
                wide = [128, 8, IMG_TOK]
                g.tensor_tensor(v3(prob[:, hf, j, :], IMG_TOK), v3(prob[:, hf, j, :], IMG_TOK),
                                srec[:, hf, j, :].unsqueeze(2).to_broadcast(wide), ALU.mult)\
                    .then_inc(s["s_norm"], 1)
            for hf in range(2):
                gp.wait_ge(s["x1_done"], hf + 1)
                t = slice(2 * hf, 2 * hf + 2)
                g.tensor_tensor(x1b[:, t, :], x1[:, t, :],
                                row("ff2_b", 0, 128).unsqueeze(1).to_broadcast([128, 2, DIM]), ALU.add)\
                    .then_inc(s["x1b_done"], 1)
            for hf in range(2):
                gp.wait_ge(s["mv2_done"], hf + 1)
                rsqrt(ve2, mv2, rs2, 4 * hf, 4 * hf + 4, TOK, "rs2_done")
            for hf in range(2):
                gp.wait_ge(s["xn_done"], hf + 1)
                b = slice(4 * hf, 4 * hf + 4)
                g.tensor_tensor(hx[:, b, :], h[:, b, :], xn[:, b, :], ALU.add).then_inc(s["hx_done"], 1)
            for n in range(2):
                gp.wait_ge(s["ug_hi"], n + 1)
                g.tensor_tensor(ug_w[n][:, 1, :], expert_raw[:, n, 0:DOWN0], f(ug_w[n][:, 0, :]), ALU.subtract)\
                    .then_inc(s["first_lo"], 1)
            for hf in range(2):
                gp.wait_ge(s["mv3_done"], hf + 1)
                rsqrt(ve3, mv3, rs3, 4 * hf, 4 * hf + 4, TOK, "rs3_done")
            for hf in range(2):
                gp.wait_ge(s["w_flat_done"], hf + 1)
                tok = slice(H2N * hf, H2N * hf + H2N)
                g.tensor_tensor(wT[32:32 + EXPERTS, tok], w_flat[:, tok], f(wT[0:EXPERTS, tok]),
                                ALU.subtract).then_inc(s["wT_lo"], 1)

        @block.tensor
        def _(pe):
            mm, tr = nc.tensor.matmul, nc.tensor.transpose

            def five(out, wA, wAl, wB, wBl, aA, aAl, aB, aBh, start=True):
                mm(out, wA, aA, start=start, stop=False)
                mm(out, wAl, aA, start=False, stop=False)
                mm(out, wA, aAl, start=False, stop=False)
                mm(out, wBl, aBh, start=False, stop=False)
                return mm(out, wB, aB, start=False, stop=True)

            def w_still(out, w, a0, b0, n, tok, lay=(tA, tB)):
                A, B = lay
                return five(out, w[:, 0, a0:a0 + n], w[:, 1, a0:a0 + n], w[:, 0, b0:b0 + n],
                            w[0:FB, 1, b0:b0 + n], A[:, 0, tok], A[:, 1, tok], B[:, tok], B[0:FB, tok])

            def x_still(out, w, a0, b0, n, tok, lay=(tA, tB)):
                A, B = lay
                mm(out, A[:, 0, tok], w[:, 0, a0:a0 + n], start=True, stop=False)
                mm(out, A[:, 0, tok], w[:, 1, a0:a0 + n], start=False, stop=False)
                mm(out, A[:, 1, tok], w[:, 0, a0:a0 + n], start=False, stop=False)
                mm(out, B[0:FB, tok], w[0:FB, 1, b0:b0 + n], start=False, stop=False)
                return mm(out, B[:, tok], w[:, 0, b0:b0 + n], start=False, stop=True)

            def keep_busy(site, out):
                for k in range(FILL[site]):
                    mm(out[:, :], filler[:, 0:128], filler[:, :], start=True, stop=True)

            def patch(t):
                if t:
                    pe.wait_ge(d_patch[t], 16)
                for k in range(PK):
                    if t == 0 and k % (PK // 2) == 0:
                        pe.wait_ge(d_pw[k // (PK // 2)], 16)
                        pe.wait_ge(d_patch0[k // (PK // 2)], 16)
                    last = mm(bank[4 * (t // 2) + t % 2][:, 0:DIM], patches[:, t, k, :], patch_w[:, k, :],
                              start=(k == 0), stop=(k == PK - 1))
                last.then_inc(s["patch_ps"], 1)

            def turn_x(src, hf, made, atA, atB):
                pe.wait_ge(s[made], hf + 1)
                for i in range(2):
                    t = 2 * hf + i
                    tr(atA[:, 128 * i:128 * i + 128], src[:, t, 0:FA], c("ident"))
                    last = tr(atB[0:FB, 128 * i:128 * i + 128], src[:, t, FA:DIM], c("ident"))
                last.then_inc(s["xT_ps"], 1)

            def hidden(hf, turned, banks, read, done):
                pe.wait_ge(s["t_hi"], 2 * (turned))
                pe.wait_ge(s["t_lo"], 2 * (turned))
                for m in range(FK):
                    if m == 3:
                        pe.wait_ge(s["ff1_lo_last"], 1)
                    if m >= 3:
                        pe.wait_ge(s[read], FK * hf + m - 2)
                    w_still(bank[4 * hf + banks[m % 3]][:, 0:H1], ff1_w, 128 * m, FF + 128 * m, 128,
                            slice(H1 * hf, H1 * hf + H1)).then_inc(s[done], 1)

            def ff_out(hf):
                outA, outB = bank[4 * hf][:, 0:H1], bank[4 * hf][:, H1:2 * H1]
                for k in range(FK):
                    pe.wait_ge(s["act1_lo"], FK * hf + k + 1)
                    hi, lo = act1s[:, hf, 0, k, :], act1s[:, hf, 1, k, :]
                    mm(outA, ff2_w[:, k, DOWN_HI["A"]], hi, start=(k == 0), stop=False)
                    mm(outA, ff2_w[:, k, DOWN_LO["A"]], hi, start=False, stop=False)
                    mm(outA, ff2_w[:, k, DOWN_HI["A"]], lo, start=False, stop=(k == FK - 1))
                for k in range(FK):
                    hi, lo = act1s[:, hf, 0, k, :], act1s[:, hf, 1, k, :]
                    mm(outB, ff2_w[:, k, B_BOTH], hi, start=(k == 0), stop=False, skip_group_check=True)
                    last = mm(outB[0:FB, :], ff2_w[:, k, DOWN_HI["B"]], lo, start=False, stop=(k == FK - 1),
                              skip_group_check=True)
                last.then_inc(s["y_ps"], 1)

            def queries_keys(hf, part):
                tok = slice(H1 * hf, H1 * hf + H1)
                for ch in range(2):
                    last = w_still(bank[4 * hf + 1 + part][0:CH, H1 * ch:H1 * ch + H1], qkv_w,
                                   DIM * part + CH * ch, 3 * DIM + DIM * part + CH * ch, CH, tok, (yA, yB))
                last.then_inc(s[("q_ps", "k_ps")[part]], 1)

            def token_values(hf):
                for i in range(2):
                    t = 2 * hf + i
                    last = x_still(bank[4 * hf + 3][:, DIM * i:DIM * i + DIM], qkv_w, 2 * DIM, 5 * DIM, DIM,
                                   slice(128 * t, 128 * t + 128), (yA, yB))
                last.then_inc(s["v_ps"], 1)

            def window_scores(i):
                hf, j = i // 3, i % 3
                pe.wait_ge(s["q_done"], 4 * hf + 4)
                pe.wait_ge(s["k_done"], 2 * hf + 2)
                for b in range(HALF_IMG):
                    for ch in range(2):
                        img = HALF_IMG * hf + b
                        last = mm(bank[4 * hf + j][:, 64 * (2 * b + ch):64 * (2 * b + ch) + 64],
                                  q_blk[32 * j:32 * j + 32, ch, img, :, :],
                                  kT[32 * j:32 * j + 32, ch, IMG_TOK * img:IMG_TOK * img + IMG_TOK],
                                  start=True, stop=True)
                last.then_inc(s["s_ps"], 1)

            def turn_prob(i):
                hf, j = i // 3, i % 3
                pe.wait_ge(s["s_norm"], i + 1)
                for b in range(HALF_IMG):
                    last = tr(bank[4 * hf + j][:, 128 * b:128 * b + 128],
                              prob[:, hf, j, 128 * b:128 * b + 128], c("ident"))
                last.then_inc(s["pT_ps"], 1)

            def window_values(i):
                hf, j = i // 3, i % 3
                pe.wait_ge(s["pT_done"], i + 1)
                pe.wait_ge(s["v_done"], 4 * hf + 4)
                for b in range(HALF_IMG):
                    last = mm(bank[4 * hf + j][0:64, 128 * b:128 * b + 128],
                              v_blk[:, HALF_IMG * hf + b, j, :], probT[:, hf, j, 128 * b:128 * b + 128],
                              start=True, stop=True)
                last.then_inc(s["o_ps"], 1)

            def project(hf):
                pe.wait_ge(s["o_done"], 3 * hf + 3)
                for i in range(2):
                    tok = slice(128 * (2 * hf + i), 128 * (2 * hf + i) + 128)
                    out = bank[4 * hf + 3][:, DIM * i:DIM * i + DIM]
                    mm(out, o01[:, tok], proj_w[:, 0, :], start=True, stop=False)
                    last = mm(out, o2[:, tok], proj_w[0:64, 1, :], start=False, stop=True)
                last.then_inc(s["proj_ps"], 1)

            def ff_out2(hf):
                for i in range(2):
                    for k in range(FK):
                        if i == 0:
                            pe.wait_ge(s["gelu2_done"], FK * hf + k + 1)
                        last = mm(bank[4 * hf + 3][:, DIM * i:DIM * i + DIM],
                                  act1[:, hf, k, 128 * i:128 * i + 128], ff2_raw[:, k, :],
                                  start=(k == 0), stop=(k == FK - 1))
                last.then_inc(s["ff2_ps"], 1)

            def hidden1(hf):
                hidden(hf, hf + 1, (1, 2, 3), "gelu_done", "hid1_ps")

            def hidden2(hf):
                hidden(hf, hf + 3, (2, 0, 1), "gelu2_done", "hid2_ps")

            pe.wait_ge(s["filler_done"], 1)
            keep_busy("patches", bank[7])
            patch(0)
            patch(1)
            patch(2)
            patch(3)
            pe.wait_ge(d_const, 16)
            keep_busy("turn_x0", bank[2])
            turn_x(x, 0, "x_done", bank[2], bank[3])
            keep_busy("hidden0", bank[1])
            pe.wait_ge(s["ff1_lo"], 1)
            hidden1(0)
            keep_busy("turn_x1", bank[6])
            turn_x(x, 1, "x_done", bank[6], bank[7])
            keep_busy("hidden1", bank[5])
            hidden1(1)
            keep_busy("ff_out0", bank[0])
            pe.wait_ge(s["ff2_lo"], 2)
            ff_out(0)
            keep_busy("ff_out1", bank[4])
            ff_out(1)
            keep_busy("qkv0", bank[1])
            pe.wait_ge(s["qkv_lo"], 1)
            pe.wait_ge(s["y_lo"], 2)
            queries_keys(0, 0)
            queries_keys(0, 1)
            token_values(0)
            keep_busy("scores0", bank[0])
            window_scores(0)
            keep_busy("qkv1", bank[5])
            pe.wait_ge(s["y_lo"], 4)
            queries_keys(1, 0)
            keep_busy("scores1", bank[1])
            window_scores(1)
            queries_keys(1, 1)
            keep_busy("scores2", bank[2])
            window_scores(2)
            token_values(1)
            pe.wait_ge(s["v_done"], 4)
            keep_busy("prob0", bank[3])
            turn_prob(0)
            for i in range(3):
                keep_busy(f"scores{3 + i}", bank[3])
                window_scores(3 + i)
                if i < 2:
                    keep_busy(f"prob{i + 1}", bank[3])
                    turn_prob(i + 1)
                keep_busy(f"values{i}", bank[3])
                window_values(i)
            keep_busy("prob3", bank[3])
            turn_prob(3)
            pe.wait_ge(d_proj, 16)
            keep_busy("project0", bank[3])
            project(0)
            keep_busy("values3", bank[2])
            window_values(3)
            keep_busy("prob4", bank[2])
            turn_prob(4)
            keep_busy("turn_x2", bank[2])
            turn_x(x1, 0, "x1_done", bank[0], bank[1])
            window_values(4)
            keep_busy("prob5", bank[2])
            turn_prob(5)
            keep_busy("values5", bank[2])
            window_values(5)
            keep_busy("hidden2", bank[2])
            hidden2(0)
            keep_busy("project1", bank[7])
            project(1)
            keep_busy("turn_x3", bank[4])
            turn_x(x1, 1, "x1_done", bank[4], bank[5])
            keep_busy("ff_out2", bank[6])
            ff_out2(0)
            keep_busy("hidden3", bank[6])
            hidden2(1)

            def turn_h(src, hf, atA, atB, done):
                for i in range(HALF_IMG):
                    b = HALF_IMG * hf + i
                    tr(atA[:, TOK * i:TOK * i + TOK], src[:, b, 0:FA], c("ident", TOK)[:, 0:TOK])
                    last = tr(atB[0:FB, TOK * i:TOK * i + TOK], src[:, b, FA:DIM], c("ident", TOK)[:, 0:TOK])
                last.then_inc(s[done], 1)

            def selection_logits(hf):
                pe.wait_ge(s["t_hi"], 2 * (hf + 5))
                pe.wait_ge(s["t_lo"], 2 * (hf + 5))
                w_still(bank[4 * hf + 1][0:2, 0:H2N], kv_w, 2 * DIM, 2 * DIM + VSEL + DIM, 2,
                        slice(H2N * hf, H2N * hf + H2N)).then_inc(s["lg_ps"], 1)

            def turn_logits(hf):
                pe.wait_ge(s["lgT_done"], hf + 1)
                for i in range(HALF_IMG):
                    last = tr(bank[4 * hf + 1][0:TOK, H2N + 2 * i:H2N + 2 * i + 2],
                              lgT[:, H2N * hf + TOK * i:H2N * hf + TOK * i + TOK], c("ident", 2)[:, 0:2])
                last.then_inc(s["lgT_ps"], 1)

            def values(hf, turn=False):
                for i in (2 * hf, 2 * hf + 1):
                    if turn and i % 2:
                        turn_logits(hf)
                    for k in range(2):
                        b = 2 * i + k
                        last = x_still(bank[4 * hf + 2 + i % 2][0:TOK, DIM * k:DIM * k + DIM], kv_w, DIM,
                                       2 * DIM + VSEL, DIM, slice(TOK * b, TOK * b + TOK))
                    last.then_inc(s["av_ps"], 1)

            def keys(hf):
                pe.wait_ge(s["lg_read"], hf + 1)
                for ch in range(2):
                    last = w_still(bank[4 * hf + ch][0:CH, 0:H2N], kv_w, CH * ch, DIM + VSEL + CH * ch, CH,
                                   slice(H2N * hf, H2N * hf + H2N))
                last.then_inc(s["ak_ps"], 1)

            keep_busy("turn_h0", bank[0])
            pe.wait_ge(s["small_split"], 1)
            pe.wait_ge(s["xn_done"], 1)
            turn_h(xn, 0, bank[0], bank[1], "hT_ps")
            keep_busy("ff_out3", bank[2])
            ff_out2(1)
            keep_busy("vk0", bank[2])
            selection_logits(0)
            values(0)
            turn_logits(0)
            keys(0)
            keep_busy("turn_h1", bank[4])
            pe.wait_ge(s["xn_done"], 2)
            turn_h(xn, 1, bank[4], bank[5], "hT_ps")
            keep_busy("vk1", bank[6])
            selection_logits(1)
            values(1, turn=True)
            pe.wait_ge(s["av_done"], 2)
            keep_busy("psel", bank[3])
            pe.wait_ge(s["psel_done"], 1)
            tr(bank[2][0:IMAGES, 0:TOK], psel[:, :], c("ident", TOK)[:, 0:TOK]).then_inc(s["psT_ps"], 1)
            keys(1)
            keep_busy("pickT", bank[3])
            pe.wait_ge(s["pickT_done"], 1)
            tr(bank[2][0:TOK, 128:128 + IMAGES], pickT[:, :], c("ident", IMAGES)[:, 0:IMAGES])\
                .then_inc(s["pick_ps"], 1)
            keep_busy("pick", bank[3])
            pe.wait_ge(s["pick_done"], 1)
            mm(bank[2][0:TOK, 256:256 + IMAGES], c("tri", TOK), pick[:, :], start=True, stop=True)\
                .then_inc(s["cum_ps"], 1)
            keep_busy("hot", bank[3])
            pe.wait_ge(s["hot_done"], 1)
            for b in range(IMAGES):
                mm(bank[3][:, PICKED * b:PICKED * b + PICKED], xn[:, b, 0:FA], hot[:, b, :],
                   start=True, stop=True)
                last = mm(bank[6][0:FB, 256 + PICKED * b:256 + PICKED * b + PICKED], xn[:, b, FA:DIM],
                          hot[:, b, :], start=True, stop=True)
            last.then_inc(s["xs_ps"], 1)
            pe.wait_ge(s["hot_done"], 2)
            tr(bank[7][0:SLOTS, 256:256 + TOK], hotp[:, :, :].rearrange("p a b -> p (a b)"),
               c("ident", TOK)[:, 0:TOK]).then_inc(s["hotpT_ps"], 1)
            keep_busy("xs", bank[2])
            pe.wait_ge(s["xs_done"], 2)
            pe.wait_ge(d_aq, 32)
            for ch in range(2):
                out = bank[7][0:CH, SLOTS * ch:SLOTS * ch + SLOTS]
                mm(out, aq_w[:, 0, CH * ch:CH * ch + CH], xsA[:, :], start=True, stop=False)
                last = mm(out, aq_w[0:FB, 1, CH * ch:CH * ch + CH], xsB[:, :], start=False, stop=True)
            last.then_inc(s["aq_ps"], 1)
            pe.wait_ge(s["ak_even"], 2)
            pe.wait_ge(s["ak_odd"], 2)
            pe.wait_ge(s["hot_spread"], 1)
            for b in range(IMAGES):
                hf, i = b // HALF_IMG, b % HALF_IMG
                mm(bank[4 * hf][0:QROWS, TOK * i:TOK * i + TOK], hot_heads[:, b, :], c("causal", TOK),
                   start=(i == 0), stop=False, skip_group_check=True)
            keep_busy("aq", bank[1])
            pe.wait_ge(s["aq_done"], 2)
            for hf in range(2):
                for i in range(HALF_IMG):
                    b = HALF_IMG * hf + i
                    for ch in range(2):
                        last = mm(bank[4 * hf][0:QROWS, TOK * i:TOK * i + TOK], aq_blk[:, ch, b, :],
                                  akT[:, ch, TOK * b:TOK * b + TOK], start=False, stop=(ch == 1),
                                  skip_group_check=True)
                last.then_inc(s["as_ps"], 1)
            def start_h2(i):
                for k in range(2):
                    mm(h2_bank[i][0:TOK, DIM * k:DIM * k + DIM], c("ident", TOK)[:, 0:TOK], hx[:, 2 * i + k, :],
                       start=(k == 0), stop=False, skip_group_check=True)

            def turn_aprob(hf):
                pe.wait_ge(s["as_norm"], hf + 1)
                for i in range(HALF_IMG):
                    last = tr(bank[4 * hf + 1][0:TOK, QROWS * i:QROWS * i + QROWS],
                              aprob[:, hf, TOK * i:TOK * i + TOK], c("ident", QROWS)[:, 0:QROWS])
                last.then_inc(s["apT_ps"], 1)

            def weighted(hf):
                pe.wait_ge(s["apT_done"], hf + 1)
                for ch in range(2):
                    for i in range(HALF_IMG):
                        at = 60 * (HALF_IMG * ch + i)
                        last = mm(ctx_bank[hf][0:CH, at:at + 60], av[:, HALF_IMG * hf + i, CH * ch:CH * ch + CH],
                                  aprobT[:, hf, QROWS * i + 60 * ch:QROWS * i + 60 * ch + 60],
                                  start=True, stop=True)
                last.then_inc(s["ac_ps"], 1)

            pe.wait_ge(s["hx_done"], 2)
            start_h2(0)
            start_h2(1)
            keep_busy("as0", bank[2])
            turn_aprob(0)
            start_h2(2)
            turn_aprob(1)
            keep_busy("ap0", bank[2])
            weighted(0)
            keep_busy("ap1", bank[4])
            weighted(1)
            start_h2(3)
            pe.wait_ge(s["hotpT_done"], 1)
            keep_busy("ac", bank[7])
            pe.wait_ge(s["ac_done"], 4)
            for ch in range(2):
                last = mm(bank[7][0:SLOTS, 0:DIM], ctxT[:, ch, :, :], out_w[:, ch, :],
                          start=(ch == 0), stop=(ch == 1))
            last.then_inc(s["ao_ps"], 1)
            keep_busy("ao", bank[2])
            pe.wait_ge(s["ao_done"], 1)
            for i in range(4):
                for k in range(2):
                    last = mm(h2_bank[i][0:TOK, DIM * k:DIM * k + DIM], hotpT[:, 2 * i + k, :],
                              arow[:, :], start=False, stop=(k == 1), skip_group_check=True)
                last.then_inc(s["h2_ps"], 1)

            for hf in range(2):
                keep_busy(f"xn2_{hf}", bank[2])
                pe.wait_ge(s["xn2_done"], hf + 1)
                turn_h(xn2, hf, bank[3 + 2 * hf], bank[4 + 2 * hf], "h2T_ps")
            pe.wait_ge(s["small_split"], 2)
            keep_busy("gl", bank[7])
            for hf in range(2):
                pe.wait_ge(s["t_hi"], 2 * (hf + 7))
                pe.wait_ge(s["t_lo"], 2 * (hf + 7))
                w_still(bank[7 if hf == 0 else 0][0:EXPERTS, 0:H2N], gate_w, 0, EXPERTS, EXPERTS,
                        slice(H2N * hf, H2N * hf + H2N)).then_inc(s["gl_ps"], 1)
                keep_busy(f"glt{hf}", bank[2])
            pe.wait_ge(s["gl_done"], 2)
            for b in range(IMAGES):
                last = tr(bank[1][0:TOK, EXPERTS * b:EXPERTS * b + EXPERTS], glT[:, TOK * b:TOK * b + TOK],
                          c("ident", EXPERTS)[:, 0:EXPERTS])
            last.then_inc(s["glt_ps"], 1)

            cuts = ((0, 512, bank[0][:, 0:512], bank[2][:, 0:512]),
                    (512, T2, bank[1][:, 0:256], bank[1][:, 256:512]))

            def up_gate(n, hf, p):
                tok = slice(H2N * hf, H2N * hf + H2N)
                if not isinstance(n, int) or n >= 1:
                    pe.wait_ge(s[f"silu{hf}"], n)
                w_still(bank[3 + 2 * hf][:, 0:H2N], ug_w[p], 0, 2 * HID, HID, tok).then_inc(s[f"u_ps{hf}"], 1)
                if not isinstance(n, int) or n >= 1:
                    pe.wait_ge(s[f"gated{hf}"], n)
                w_still(bank[4 + 2 * hf][:, 0:H2N], ug_w[p], HID, 3 * HID, HID, tok)\
                    .then_inc(s[f"g_ps{hf}"], 1)

            def spread(hf):
                if hf:
                    pe.wait_ge(s["weighed"], 1)
                mm(bank[7][:, 0:H2N], sel_w[:, :], wT[:, H2N * hf:H2N * hf + H2N],
                   start=True, stop=True).then_inc(s["wb_ps"], 1)

            def down(n, part, p):
                a, b, outA, outB = cuts[part]
                hi, lo = hid_s[p][:, 0, a:b], hid_s[p][:, 1, a:b]
                kw = {"start": False, "stop": False, "skip_group_check": True}
                mm(outA, dn_w[p][:, DOWN_HI["A"]], hi, **kw)
                mm(outA, dn_w[p][:, DOWN_LO["A"]], hi, **kw)
                mm(outA, dn_w[p][:, DOWN_HI["A"]], lo, **kw)
                mm(outB, dn_w[p][:, B_BOTH], hi, **kw)
                return mm(outB[0:FB, :], dn_w[p][:, DOWN_HI["B"]], lo, **kw)

            def weights_ready(n):
                pe.wait_ge(s["ug_hi"], n + 1)
                if isinstance(n, int) and n < 2:
                    pe.wait_ge(s["first_lo"], n + 1)
                else:
                    pe.wait_ge(s["ug_lo"], n - 1)

            def hidden_ready(n):
                pe.wait_ge(s["hid_hi"], 2 * n + 2)
                pe.wait_ge(s["hid_lo"], 2 * n + 2)
                pe.wait_ge(s["dn_hi"], n + 1)
                pe.wait_ge(s["dn_lo"], 2 * n + 2)

            def expert(n, p):
                weights_ready(n)
                up_gate(n, 0, p)
                up_gate(n, 1, p)
                hidden_ready(n - 1)
                down(n - 1, 0, 1 - p)
                down(n - 1, 1, 1 - p).then_inc(s["down_done"], 1)

            def residual_sums(cuts_of):
                started = set()
                for cut, part in cuts_of:
                    lo, hi, outs = cuts[cut][0], cuts[cut][1], cuts[cut][2:]
                    for b in range(IMAGES):
                        t0, t1 = max(TOK * b, lo), min(TOK * b + TOK, hi)
                        if t0 < t1:
                            mm(outs[part][:, t0 - lo:t1 - lo], h2[:, b, FA * part:FA * part + FA],
                               c("ident", TOK)[:, t0 - TOK * b:t1 - TOK * b],
                               start=(cut, part if cut == 0 else 0) not in started, stop=False,
                               skip_group_check=True)
                            started.add((cut, part if cut == 0 else 0))

            weights_ready(0)
            up_gate(0, 0, 0)
            up_gate(0, 1, 0)
            pe.wait_ge(s["gd_done"], 1)
            residual_sums(((0, 0), (1, 0), (1, 1)))
            weights_ready(1)
            keep_busy("ug1", bank[2])
            up_gate(1, 0, 1)
            up_gate(1, 1, 1)
            keep_busy("wfull", bank[2])
            pe.wait_ge(s["wfull_done"], 1)
            for hf in range(2):
                for i in range(HALF_IMG):
                    last = tr(bank[7 if hf == 0 else 2][0:EXPERTS, TOK * i:TOK * i + TOK],
                              wfull[:, HALF_IMG * hf + i, :], c("ident", TOK)[:, 0:TOK])
                last.then_inc(s["wT_ps"], 1)
            hidden_ready(0)
            down(0, 1, 0)
            pe.wait_ge(s["w_flat_done"], 2)
            residual_sums(((0, 1),))
            pe.wait_ge(s["sel_done"], 1)
            pe.wait_ge(s["wT_lo"], 1)
            spread(0)
            pe.wait_ge(s["small_split"], 3)
            kw = {"start": False, "stop": False, "skip_group_check": True}
            for a, b, outA, outB in cuts:
                mm(outA, bd_w[0:EXPERTS, 1, 0:FA], wT[0:EXPERTS, a:b], **kw)
                mm(outB[0:FB, :], bd_w[0:EXPERTS, 1, FA:DIM], wT[0:EXPERTS, a:b], **kw)
            down(0, 0, 0).then_inc(s["down_done"], 1)
            pe.wait_ge(s["wT_lo"], 2)
            for a, b, outA, outB in cuts:
                mm(outA, bd_w[0:48, 0, 0:FA], wT[0:48, a:b], **kw)
                mm(outB[0:FB, :], bd_w[0:48, 0, FA:DIM], wT[0:48, a:b], **kw)
            spread(1)
            with pe.Fori(0, 7) as it:
                expert(2 * it + 2, 0)
                expert(2 * it + 3, 1)
            expert(16, 0)
            hidden_ready(16)
            down(16, 0, 0).then_inc(s["sum_done"], 1)
            down(16, 1, 0).then_inc(s["sum_done"], 1)

        @block.scalar
        def _(act):
            a = nc.scalar.activation

            def hi_of_turned(atA, atB, n, tok, done, k):
                act.wait_ge(s[done], k)
                a(tA[:, 0, tok], atA, ACT.Copy).then_inc(s["t_hi"], 1)
                a(tB[0:FB, tok], atB, ACT.Copy).then_inc(s["t_hi"], 1)

            def turned_hi(hf, k, atA, atB):
                hi_of_turned(atA[:, 0:H1], atB[0:FB, 0:H1], H1, slice(H1 * hf, H1 * hf + H1), "xT_ps", k)

            def gelu(hf, banks, ready, done):
                for m in range(FK):
                    act.wait_ge(s[ready], FK * hf + m + 1)
                    a(act1[:, hf, m, :], bank[4 * hf + banks[m % 3]][:, 0:H1], ACT.Gelu_apprx_tanh,
                      bias=col("ff1_b", 128, m)).then_inc(s[done], 1)

            def ff_out(hf):
                tok = slice(H1 * hf, H1 * hf + H1)
                act.wait_ge(s["y_ps"], hf + 1)
                a(ytmp[:, tok], bank[4 * hf][FB:128, H1:2 * H1], ACT.Copy).then_inc(s["yB_moved"], 1)
                a(yA[:, 0, tok], bank[4 * hf][:, 0:H1], ACT.Identity, bias=col("ff2_bA", 128))\
                    .then_inc(s["yA_hi"], 1)
                act.wait_ge(s["yB_sum"], hf + 1)
                a(yB[0:FB, tok], ybf[:, tok], ACT.Copy).then_inc(s["yB_hi"], 1)

            def queries(hf):
                act.wait_ge(s["q_ps"], hf + 1)
                for ch in range(2):
                    for par in range(2):
                        a(q_blk[:, ch, HALF_IMG * hf:HALF_IMG * hf + HALF_IMG, par, :],
                          v3(bank[4 * hf + 1][0:CH, H1 * ch:H1 * ch + H1], IMG_TOK), ACT.Identity,
                          bias=bqm[:, ch, par:par + 1], scale=c("parity", CH)[:, par:par + 1])\
                            .then_inc(s["q_done"], 1)

            def window_exp(i):
                act.wait_ge(s["s_sub"], i + 1)
                a(prob[:, i // 3, i % 3, :], prob[:, i // 3, i % 3, :], ACT.Exp, scale=HEAD ** -0.5)\
                    .then_inc(s["s_exp"], 1)

            def prob_out(i):
                act.wait_ge(s["pT_ps"], i + 1)
                a(probT[:, i // 3, i % 3, :], bank[4 * (i // 3) + i % 3][:, :], ACT.Copy)\
                    .then_inc(s["pT_done"], 1)

            def even_heads(i):
                hf, j = i // 3, i % 3
                act.wait_ge(s["o_ps"], i + 1)
                even = bank[4 * hf + j][0:64, :].rearrange("p (b h q) -> p b h q", h=2, q=IMG_TOK)[:, :, 0, :]
                a(v3(otmp[:, hf, j, :], IMG_TOK), even, ACT.Copy, scale=c("parity", 64)[:, 0:1])\
                    .then_inc(s["o_even"], 1)

            def load_table(function, k):
                act.wait_ge(s["filler_done"], 2)
                a(table[0:1, k:k + 1], table[0:1, k:k + 1], function)

            load_table(ACT.Gelu_apprx_tanh, 0)
            act.wait_ge(d_ff1, 16)
            a(ff1_w[:, 0, :], ff1_raw[:, :], ACT.Copy).then_inc(s["ff1_hi"], 1)
            turned_hi(0, 1, bank[2], bank[3])
            act.wait_ge(d_ff2, 16)
            a(ff2_w[:, :, 0:DIM], ff2_raw[:, :, :], ACT.Copy).then_inc(s["ff2_hi"], 1)
            act.wait_ge(d_qkv, 16)
            a(qkv_w[:, 0, :], qkv_raw[:, :], ACT.Copy).then_inc(s["qkv_hi"], 1)
            act.wait_ge(d_cols, 16)
            gelu(0, (1, 2, 3), "hid1_ps", "gelu_done")
            turned_hi(1, 2, bank[6], bank[7])
            gelu(1, (1, 2, 3), "hid1_ps", "gelu_done")
            load_table(ACT.Exp, 1)
            ff_out(0)
            ff_out(1)
            act.wait_ge(s["bqm_done"], 2)
            queries(0)
            window_exp(0)
            window_exp(1)
            queries(1)
            window_exp(2)
            prob_out(0)
            window_exp(3)
            prob_out(1)
            even_heads(0)
            window_exp(4)
            prob_out(2)
            even_heads(1)
            even_heads(2)
            window_exp(5)
            prob_out(3)
            load_table(ACT.Gelu_apprx_tanh, 2)
            even_heads(3)
            prob_out(4)
            turned_hi(0, 3, bank[0], bank[1])
            even_heads(4)
            prob_out(5)
            even_heads(5)
            gelu(0, (2, 0, 1), "hid2_ps", "gelu2_done")
            turned_hi(1, 4, bank[4], bank[5])
            gelu(1, (2, 0, 1), "hid2_ps", "gelu2_done")

            load_table(ACT.Exp, 3)
            def keys_chunk0(hf):
                act.wait_ge(s["ak_ps"], hf + 1)
                a(akT[:, 0, H2N * hf:H2N * hf + H2N], bank[4 * hf][0:CH, 0:H2N], ACT.Identity,
                  bias=col("ak_b", CH, 0)).then_inc(s["ak_even"], 1)

            def logits_out(hf):
                act.wait_ge(s["lg_ps"], hf + 1)
                a(lgT[:, H2N * hf:H2N * hf + H2N], bank[4 * hf + 1][0:2, 0:H2N], ACT.Identity,
                  bias=col("sel_b", 2)).then_inc(s["lgT_done"], 1)

            def first_split(n):
                act.wait_ge(d_ug[n], 16)
                a(ug_w[n][:, 0, :], expert_raw[:, n, 0:DOWN0], ACT.Copy).then_inc(s["ug_hi"], 1)

            hi_of_turned(bank[0][:, 0:H2N], bank[1][0:FB, 0:H2N], H2N, slice(0, H2N), "hT_ps", 1)
            logits_out(0)
            hi_of_turned(bank[4][:, 0:H2N], bank[5][0:FB, 0:H2N], H2N, slice(H2N, T2), "hT_ps", 2)
            keys_chunk0(0)
            logits_out(1)
            act.wait_ge(s["ld_done"], 1)
            a(le[:, :, :], ld[:, :, :], ACT.Exp).then_inc(s["le_done"], 1)
            first_split(0)
            keys_chunk0(1)
            act.wait_ge(s["hot_done"], 1)
            a(hot_heads[:, :, :].rearrange("p b (h i) -> p b h i", h=HEADS),
              hot[:, :, :].unsqueeze(2).to_broadcast([TOK, IMAGES, HEADS, PICKED]), ACT.Copy)\
                .then_inc(s["hot_spread"], 1)
            first_split(1)
            act.wait_ge(d_dn[0], 16)
            a(dn_w[0][:, 0:DIM], expert_raw[:, 0, DOWN0:DOWN0 + DIM], ACT.Copy).then_inc(s["dn_hi"], 1)
            act.wait_ge(s["xs_ps"], 1)
            a(xsB[:, :], bank[6][0:FB, 256:256 + SLOTS], ACT.Copy).then_inc(s["xs_done"], 1)
            for hf in range(2):
                act.wait_ge(s["as_sub"], hf + 1)
                a(aprob[:, hf, :], aprob[:, hf, :], ACT.Exp).then_inc(s["as_exp"], 1)
            for hf in range(2):
                act.wait_ge(s["apT_ps"], hf + 1)
                a(aprobT[:, hf, :], bank[4 * hf + 1][0:TOK, 0:HALF_IMG * QROWS], ACT.Copy)\
                    .then_inc(s["apT_done"], 1)

            for i in range(4):
                act.wait_ge(s["h2_read"], i + 1)
                a(h2[:, 2 * i:2 * i + 2, 0:DIM], v3(h2_bank[i][0:TOK, 0:2 * DIM], DIM), ACT.Copy)\
                    .then_inc(s["h2_done"], 1)

            for hf in range(2):
                hi_of_turned(bank[3 + 2 * hf][:, 0:H2N], bank[4 + 2 * hf][0:FB, 0:H2N], H2N,
                             slice(H2N * hf, H2N * hf + H2N), "h2T_ps", hf + 1)
            for hf in range(2):
                act.wait_ge(s["gl_ps"], hf + 1)
                a(glT[:, H2N * hf:H2N * hf + H2N], bank[7 if hf == 0 else 0][0:EXPERTS, 0:H2N], ACT.Identity,
                  bias=col("gate_b", EXPERTS)).then_inc(s["gl_done"], 1)
            act.wait_ge(s["gd_done"], 1)
            a(gexp[:, :, :], gexp[:, :, :], ACT.Exp).then_inc(s["ge_done"], 1)

            load_table(ACT.Silu, 4)

            def split_up(n, p):
                act.wait_ge(d_ug[p], 8 * (n - p) + 16)
                if not isinstance(n, int) or n >= 2:
                    act.wait_ge(s["u_ps1"], n - 1)
                    act.wait_ge(s["g_ps1"], n - 1)
                a(ug_w[p][:, 0, :], expert_raw[:, p, 0:4 * HID], ACT.Copy).then_inc(s["ug_hi"], 1)

            def gate_act(n, hf, p):
                if hf == 0:
                    act.wait_ge(d_dn[p], 8 * (n - p) + 16)
                act.wait_ge(s[f"u_ps{hf}"], n + 1)
                if not isinstance(n, int) or n >= 1:
                    act.wait_ge(s[f"gated{hf}"], n)
                a(silu[hf][:, :], bank[3 + 2 * hf][:, 0:H2N], ACT.Silu,
                  bias=expert_raw[:, p, BU:BU + 1]).then_inc(s[f"silu{hf}"], 1)

            def hid_hi(n, hf, p):
                if isinstance(n, int) and n == 0:
                    act.wait_ge(s[f"gated{hf}"], 1)
                else:
                    act.wait_ge(s["weighed"], 2 * (n - 1) + hf + 1)
                    if not isinstance(n, int) or n > 1:
                        act.wait_ge(s["down_done"], n - 1)
                a(hid_s[p][:, 0, H2N * hf:H2N * hf + H2N], hid[hf][:, :], ACT.Copy)\
                    .then_inc(s["hid_hi"], 1)

            def expert(n, p, more=True):
                gate_act(n, 0, p)
                if more:
                    split_up(n + 1, 1 - p)
                if not isinstance(n, int) or n > 1:
                    act.wait_ge(s["down_done"], n - 1)
                a(dn_w[p][:, 0:DIM], expert_raw[:, p, DOWN0:DOWN0 + DIM], ACT.Copy).then_inc(s["dn_hi"], 1)
                gate_act(n, 1, p)
                hid_hi(n, 0, p)
                hid_hi(n, 1, p)

            gate_act(0, 0, 0)
            gate_act(0, 1, 0)
            hid_hi(0, 0, 0)
            hid_hi(0, 1, 0)
            act.wait_ge(s["zeros_done"], 11)
            for hf in range(2):
                act.wait_ge(s["wT_ps"], hf + 1)
                a(wT[0:EXPERTS, H2N * hf:H2N * hf + H2N], bank[7 if hf == 0 else 2][0:EXPERTS, 0:H2N], ACT.Copy)\
                    .then_inc(s["wT_hi"], 1)
            expert(1, 1)
            with act.Fori(0, 7) as it:
                expert(2 * it + 2, 0)
                expert(2 * it + 3, 1)
            expert(16, 0, more=False)
            act.wait_ge(s["sum_done"], 1)
            a(fin_tmp[:, 0:512], bank[2][FB:128, 0:512], ACT.Copy).then_inc(s["fin_moved"], 1)
            act.wait_ge(s["sum_done"], 2)
            a(fin_tmp[:, 512:T2], bank[1][FB:128, 256:512], ACT.Copy).then_inc(s["fin_moved"], 1)
            a(finA[:, 512:T2], bank[1][:, 0:256], ACT.Identity, bias=col("sbdA", 128)).then_inc(s["fin_moved"], 1)

        @block.vector
        def _(dve):
            v = nc.vector
            step, after = chain(dve, "vec_step")

            def lo_of_turned(atA, atB, tok, k):
                dve.wait_ge(s["t_hi"], 2 * k - 1)
                v.tensor_tensor(tA[:, 1, tok], atA, f(tA[:, 0, tok]), ALU.subtract).then_inc(s["t_lo"], 1)
                dve.wait_ge(s["t_hi"], 2 * k)
                v.tensor_tensor(tB[FB:128, tok], atB, f(tB[0:FB, tok]), ALU.subtract).then_inc(s["t_lo"], 1)

            def token_stats(t):
                dve.wait_ge(s["patch_ps"], t + 1)
                k = step(v.tensor_tensor(x0[:, t, :], bank[4 * (t // 2) + t % 2][:, 0:DIM],
                                         row("patch_b", 0, 128), ALU.add))
                after(k)
                k = step(v.bn_stats(st1[:, t, :], x0[:, t, :]))
                after(k)
                v.bn_aggr(mv1[:, t, :], st1[:, t, :]).then_inc(s["mv1_done"], 1)

            def token_norm(hf, kb):
                ts = slice(2 * hf, 2 * hf + 2)
                dve.wait_ge(s["mv1_done"], 2 * hf + 2)
                dve.wait_ge(s["rs1_done"], hf + 1)
                for t in (2 * hf, 2 * hf + 1):
                    k = step(v.tensor_scalar(x0[:, t, :], x0[:, t, :], mv1[:, t, 0:1], rs1[:, t:t + 1],
                                             ALU.subtract, ALU.mult))
                after(k)
                k = step(v.tensor_tensor(x0[:, ts, :], x0[:, ts, :],
                                         row("ln_g", 0, 128).unsqueeze(1).to_broadcast([128, 2, DIM]), ALU.mult))
                after(max(k, kb))
                v.tensor_tensor(x[:, ts, :], x0[:, ts, :], bpe[:, :].unsqueeze(1).to_broadcast([128, 2, DIM]),
                                ALU.add).then_inc(s["x_done"], 1)

            def turned_lo(hf, k, atA, atB):
                lo_of_turned(atA[:, 0:H1], atB[0:FB, 0:H1], slice(H1 * hf, H1 * hf + H1), k)

            def split_hidden(hf):
                for m in range(FK):
                    i = FK * hf + m
                    dve.wait_ge(s["gelu_done"], i + 1)
                    k = step(v.tensor_copy(act1s[:, hf, 0, m, :], act1[:, hf, m, :]))
                    after(k)
                    v.tensor_tensor(act1s[:, hf, 1, m, :], act1[:, hf, m, :], f(act1s[:, hf, 0, m, :]),
                                    ALU.subtract).then_inc(s["act1_lo"], 1)

            def ff_out(hf):
                tok = slice(H1 * hf, H1 * hf + H1)
                dve.wait_ge(s["yB_moved"], hf + 1)
                dve.wait_ge(s["yA_hi"], hf + 1)
                v.scalar_tensor_tensor(ybf[:, tok], bank[4 * hf][0:FB, H1:2 * H1], col("ff2_bB", FB),
                                       ytmp[:, tok], ALU.add, ALU.add).then_inc(s["yB_sum"], 1)
                v.scalar_tensor_tensor(yA[:, 1, tok], bank[4 * hf][:, 0:H1], col("ff2_bA", 128),
                                       f(yA[:, 0, tok]), ALU.add, ALU.subtract).then_inc(s["y_lo"], 1)
                dve.wait_ge(s["yB_hi"], hf + 1)
                v.tensor_tensor(yB[FB:128, tok], ybf[:, tok], f(yB[0:FB, tok]), ALU.subtract)\
                    .then_inc(s["y_lo"], 1)

            def keys(hf):
                dve.wait_ge(s["k_ps"], hf + 1)
                for ch in range(2):
                    v.tensor_scalar(kT[:, ch, H1 * hf:H1 * hf + H1],
                                    bank[4 * hf + 2][0:CH, H1 * ch:H1 * ch + H1],
                                    col("k_b", CH, ch), None, ALU.add).then_inc(s["k_done"], 1)

            def values(hf):
                dve.wait_ge(s["v_ps"], hf + 1)
                for i in range(2):
                    for ch in range(2):
                        src = bank[4 * hf + 3][64 * i:64 * i + 64, 0:2 * DIM].rearrange(
                            "p (t c j k) -> p t c j k", t=2, c=2, j=3)[:, :, ch, :, :]
                        bias = row("v_b", 64 * i, 64 * i + 64)[:, CH * ch:CH * ch + CH]
                        first = HALF_IMG * hf + i
                        v.tensor_tensor(v_blk[64 * ch:64 * ch + 64, first:first + 3:2, :, 32 * ch:32 * ch + 32],
                                        src, v3(bias, 32).unsqueeze(1).to_broadcast([64, 2, 3, 32]), ALU.add)\
                            .then_inc(s["v_done"], 1)

            def softmax_sub(src, dst, mx, n, groups, ready, k, sub):
                wide = [n, groups, src.shape[-1]]
                dve.wait_ge(s[ready], k)
                j = step(v.tensor_reduce(mx, src, AXX, ALU.max))
                after(j)
                v.tensor_tensor(dst, src, mx.unsqueeze(2).to_broadcast(wide), ALU.subtract).then_inc(s[sub], 1)

            def softmax_norm(dst, sm, rc, n, groups, k, exp, norm):
                wide = [n, groups, dst.shape[-1]]
                dve.wait_ge(s[exp], k)
                j = step(v.tensor_reduce(sm, dst, AXX, ALU.add))
                after(j)
                j = step(v.reciprocal(rc, sm))
                after(j)
                v.tensor_tensor(dst, dst, rc.unsqueeze(2).to_broadcast(wide), ALU.mult).then_inc(s[norm], 1)

            def window_sub(i):
                hf, j = i // 3, i % 3
                softmax_sub(v3(bank[4 * hf + j][:, :], IMG_TOK), v3(prob[:, hf, j, :], IMG_TOK),
                            smax[:, hf, j, :], 128, 8, "s_ps", i + 1, "s_sub")

            def window_norm(i):
                hf, j = i // 3, i % 3
                dve.wait_ge(s["s_exp"], i + 1)
                k = step(v.tensor_reduce(ssum[:, hf, j, :], v3(prob[:, hf, j, :], IMG_TOK), AXX, ALU.add))
                after(k)
                v.reciprocal(srec[:, hf, j, :], ssum[:, hf, j, :]).then_inc(s["s_rec"], 1)

            def odd_heads(i):
                hf, j = i // 3, i % 3
                dve.wait_ge(s["o_even"], i + 1)
                odd = bank[4 * hf + j][0:64, :].rearrange("p (b h q) -> p b h q", h=2, q=IMG_TOK)[:, :, 1, :]
                tok = slice(H1 * hf, H1 * hf + H1)
                dst = (o01[0:64, tok], o01[64:128, tok], o2[:, tok])[j]
                v.scalar_tensor_tensor(v3(dst, IMG_TOK), odd, c("parity", 64)[:, 1:2],
                                       v3(otmp[:, hf, j, :], IMG_TOK), ALU.mult, ALU.add)\
                    .then_inc(s["o_done"], 1)

            def residual(hf):
                dve.wait_ge(s["proj_ps"], hf + 1)
                dve.wait_ge(s["xpb_done"], hf + 1)
                ts = slice(2 * hf, 2 * hf + 2)
                v.tensor_tensor(x1[:, ts, :], v3(bank[4 * hf + 3][:, 0:2 * DIM], DIM), xpb[:, ts, :], ALU.add)\
                    .then_inc(s["x1_done"], 1)

            dve.wait_ge(d_rows, 16)
            token_stats(0)
            token_stats(1)
            dve.wait_ge(d_const, 16)
            kb = step(v.tensor_tensor(bpe[:, :], row("ln_b", 0, 128), c("pe"), ALU.add))
            token_norm(0, kb)
            token_stats(2)
            dve.wait_ge(d_ff1, 16)
            dve.wait_ge(s["ff1_hi"], 1)
            three = v3(ff1_raw[:, :], FF)[:, :, 0:FF // 2]
            v.tensor_tensor(v3(ff1_w[:, 1, :], FF)[:, :, 0:FF // 2], three, v3(f(ff1_w[:, 0, :]), FF)[:, :, 0:FF // 2],
                            ALU.subtract).then_inc(s["ff1_lo"], 1)
            turned_lo(0, 1, bank[2], bank[3])
            token_stats(3)
            token_norm(1, kb)
            dve.wait_ge(d_cols, 16)
            for ch in range(2):
                v.tensor_scalar(bqm[:, ch, :], c("parity", CH), col("q_b", CH, ch), None, ALU.mult)\
                    .then_inc(s["bqm_done"], 1)
            turned_lo(1, 2, bank[6], bank[7])
            split_hidden(0)
            split_hidden(1)
            ff_out(0)
            ff_out(1)
            dve.wait_ge(s["zeros_done"], 1)
            dve.wait_ge(d_rows2, 16)
            keys(0)
            values(0)
            window_sub(0)
            window_sub(1)
            window_norm(0)
            keys(1)
            window_sub(2)
            window_norm(1)
            values(1)
            window_sub(3)
            window_norm(2)
            odd_heads(0)
            window_sub(4)
            window_norm(3)
            odd_heads(1)
            window_sub(5)
            odd_heads(2)
            window_norm(4)
            window_norm(5)
            residual(0)
            odd_heads(3)
            turned_lo(0, 3, bank[0], bank[1])
            odd_heads(4)
            odd_heads(5)
            residual(1)

            def token_moments(src, st, mv, hf, done_mv):
                for b in range(HALF_IMG * hf, HALF_IMG * hf + HALF_IMG):
                    k = step(v.bn_stats(st[:, b, :], src[:, b, 0:DIM]))
                for b in range(HALF_IMG * hf, HALF_IMG * hf + HALF_IMG):
                    if b == HALF_IMG * hf:
                        after(k)
                    last = v.bn_aggr(mv[:, b, :], st[:, b, :])
                last.then_inc(s[done_mv], 1)

            def normalise(src, mv, rs, dst, hf, done_mv, done_rs, done):
                if done == "xn2_done":
                    dve.wait_ge(s["h2_done"], 2 * hf + 2)
                dve.wait_ge(s[done_mv], hf + 1)
                dve.wait_ge(s[done_rs], hf + 1)
                for b in range(HALF_IMG * hf, HALF_IMG * hf + HALF_IMG):
                    last = v.tensor_scalar(dst[:, b, :], src[:, b, 0:DIM], mv[:, b, 0:1], rs[:, b:b + 1],
                                           ALU.subtract, ALU.mult)
                last.then_inc(s[done], 1)

            def down_lo(n, p):
                dve.wait_ge(s["dn_hi"], n + 1)
                raw = expert_raw[:, p, DOWN0:DOWN0 + DIM]
                for part in "AB":
                    v.tensor_tensor(dn_w[p][:, DOWN_LO[part]], raw[:, DOWN_HI[part]],
                                    f(dn_w[p][:, DOWN_HI[part]]), ALU.subtract).then_inc(s["dn_lo"], 1)

            def image_rows(hf):
                dve.wait_ge(s["ff2_ps"], hf + 1)
                dve.wait_ge(s["x1b_done"], hf + 1)
                for i in range(2):
                    first = HALF_IMG * hf + i
                    k = step(v.tensor_tensor(h[0:IMG_TOK, first:first + 3:2, :],
                                             v3(bank[4 * hf + 3][64 * i:64 * i + 64, 0:2 * DIM], DIM),
                                             x1b[64 * i:64 * i + 64, 2 * hf:2 * hf + 2, :], ALU.add))
                after(k)
                token_moments(h, st2, mv2, hf, "mv2_done")

            def selection_scale(hf):
                dve.wait_ge(s["lgT_ps"], hf + 1)
                v.tensor_scalar(lgt[:, 4 * hf:4 * hf + 4, :],
                                v3(bank[4 * hf + 1][0:TOK, H2N:H2N + 2 * HALF_IMG], 2), itemp[:, 0:1],
                                None, ALU.mult).then_inc(s["lg_read"], 1)

            def values(i):
                dve.wait_ge(s["av_ps"], i + 1)
                v.tensor_tensor(av[:, 2 * i:2 * i + 2, :],
                                v3(bank[4 * (i // 2) + 2 + i % 2][0:TOK, 0:2 * DIM], DIM),
                                row("av_b", 0, TOK).unsqueeze(1).to_broadcast([TOK, 2, DIM]), ALU.add)\
                    .then_inc(s["av_done"], 1)

            def keys_chunk1(hf):
                dve.wait_ge(s["ak_ps"], hf + 1)
                v.tensor_scalar(akT[:, 1, H2N * hf:H2N * hf + H2N], bank[4 * hf + 1][0:CH, 0:H2N],
                                col("ak_b", CH, 1), None, ALU.add).then_inc(s["ak_odd"], 1)

            dve.wait_ge(d_txt, 16)
            turned_lo(1, 4, bank[4], bank[5])
            image_rows(0)
            k_temp = step(v.reciprocal(itemp[:, :], row("temp", 0, TOK)))
            normalise(h, mv2, rs2, xn, 0, "mv2_done", "rs2_done", "xn_done")
            lo_of_turned(bank[0][:, 0:H2N], bank[1][0:FB, 0:H2N], slice(0, H2N), 5)
            image_rows(1)
            after(k_temp)
            selection_scale(0)
            normalise(h, mv2, rs2, xn, 1, "mv2_done", "rs2_done", "xn_done")
            values(0)
            lo_of_turned(bank[4][:, 0:H2N], bank[5][0:FB, 0:H2N], slice(H2N, T2), 6)
            values(1)
            keys_chunk1(0)
            selection_scale(1)
            dve.wait_ge(s["lg_read"], 2)
            k = step(v.tensor_tensor(lmax[:, :], lgt[:, :, 0], lgt[:, :, 1], ALU.max))
            after(k)
            v.tensor_tensor(ld[:, :, :], lgt[:, :, :], lmax[:, :].unsqueeze(2).to_broadcast([TOK, IMAGES, 2]),
                            ALU.subtract).then_inc(s["ld_done"], 1)
            values(2)
            dve.wait_ge(s["le_done"], 1)
            k = step(v.tensor_tensor(lsum[:, :], le[:, :, 0], le[:, :, 1], ALU.add))
            after(k)
            k = step(v.reciprocal(lrec[:, :], lsum[:, :]))
            after(k)
            v.tensor_tensor(psel[:, :], le[:, :, 1], lrec[:, :], ALU.mult).then_inc(s["psel_done"], 1)
            values(3)
            dve.wait_ge(s["psT_ps"], 1)
            dve.wait_ge(s["zeros_done"], 11)
            k = step(v.tensor_copy(pT[:, 0:TOK], bank[2][0:IMAGES, 0:TOK]))
            after(k)
            k = step(v.max(top8[:, :], pT[:, 0:TOK]))
            after(k)
            k = step(v.match_replace(out=pT8[:, :], in_to_replace=top8[:, :], in_values=pT[:, :], imm_value=GONE))
            after(k)
            k = step(v.max(next8[:, :], pT8[:, 0:TOK]))
            after(k)
            k = step(v.tensor_copy(last2[:, 0:2], next8[:, 0:2]))
            after(k)
            k = step(v.match_replace(out=pT10[:, :], in_to_replace=last2[:, :], in_values=pT8[:, :],
                                     imm_value=GONE))
            after(k)
            v.tensor_tensor(pickT[:, :], pT10[:, 0:TOK], pT[:, 0:TOK], ALU.not_equal)\
                .then_inc(s["pickT_done"], 1)
            dve.wait_ge(s["pick_ps"], 1)
            v.tensor_copy(pick[:, :], bank[2][0:TOK, 128:128 + IMAGES]).then_inc(s["pick_done"], 1)
            keys_chunk1(1)
            dve.wait_ge(s["cum_ps"], 1)
            dve.wait_ge(s["pick_done"], 1)
            k = step(v.tensor_tensor(rank[:, :], bank[2][0:TOK, 256:256 + IMAGES], pick[:, :], ALU.mult))
            after(k)
            wide = [TOK, IMAGES, PICKED]
            v.tensor_tensor(hot[:, :, :], rank[:, :].unsqueeze(2).to_broadcast(wide),
                            c("iota", TOK).unsqueeze(1).to_broadcast(wide), ALU.is_equal)\
                .then_inc(s["hot_done"], 1)
            dve.wait_ge(s["hot_done"], 1)
            v.tensor_tensor(hotp[:, :, :], hot[:, :, :], psel[:, :].unsqueeze(2).to_broadcast(wide), ALU.mult)\
                .then_inc(s["hot_done"], 1)
            down_lo(0, 0)
            dve.wait_ge(s["xs_ps"], 1)
            v.tensor_copy(xsA[:, :], bank[3][:, 0:SLOTS]).then_inc(s["xs_done"], 1)
            dve.wait_ge(s["aq_ps"], 1)
            for ch in range(2):
                k = step(v.tensor_scalar(aq[:, ch, :], bank[7][0:CH, SLOTS * ch:SLOTS * ch + SLOTS],
                                         col("aq_b", CH, ch), HEAD ** -0.5, ALU.add, ALU.mult))
            after(k)
            wide = [CH, IMAGES, CHH, PICKED]
            for ch in range(2):
                dst = aq_blk[:, ch, :, 60 * ch:60 * ch + 60].rearrange("p b (h i) -> p b h i", h=CHH)
                v.tensor_tensor(dst, v3(aq[:, ch, :], PICKED).unsqueeze(2).to_broadcast(wide),
                                c("head", CH).unsqueeze(1).unsqueeze(3).to_broadcast(wide), ALU.mult)\
                    .then_inc(s["aq_done"], 1)
            for hf in range(2):
                b = slice(HALF_IMG * hf, HALF_IMG * hf + HALF_IMG)
                softmax_sub(v3(bank[4 * hf][0:QROWS, 0:H2N], TOK), v3(aprob[:, hf, :], TOK), amax[:, b],
                            QROWS, HALF_IMG, "as_ps", hf + 1, "as_sub")
            for hf in range(2):
                b = slice(HALF_IMG * hf, HALF_IMG * hf + HALF_IMG)
                softmax_norm(v3(aprob[:, hf, :], TOK), asum[:, b], arec[:, b], QROWS, HALF_IMG, hf + 1,
                             "as_exp", "as_norm")
            dve.wait_ge(s["hotpT_ps"], 1)
            wide = [SLOTS, IMAGES, TOK]
            v.tensor_tensor(hotpT[:, :, :], bank[7][0:SLOTS, 256:256 + TOK].unsqueeze(1).to_broadcast(wide),
                            c("block", SLOTS).unsqueeze(2).to_broadcast(wide), ALU.mult)\
                .then_inc(s["hotpT_done"], 1)
            for hf in range(2):
                dve.wait_ge(s["ac_ps"], hf + 1)
                wide = [CH, 2 * HALF_IMG, CHH, PICKED]
                buf = actx[:, hf, :, :]
                k = step(v.tensor_tensor(
                    buf.rearrange("p c (h i) -> p c h i", h=CHH),
                    ctx_bank[hf][0:CH, 0:480].rearrange("p (c h i) -> p c h i", c=2 * HALF_IMG, h=CHH),
                    c("head", CH).unsqueeze(1).unsqueeze(3).to_broadcast(wide), ALU.mult))
                after(k)
                for ch in range(2):
                    v.tensor_reduce(v3(ctxT[:, ch, hf, :], PICKED),
                                    buf[:, HALF_IMG * ch:HALF_IMG * ch + HALF_IMG, :].rearrange(
                                        "p c (h i) -> p c i h", h=CHH), AXX, ALU.add)\
                        .then_inc(s["ac_done"], 1)
            dve.wait_ge(s["ao_ps"], 1)
            v.tensor_tensor(arow[:, :], bank[7][0:SLOTS, 0:DIM], row("out_b", 0, SLOTS), ALU.add)\
                .then_inc(s["ao_done"], 1)
            for i in range(4):
                dve.wait_ge(s["h2_ps"], i + 1)
                for k in range(2):
                    k_st = v.bn_stats(st3[:, 2 * i + k, :], h2_bank[i][0:TOK, DIM * k:DIM * k + DIM])
                k_st.then_inc(s["h2_read"], 1)
                if i % 2:
                    dve.wait_ge(s["h2_read"], i + 1)
                    for b in range(2 * i - 2, 2 * i + 2):
                        last = v.bn_aggr(mv3[:, b, :], st3[:, b, :])
                    last.then_inc(s["mv3_done"], 1)
            for hf in range(2):
                normalise(h2, mv3, rs3, xn2, hf, "mv3_done", "rs3_done", "xn2_done")

            for hf in range(2):
                lo_of_turned(bank[3 + 2 * hf][:, 0:H2N], bank[4 + 2 * hf][0:FB, 0:H2N],
                             slice(H2N * hf, H2N * hf + H2N), hf + 7)
            def split_up(n, p):
                dve.wait_ge(s["ug_hi"], n + 1)
                v.tensor_tensor(ug_w[p][:, 1, :], expert_raw[:, p, 0:4 * HID], f(ug_w[p][:, 0, :]),
                                ALU.subtract).then_inc(s["ug_lo"], 1)

            def gate(n, hf, p):
                first = isinstance(n, int) and n == 0
                dve.wait_ge(s[f"silu{hf}"], n + 1)
                dve.wait_ge(s[f"g_ps{hf}"], n + 1)
                if not isinstance(n, int) or n > 1:
                    dve.wait_ge(s["weighed"], 2 * (n - 1))
                v.scalar_tensor_tensor((hid if first else gated)[hf][:, :], bank[4 + 2 * hf][:, 0:H2N],
                                       expert_raw[:, p, BG:BG + 1],
                                       silu[hf][:, :], ALU.add, ALU.mult).then_inc(s[f"gated{hf}"], 1)

            def weigh(n, hf, p):
                if isinstance(n, int) and n == 0:
                    return
                dve.wait_ge(s[f"gated{hf}"], n + 1)
                if isinstance(n, int) and n == 1:
                    dve.wait_ge(s["wb_ps"], hf + 1)
                    weights = bank[7][:, 0:H2N]
                else:
                    if hf == 0:
                        dve.wait_ge(d_w_all[p], 8 * (n - p))
                    weights = w_all[p][:, H2N * hf:H2N * hf + H2N]
                dve.wait_ge(s["hid_hi"], 2 * (n - 1) + hf + 1)
                dve.wait_ge(s["hid_lo"], 2 * (n - 1) + hf + 1)
                v.tensor_tensor(hid[hf][:, :], weights, gated[hf][:, :], ALU.mult)\
                    .then_inc(s["weighed"], 1)

            def hidden_lo(n, hf, p):
                dve.wait_ge(s["hid_hi"], 2 * n + hf + 1)
                tok = slice(H2N * hf, H2N * hf + H2N)
                v.tensor_tensor(hid_s[p][:, 1, tok], hid[hf][:, :], f(hid_s[p][:, 0, tok]), ALU.subtract)\
                    .then_inc(s["hid_lo"], 1)

            def expert(n, p, more=True):
                gate(n, 0, p)
                if more:
                    split_up(n + 1, 1 - p)
                weigh(n, 0, p)
                down_lo(n, p)
                gate(n, 1, p)
                hidden_lo(n, 0, p)
                weigh(n, 1, p)
                hidden_lo(n, 1, p)

            wide = [TOK, IMAGES, EXPERTS]
            dve.wait_ge(s["glt_ps"], 1)
            logits = v3(bank[1][0:TOK, 0:IMAGES * EXPERTS], EXPERTS)
            k = step(v.tensor_reduce(gmax[:, :], logits, AXX, ALU.max))
            after(k)
            v.tensor_tensor(gexp[:, :, :], logits, gmax[:, :].unsqueeze(2).to_broadcast(wide), ALU.subtract)\
                .then_inc(s["gd_done"], 1)
            dve.wait_ge(s["ge_done"], 1)
            k = step(v.tensor_reduce(gsum[:, :], gexp[:, :, :], AXX, ALU.add))
            after(k)
            k = step(v.reciprocal(grec[:, :], gsum[:, :]))
            after(k)
            k = step(v.tensor_tensor(score[:, :, :], gexp[:, :, :], grec[:, :].unsqueeze(2).to_broadcast(wide),
                                     ALU.mult))
            after(k)
            k = step(v.tensor_tensor(sbias[:, :, :], score[:, :, :],
                                     row("bias", 0, TOK).unsqueeze(1).to_broadcast(wide), ALU.add))
            after(k)
            pair = sbias[:, :, :].rearrange("p b (g e) -> p b g e", e=2)
            k = step(v.tensor_tensor(grp[:, :, 0:GROUPS], pair[:, :, :, 0], pair[:, :, :, 1], ALU.add))
            after(k)

            def best_four(values, top, picked, out, n):
                for b in range(IMAGES):
                    k = step(v.max(top[:, b, :], values[:, b, 0:n]))
                after(k)
                k = step(v.tensor_copy(picked[:, :, 0:TOPK], top[:, :, 0:TOPK]))
                after(k)
                for b in range(IMAGES):
                    k = step(v.match_replace(out=out[:, b, :], in_to_replace=picked[:, b, :],
                                             in_values=values[:, b, :], imm_value=GONE))
                after(k)

            best_four(grp, grp_top, grp_val, grp_out, GROUPS)
            k = step(v.tensor_tensor(grp_in[:, :, :], grp_out[:, :, 0:GROUPS], grp[:, :, 0:GROUPS],
                                     ALU.not_equal))
            after(k)
            step(v.tensor_scalar(grp_low[:, :, :], grp_in[:, :, :], 1.0, -GONE, ALU.subtract, ALU.mult))
            wide = [TOK, IMAGES, GROUPS, 2]
            k = step(v.tensor_tensor(smask[:, :, :].rearrange("p b (g e) -> p b g e", e=2), pair,
                                     grp_in[:, :, :].unsqueeze(3).to_broadcast(wide), ALU.mult))
            after(k)
            k = step(v.tensor_tensor(exq[:, :, 0:EXPERTS].rearrange("p b (g e) -> p b g e", e=2),
                                     smask[:, :, :].rearrange("p b (g e) -> p b g e", e=2),
                                     grp_low[:, :, :].unsqueeze(3).to_broadcast(wide), ALU.add))
            after(k)
            gate(0, 0, 0)
            gate(0, 1, 0)
            best_four(exq, exq_top, exq_val, exq_out, EXPERTS)
            k = step(v.tensor_tensor(exq_in[:, :, :], exq_out[:, :, 0:EXPERTS], exq[:, :, 0:EXPERTS],
                                     ALU.not_equal))
            after(k)
            v.scalar_tensor_tensor(wfull[:, :, :].rearrange("p b e -> p (b e)"),
                                   score[:, :, :].rearrange("p b e -> p (b e)"), ROUTE_SCALE,
                                   exq_in[:, :, :].rearrange("p b e -> p (b e)"), ALU.mult, ALU.mult)\
                .then_inc(s["wfull_done"], 1)

            hidden_lo(0, 0, 0)
            hidden_lo(0, 1, 0)
            for hf in range(2):
                dve.wait_ge(s["wT_hi"], hf + 1)
                v.tensor_copy(w_flat[:, H2N * hf:H2N * hf + H2N], bank[7 if hf == 0 else 2][0:EXPERTS, 0:H2N])\
                    .then_inc(s["w_flat_done"], 1)
            expert(1, 1)
            with dve.Fori(0, 7) as it:
                expert(2 * it + 2, 0)
                expert(2 * it + 3, 1)
            expert(16, 0, more=False)
            dve.wait_ge(s["sum_done"], 1)
            v.tensor_scalar(finA[:, 0:512], bank[0][:, :], col("sbdA", 128), None, ALU.add)\
                .then_inc(s["finA_done"], 1)
            dve.wait_ge(s["fin_moved"], 1)
            v.scalar_tensor_tensor(finB[:, 0:512], bank[2][0:FB, :], col("sbdB", FB), fin_tmp[:, 0:512],
                                   ALU.add, ALU.add).then_inc(s["finB_done"], 1)
            dve.wait_ge(s["fin_moved"], 3)
            v.scalar_tensor_tensor(finB[:, 512:T2], bank[1][0:FB, 256:512], col("sbdB", FB), fin_tmp[:, 512:T2],
                                   ALU.add, ALU.add).then_inc(s["finB_done"], 1)


def constants():
    out = np.zeros((128, NCONST), np.float32)

    def put(name, a):
        out[:a.shape[0], CONST[name][0]:CONST[name][1]] = a

    put("ident", np.eye(128, dtype=np.float32))
    pos = np.arange(IMG_TOK, dtype=np.float32)[:, None]
    i = np.arange(DIM // 2, dtype=np.float32)[None, :]
    ang = pos / np.power(np.float32(10000.0), np.float32(2.0) * i / np.float32(DIM))
    pe = np.zeros((IMG_TOK, DIM), np.float32)
    pe[:, 0::2], pe[:, 1::2] = np.sin(ang), np.cos(ang)
    put("pe", np.concatenate([pe, pe]))
    key = np.arange(TOK)
    put("causal", np.where(key[None, :] > key[:, None], -10000.0, 0.0))
    put("tri", (key[:, None] <= key[None, :]).astype(np.float32))
    feat = np.arange(128)
    put("head", (feat[:CH, None] // HEAD == np.arange(CHH)[None, :]).astype(np.float32))
    put("parity", (feat[:, None] // HEAD % 2 == np.arange(2)[None, :]).astype(np.float32))
    put("block", (np.arange(SLOTS)[:, None] // PICKED == np.arange(IMAGES)[None, :]).astype(np.float32))
    put("iota", np.tile(np.arange(1, PICKED + 1, dtype=np.float32), (128, 1)))
    return out


def arrays_of(i):
    i = {k: np.asarray(v) for k, v in i.items()}

    def ab(w):
        return [w[:FA], np.concatenate([w[FA:], w[FA:]])]

    def tall(w, n=128):
        out = np.zeros((n,) + w.shape[1:], w.dtype)
        out[:len(w)] = w
        return out

    x = i["x"].reshape(IMAGES, CHANNELS, GRID, PATCH, GRID, PATCH).transpose(1, 3, 5, 0, 2, 4)
    x = x.reshape(PK, 128, 4, 128).transpose(2, 1, 0, 3)
    tok, at, fn = "L0_tok_", "L0_attn_", "L0_ffn_"
    out = {"patches": x}
    out["patch_w"] = i[tok + "patch_w"].reshape(DIM, PK, 128).transpose(2, 1, 0)
    out["const"] = constants()
    cols = np.zeros((128, NCOLS), np.float32)

    def put(name, a):
        cols[:a.shape[0], COLS[name][0]:COLS[name][1]] = a

    put("ff1_b", i[tok + "ff1_b"].reshape(FK, 128).T)
    put("ff2_bA", i[tok + "ff2_b"][:FA, None])
    put("ff2_bB", i[tok + "ff2_b"][FA:, None])
    put("q_b", i[tok + "qkv_b"][:DIM].reshape(2, CH).T)
    put("k_b", i[tok + "qkv_b"][DIM:2 * DIM].reshape(2, CH).T)
    put("aq_b", i[at + "Wqkv_b"][:DIM].reshape(2, CH).T)
    put("ak_b", i[at + "Wqkv_b"][DIM:2 * DIM].reshape(2, CH).T)
    put("gate_b", i[fn + "gate_b"][:, None])
    put("sel_b", i[at + "sel_b"][:, None])
    put("sbdA", i[fn + "sbd"][:FA, None])
    put("sbdB", i[fn + "sbd"][FA:, None])
    out["cols"] = cols
    out["rows"] = np.concatenate([
        i[tok + "patch_b"], i[tok + "ln_g"], i[tok + "ln_b"], i[tok + "qkv_b"][2 * DIM:], i[tok + "proj_b"],
        i[tok + "ff2_b"], i[at + "Wqkv_b"][2 * DIM:], i[at + "out_b"], i[fn + "bias"],
        i[at + "temperature"]])[None]
    out["ff1"] = np.concatenate(ab(i[tok + "ff1_w"]), 1)
    out["ff2"] = i[tok + "ff2_w"].reshape(FK, 128, DIM).transpose(1, 0, 2)
    out["qkv"] = np.concatenate(ab(i[tok + "qkv_w"]), 1)
    pw = i[tok + "proj_w"].reshape(2, 3, 32, DIM).transpose(1, 0, 2, 3).reshape(DIM, DIM)
    out["proj"] = np.stack([pw[:FA], tall(pw[FA:])], 1)
    kv = np.concatenate([i[at + "Wqkv_w"][:, DIM:], i[at + "sel_w"]], 1)
    out["kv"] = np.concatenate(ab(kv), 1)
    aq = i[at + "Wqkv_w"][:, :DIM]
    out["aq"] = np.stack([aq[:FA], tall(aq[FA:])], 1)
    out["out_w"] = i[at + "out_w"].reshape(2, CH, DIM).transpose(1, 0, 2)
    out["gate"] = np.concatenate(ab(i[fn + "gate_w"]), 1)
    bd = np.zeros((48, DIM), np.float32)
    bd[:EXPERTS], bd[32:] = i[fn + "bd"], i[fn + "bd"]
    out["bd"] = bd
    out["txt"] = i["txt"].transpose(1, 0, 2)
    wu = np.concatenate([i[fn + "sWu"][None], i[fn + "Wu"]])
    wg = np.concatenate([i[fn + "sWg"][None], i[fn + "Wg"]])
    wd = np.concatenate([i[fn + "sWd"][None], i[fn + "Wd"]])
    twice = [np.concatenate([w[:, FA:], w[:, FA:]], 1) for w in (wu, wg)]
    bu = np.concatenate([i[fn + "sbu"][None], i[fn + "bu"]])[:, :, None]
    bg = np.concatenate([i[fn + "sbg"][None], i[fn + "bg"]])[:, :, None]
    out["experts"] = np.concatenate([wu[:, :FA], wg[:, :FA], *twice, wd, bu, bg], 2)
    return {k: np.ascontiguousarray(v) for k, v in out.items()}


def kernel(**inputs):
    import concourse.bacc as _bacc
    from concourse.bass_utils import run_bass_kernel_spmd as _run

    nc = _bacc.Bacc("TRN2", target_bir_lowering=False, num_devices=1)
    arrays = arrays_of(inputs)
    args = {k: nc.dram_tensor("in_" + k, a.shape, mybir.dt.from_np(a.dtype), kind="ExternalInput").ap()
            for k, a in arrays.items()}
    args["out"] = nc.dram_tensor("out", (DIM, T2), F32, kind="ExternalOutput").ap()
    build(nc, args)
    r = _run(nc, [{"in_" + k: a for k, a in arrays.items()}], core_ids=[0])
    return np.ascontiguousarray(r.results[0]["out"].T.reshape(IMAGES, TOK, DIM))
```
